# Optimizing a Trainium2 kernel written in Bass

```python
import numpy as np
import jax
import jax.numpy as jnp

def _softmax(x, axis=-1):
    return jax.nn.softmax(x, axis=axis)

def _gelu(x):
    return jax.nn.gelu(x, approximate=True)

def _silu(x):
    return jax.nn.silu(x)

def _sigmoid(x):
    return jax.nn.sigmoid(x)

def _layernorm(x, axis=-1, eps=1e-05):
    m = jnp.mean(x, axis=axis, keepdims=True)
    v = jnp.var(x, axis=axis, keepdims=True)
    return (x - m) / jnp.sqrt(v + eps)

def _scatter_add(tgt, idx, src, axis=0):
    return tgt.at[idx].add(src)

def _segment_sum(src, seg, n):
    return jax.ops.segment_sum(src, seg, n)
kernel_name = 'mk_vit_tower_cls_d1_tok_img1024_r4_862ef4'

def setup_inputs(seed: int=0):
    np.random.seed(seed)
    _w = jnp.asarray

    def _rec_inputs():
        import jax
        import jax.numpy as jnp
        _rk = jax.random.key(seed)
        x = -0.00016672 + 0.999947 * jax.random.normal(jax.random.fold_in(_rk, 1), (16, 3, 128, 128), jnp.float32)
        cls_tok = 0.02 * jax.random.normal(jax.random.fold_in(_rk, 5), (1, 1, 256), jnp.float32)
        return (x, cls_tok)
    x, cls_tok = _rec_inputs()

    def _L0_tok_setup():
        import jax, jax.numpy as jnp
        import numpy as np
        PATCH = 16
        D_MODEL = 256

        def patchify(imgs, p):
            n, c, H, W = imgs.shape
            h, w = (H // p, W // p)
            x = imgs.reshape(n, c, h, p, w, p)
            x = jnp.einsum('nchpwq->nhwpqc', x)
            return x.reshape(n, h * w, p * p * c)
        key = jax.random.key(seed)
        k1, k2, k3 = jax.random.split(key, 3)
        val = jax.random.normal(k1, (64, 3, 96, 96), dtype=jnp.float32)
        in_dim = PATCH * PATCH * 3
        bound = 1.0 / np.sqrt(in_dim)
        W = jax.random.uniform(k2, (D_MODEL, in_dim), dtype=jnp.float32, minval=-bound, maxval=bound)
        b = jax.random.uniform(k3, (D_MODEL,), dtype=jnp.float32, minval=-bound, maxval=bound)
        return {'val': val, 'W': W, 'b': b}
    _L0_tok_all = _L0_tok_setup()
    _L0_tok_in = {k: v for k, v in _L0_tok_all.items() if k in ('W', 'b')}
    del _L0_tok_all

    def _L0_attn_setup():
        import jax, jax.numpy as jnp
        import numpy as np
        B, S, D, H = (2, 512, 256, 16)
        HD = D // H
        FF = 1024
        NUM_ITERS = 8
        DT = 0.1
        LN_EPS = 1e-05

        def _ln(x, g, b):
            m = jnp.mean(x, axis=-1, keepdims=True)
            v = jnp.var(x, axis=-1, keepdims=True)
            return (x - m) * jax.lax.rsqrt(v + LN_EPS) * g + b

        def _forward(x, qkv_w, qkv_b, out_w, out_b, g_attn, b_attn, g1, b1, g2, b2, w_ctx, w_x, b_inl, ff_w1, ff_b1, ff_w2, ff_b2):
            b, s, d = x.shape
            xn = _ln(x, g_attn, b_attn)
            qkv = (xn @ qkv_w + qkv_b).reshape(b, s, 3, H, HD)
            qkv = jnp.transpose(qkv, (2, 0, 3, 1, 4))
            q, k, v = (qkv[0], qkv[1], qkv[2])
            scores = jnp.einsum('bhqd,bhkd->bhqk', q, k) / np.sqrt(HD).astype(np.float32)
            causal = jnp.triu(jnp.ones((s, s), dtype=bool), 1)
            scores = jnp.where(causal[None, None], -jnp.inf, scores)
            attn_w = jax.nn.softmax(scores, axis=-1)
            attn = jnp.einsum('bhqk,bhkd->bhqd', attn_w, v)
            attn = jnp.transpose(attn, (0, 2, 1, 3)).reshape(b, s, d)
            attn = attn @ out_w + out_b
            x = x + attn
            ctx = attn.reshape(b * s, d)
            xs = _ln(x, g1, b1).reshape(b * s, d)
            vs = jnp.zeros_like(xs)

            def step(carry, _):
                xs, vs = carry
                u = jnp.tanh(ctx @ w_ctx + xs @ w_x + b_inl)
                vn = vs + DT * (u - xs - vs)
                xn_ = xs + DT * vn
                return ((xn_, vn), None)
            (xs, vs), _ = jax.lax.scan(step, (xs, vs), None, length=NUM_ITERS)
            x = x + xs.reshape(b, s, d)
            h = _ln(x, g2, b2)
            h = jax.nn.gelu(h @ ff_w1 + ff_b1, approximate=False)
            x = x + (h @ ff_w2 + ff_b2)
            return x
        key = jax.random.key(seed)
        ks = jax.random.split(key, 16)

        def xav(k, shape):
            lim = np.sqrt(6.0 / (shape[0] + shape[1]))
            return jax.random.uniform(k, shape, minval=-lim, maxval=lim, dtype=jnp.float32)
        return {'x': jax.random.normal(ks[0], (B, S, D), dtype=jnp.float32), 'qkv_w': xav(ks[1], (D, 3 * D)), 'qkv_b': jnp.zeros((3 * D,), jnp.float32), 'out_w': xav(ks[2], (D, D)), 'out_b': jnp.zeros((D,), jnp.float32), 'g_attn': jnp.ones((D,), jnp.float32), 'b_attn': jnp.zeros((D,), jnp.float32), 'g1': jnp.ones((D,), jnp.float32), 'b1': jnp.zeros((D,), jnp.float32), 'g2': jnp.ones((D,), jnp.float32), 'b2': jnp.zeros((D,), jnp.float32), 'w_ctx': xav(ks[3], (D, D)), 'w_x': xav(ks[4], (D, D)), 'b_inl': jnp.zeros((D,), jnp.float32), 'ff_w1': xav(ks[5], (D, FF)), 'ff_b1': jnp.zeros((FF,), jnp.float32), 'ff_w2': xav(ks[6], (FF, D)), 'ff_b2': jnp.zeros((D,), jnp.float32)}
    _L0_attn_all = _L0_attn_setup()
    _L0_attn_in = {k: v for k, v in _L0_attn_all.items() if k in ('qkv_w', 'qkv_b', 'out_w', 'out_b', 'g_attn', 'b_attn', 'g1', 'b1', 'g2', 'b2', 'w_ctx', 'w_x', 'b_inl', 'ff_w1', 'ff_b1', 'ff_w2', 'ff_b2')}
    del _L0_attn_all

    def _L0_ffn_setup():
        import jax, jax.numpy as jnp
        import numpy as np
        D, H, O, E, TOPK = (256, 1024, 256, 8, 2)
        B, L = (2, 512)
        ROUTE_SCALE = 1.0
        key = jax.random.key(seed)
        ks = jax.random.split(key, 7)
        gb = float(np.sqrt(6.0 / (E + D)))
        return {'x': jax.random.normal(ks[0], (B, L, D), dtype=jnp.float32), 'gate_w': jax.random.uniform(ks[1], (E, D), jnp.float32, -gb, gb), 'gate_b': jnp.zeros((E,), jnp.float32), 'w1': jax.random.normal(ks[2], (E, D, H), jnp.float32) * 0.02, 'b1': jnp.zeros((E, H), jnp.float32), 'w2': jax.random.normal(ks[3], (E, H, O), jnp.float32) * 0.02, 'b2': jnp.zeros((E, O), jnp.float32)}
    _L0_ffn_all = _L0_ffn_setup()
    _L0_ffn_in = {k: v for k, v in _L0_ffn_all.items() if k in ('gate_w', 'gate_b', 'w1', 'b1', 'w2', 'b2')}
    del _L0_ffn_all
    return {'x': x, 'cls_tok': cls_tok, 'L0_tok_W': _L0_tok_in['W'], 'L0_tok_b': _L0_tok_in['b'], 'L0_attn_qkv_w': _L0_attn_in['qkv_w'], 'L0_attn_qkv_b': _L0_attn_in['qkv_b'], 'L0_attn_out_w': _L0_attn_in['out_w'], 'L0_attn_out_b': _L0_attn_in['out_b'], 'L0_attn_g_attn': _L0_attn_in['g_attn'], 'L0_attn_b_attn': _L0_attn_in['b_attn'], 'L0_attn_g1': _L0_attn_in['g1'], 'L0_attn_b1': _L0_attn_in['b1'], 'L0_attn_g2': _L0_attn_in['g2'], 'L0_attn_b2': _L0_attn_in['b2'], 'L0_attn_w_ctx': _L0_attn_in['w_ctx'], 'L0_attn_w_x': _L0_attn_in['w_x'], 'L0_attn_b_inl': _L0_attn_in['b_inl'], 'L0_attn_ff_w1': _L0_attn_in['ff_w1'], 'L0_attn_ff_b1': _L0_attn_in['ff_b1'], 'L0_attn_ff_w2': _L0_attn_in['ff_w2'], 'L0_attn_ff_b2': _L0_attn_in['ff_b2'], 'L0_ffn_gate_w': _L0_ffn_in['gate_w'], 'L0_ffn_gate_b': _L0_ffn_in['gate_b'], 'L0_ffn_w1': _L0_ffn_in['w1'], 'L0_ffn_b1': _L0_ffn_in['b1'], 'L0_ffn_w2': _L0_ffn_in['w2'], 'L0_ffn_b2': _L0_ffn_in['b2']}

def reference(x, cls_tok, L0_tok_W, L0_tok_b, L0_attn_qkv_w, L0_attn_qkv_b, L0_attn_out_w, L0_attn_out_b, L0_attn_g_attn, L0_attn_b_attn, L0_attn_g1, L0_attn_b1, L0_attn_g2, L0_attn_b2, L0_attn_w_ctx, L0_attn_w_x, L0_attn_b_inl, L0_attn_ff_w1, L0_attn_ff_b1, L0_attn_ff_w2, L0_attn_ff_b2, L0_ffn_gate_w, L0_ffn_gate_b, L0_ffn_w1, L0_ffn_b1, L0_ffn_w2, L0_ffn_b2):
    import jax
    import jax.numpy as jnp

    def _L0_tok_ref(val, W, b):
        import jax, jax.numpy as jnp
        import numpy as np
        PATCH = 16
        D_MODEL = 256

        def patchify(imgs, p):
            n, c, H, W = imgs.shape
            h, w = (H // p, W // p)
            x = imgs.reshape(n, c, h, p, w, p)
            x = jnp.einsum('nchpwq->nhwpqc', x)
            return x.reshape(n, h * w, p * p * c)
        patches = patchify(val, PATCH)
        return jnp.einsum('nld,md->nlm', patches, W) + b

    def _L0_attn_ref(x, qkv_w, qkv_b, out_w, out_b, g_attn, b_attn, g1, b1, g2, b2, w_ctx, w_x, b_inl, ff_w1, ff_b1, ff_w2, ff_b2):
        import jax, jax.numpy as jnp
        import numpy as np
        B, S, D, H = (2, 512, 256, 16)
        HD = D // H
        FF = 1024
        NUM_ITERS = 8
        DT = 0.1
        LN_EPS = 1e-05

        def _ln(x, g, b):
            m = jnp.mean(x, axis=-1, keepdims=True)
            v = jnp.var(x, axis=-1, keepdims=True)
            return (x - m) * jax.lax.rsqrt(v + LN_EPS) * g + b

        def _forward(x, qkv_w, qkv_b, out_w, out_b, g_attn, b_attn, g1, b1, g2, b2, w_ctx, w_x, b_inl, ff_w1, ff_b1, ff_w2, ff_b2):
            b, s, d = x.shape
            xn = _ln(x, g_attn, b_attn)
            qkv = (xn @ qkv_w + qkv_b).reshape(b, s, 3, H, HD)
            qkv = jnp.transpose(qkv, (2, 0, 3, 1, 4))
            q, k, v = (qkv[0], qkv[1], qkv[2])
            scores = jnp.einsum('bhqd,bhkd->bhqk', q, k) / np.sqrt(HD).astype(np.float32)
            causal = jnp.triu(jnp.ones((s, s), dtype=bool), 1)
            scores = jnp.where(causal[None, None], -jnp.inf, scores)
            attn_w = jax.nn.softmax(scores, axis=-1)
            attn = jnp.einsum('bhqk,bhkd->bhqd', attn_w, v)
            attn = jnp.transpose(attn, (0, 2, 1, 3)).reshape(b, s, d)
            attn = attn @ out_w + out_b
            x = x + attn
            ctx = attn.reshape(b * s, d)
            xs = _ln(x, g1, b1).reshape(b * s, d)
            vs = jnp.zeros_like(xs)

            def step(carry, _):
                xs, vs = carry
                u = jnp.tanh(ctx @ w_ctx + xs @ w_x + b_inl)
                vn = vs + DT * (u - xs - vs)
                xn_ = xs + DT * vn
                return ((xn_, vn), None)
            (xs, vs), _ = jax.lax.scan(step, (xs, vs), None, length=NUM_ITERS)
            x = x + xs.reshape(b, s, d)
            h = _ln(x, g2, b2)
            h = jax.nn.gelu(h @ ff_w1 + ff_b1, approximate=False)
            x = x + (h @ ff_w2 + ff_b2)
            return x
        return _forward(x, qkv_w, qkv_b, out_w, out_b, g_attn, b_attn, g1, b1, g2, b2, w_ctx, w_x, b_inl, ff_w1, ff_b1, ff_w2, ff_b2)

    def _L0_ffn_ref(x, gate_w, gate_b, w1, b1, w2, b2):
        import jax, jax.numpy as jnp
        import numpy as np
        D, H, O, E, TOPK = (256, 1024, 256, 8, 2)
        B, L = (2, 512)
        ROUTE_SCALE = 1.0
        Bb, Ll, Dd = x.shape
        N = Bb * Ll
        x_flat = x.reshape(N, Dd)
        logits = x_flat @ gate_w.T + gate_b
        probs = jax.nn.softmax(logits * ROUTE_SCALE, axis=-1)
        topk_vals, topk_idx = jax.lax.top_k(probs, TOPK)
        dense_gate = jnp.zeros((N, E), probs.dtype).at[jnp.arange(N)[:, None], topk_idx].set(topk_vals)
        h = jax.nn.relu(jnp.einsum('nd,edh->neh', x_flat, w1) + b1)
        y = jnp.einsum('neh,eho->neo', h, w2) + b2
        out_flat = jnp.einsum('ne,neo->no', dense_gate, y)
        return out_flat.reshape(Bb, Ll, O)
    h = _L0_tok_ref(x, L0_tok_W, L0_tok_b)
    h = jnp.concatenate([jnp.broadcast_to(cls_tok, (h.shape[0], 1, h.shape[2])), h], axis=1)
    h = h + _L0_attn_ref(_layernorm(h, axis=-1), L0_attn_qkv_w, L0_attn_qkv_b, L0_attn_out_w, L0_attn_out_b, L0_attn_g_attn, L0_attn_b_attn, L0_attn_g1, L0_attn_b1, L0_attn_g2, L0_attn_b2, L0_attn_w_ctx, L0_attn_w_x, L0_attn_b_inl, L0_attn_ff_w1, L0_attn_ff_b1, L0_attn_ff_w2, L0_attn_ff_b2)
    h = h + _L0_ffn_ref(_layernorm(h, axis=-1), L0_ffn_gate_w, L0_ffn_gate_b, L0_ffn_w1, L0_ffn_b1, L0_ffn_w2, L0_ffn_b2)
    return h

_drawn_inputs = setup_inputs


def setup_inputs(seed=0):
    import zlib

    import numpy as np

    out = dict(_drawn_inputs(seed))
    spreads = {'L0_attn_qkv_b': (0.0, 0.1),
     'L0_attn_out_b': (0.0, 0.1),
     'L0_attn_g_attn': (1.0, 0.2),
     'L0_attn_b_attn': (0.0, 0.1),
     'L0_attn_g1': (1.0, 0.2),
     'L0_attn_b1': (0.0, 0.1),
     'L0_attn_g2': (1.0, 0.2),
     'L0_attn_b2': (0.0, 0.357),
     'L0_attn_b_inl': (0.0, 0.8),
     'L0_attn_ff_b1': (0.0, 0.1),
     'L0_attn_ff_b2': (0.0, 0.1),
     'L0_ffn_gate_b': (0.0, 0.8),
     'L0_ffn_b1': (0.0, 0.776),
     'L0_ffn_b2': (0.0, 0.35)}
    factors = {}
    for name, (base, spread) in spreads.items():
        noise = np.random.default_rng([zlib.crc32(name.encode()), seed]).standard_normal(out[name].shape)
        drawn = base * np.exp(spread * noise) if base else spread * noise
        out[name] = jnp.asarray(drawn.astype(out[name].dtype))
    for name, factor in factors.items():
        out[name] = (out[name] * factor).astype(out[name].dtype)
    return out
```

```python
from contextlib import ExitStack

import concourse.bass as bass
from concourse import mybir

F32 = mybir.dt.float32
BF16 = mybir.dt.bfloat16
I32 = mybir.dt.int32
ALU = mybir.AluOpType
ACT = mybir.ActivationFunctionType
AX_X = mybir.AxisListType.X

P = 128
IMG = 16
PATCHES = 64
SEQ = PATCHES + 1
TOK = IMG * SEQ
D = 256
KD = D // P
KPATCH = 768 // P
NCH = 4
CI = IMG // NCH
CT = CI * SEQ
CP = CI * PATCHES
H = 16
HD = D // H
HG = H // KD
HB = 4
FF = 1024
KF = FF // P
ITERS = 8
DT = 0.1
EPS = 1e-5
E = 8
EH = 1024
KE = EH // P
WE = KD * EH + KE * D
NT = -(-TOK // P)
LAST = TOK - (NT - 1) * P
TP = NT * P
SLOT_TILES = (2 * TOK + E * (P - 1)) // P
ROW = D + 2
XR = 4
NEG = -3.0e38

VEC = (("tok_b", KD), ("cls", KD), ("g_attn", KD), ("b_attn", KD), ("g1", KD), ("b1", KD), ("g2", KD), ("b2", KD),
       ("b_inl", KD), ("qk_b", 2 * KD), ("out_b", KD), ("ff_b1", KF), ("ff_b2", KD), ("moe_b1", E * KE))
NVEC = sum(n for _, n in VEC)


class Norm:

    def __init__(self, sem, name, source, ready, per_chunk, mean_banks, var_banks):
        self.source = source
        self.ready = ready
        self.per_chunk = per_chunk
        self.mean_banks = mean_banks
        self.var_banks = var_banks
        self.mean = sem(f"{name}_mean")
        self.centered = sem(f"{name}_centered")
        self.squared = sem(f"{name}_squared")
        self.var = sem(f"{name}_var")
        self.logged = sem(f"{name}_logged")
        self.rstd = sem(f"{name}_rstd")
        self.var_used = self.rstd
        self.scaled = sem(f"{name}_scaled")
        self.done = sem(f"{name}_done")


def vit_block(nc, patches, tok_w, qkv_w, out_w, ctx_w, x_w, ff1_w, ff2_w, moe_w, gate_w, vec, v_b, gate_b, moe_b2,
              out):
    slots = nc.dram_tensor("slots", (SLOT_TILES * P, ROW), F32, kind="Internal").ap()
    acc = nc.dram_tensor("acc", (TOK + P, D), F32, kind="Internal").ap()

    with ExitStack() as ctx:
        def sb(name, shape, dt=F32):
            return ctx.enter_context(nc.sbuf_tensor(name, shape, dt))

        def sem(name):
            return ctx.enter_context(nc.semaphore(name))

        def carve(flat, at, *dims):
            n = 1
            for d in dims:
                n *= d
            names = "abcd"[:len(dims)]
            view = flat[:, at:at + n].rearrange(f"p ({' '.join(names)}) -> p {' '.join(names)}",
                                                **dict(zip(names, dims)))
            return view, at + n

        W = sb("W", [P, E * WE])
        at = (E - 1) * WE
        wtok, at = carve(W, at, KPATCH, D)
        wqkv, at = carve(W, at, KD, 3 * D)
        wout, at = carve(W, at, KD, D)
        wctx, at = carve(W, at, KD, D)
        at = (E - 2) * WE
        wff1, at = carve(W, at, KD, FF)
        wff2, at = carve(W, at, KF, D)
        qk, _ = carve(W, (E - 3) * WE, 2, 2 * KD, 2 * SEQ)
        wx = sb("wx", [P, KD, D])
        wxd = sb("wxd", [P, KD, D])
        gate_t = sb("gate_t", [P, KD, E])
        vecs = sb("vecs", [P, NVEC])
        vec_at, at = {}, 0
        for name, n in VEC:
            vec_at[name] = at
            at += n

        def vcol(name, m=0, n=1):
            return vecs[:, vec_at[name] + m:vec_at[name] + m + n]

        vb_rows = sb("vb_rows", [P, D])
        gb_rows = sb("gb_rows", [P, E])
        b2_rows = sb("b2_rows", [E, D])

        hT = sb("hT", [P, KD, TOK])
        nT = sb("nT", [P, KD, TP])
        arena = sb("arena", [P, 4 * KD * TOK])
        x0T, _ = carve(arena, 0, KD, TOK)
        xsT, _ = carve(arena, KD * TOK, KD, TOK)
        eT, _ = carve(arena, 2 * KD * TOK, KD, TOK)
        rT, _ = carve(arena, 3 * KD * TOK, KD, TOK)
        xc = sb("xc", [P, 2, KD, CT])
        sq = sb("sq", [P, 2, KD, CT])
        rs = sb("rs", [P, 2, CT])
        pe, u = xc, sq

        pt = [carve(arena, (2 + i) * KD * TOK, KPATCH, CP)[0] for i in range(2)]
        kx = [carve(arena, (2 * KD + i) * TOK, KD, HG, SEQ)[0] for i in range(2)]
        ex, pT = [], []
        at = 3 * KD * TOK
        for i in range(2):
            view, at = carve(arena, at, HG, SEQ)
            ex.append(view)
        for i in range(2):
            view, at = carve(arena, at, 2, HB * SEQ)
            pT.append(view)
        fh = [carve(arena, (2 + i) * KD * TOK, KF, CT)[0] for i in range(2)]
        at = KD * TOK
        sh, va = [], []
        for i in range(2):
            view, at = carve(arena, at, HG, SEQ)
            sh.append(view)
        for i in range(2):
            view, at = carve(arena, at, H, HD + 1)
            va.append(view)
        att, at = carve(arena, at, H, HD)
        assert at <= 2 * KD * TOK
        xi = sb("xi", [P, 2, KD, 2 * SEQ])
        ffb_buf = xi[:, :, :, :].rearrange("p a b s -> p (a b s)").rearrange("p (k t) -> p k t", k=KD)
        mx = sb("mx", [P, 2, HG])
        rc = sb("rc", [P, H])

        at = 0
        rows, at = carve(arena, at, 2, NT * ROW)
        rows = [rows[:, k, :].rearrange("p (t n) -> p t n", t=NT) for k in range(2)]
        xin, at = carve(arena, at, XR, ROW)
        xt, at = carve(arena, at, 2, KD, P)
        hid, at = carve(arena, at, KE, P)
        gT, at = carve(arena, at, TOK)
        assert at <= 4 * KD * TOK
        zs = sq[:, :, :, :].rearrange("p a b c -> p (a b c)")[:, 0:EH]
        y_flat = xc[:, :, :, :].rearrange("p a b c -> p (a b c)")
        yt, at = carve(y_flat, 0, 2, D)
        hrow, at = carve(y_flat, at, 2, D)

        ident = sb("ident", [P, P])
        identb = sb("identb", [P, P], BF16)
        maskb = sb("maskb", [P, HB, SEQ], BF16)
        mean_m = sb("mean_m", [P, P])
        ones = sb("ones", [P, P])
        below = sb("below", [P, P])
        head_of = sb("head_of", [P, HG])
        eps = sb("eps", [P, 1])
        before = sb("before", [P, E, E])
        iw = sb("iw", [P, 2 * NT + SLOT_TILES + E], I32)
        fw = sb("fw", [P, 2 * NT + SLOT_TILES + E])
        multiples, at = carve(fw, 0, NT)
        token_no, at = carve(fw, at, NT)
        tile_no, at = carve(fw, at, SLOT_TILES)
        rank, at = carve(fw, at, E)
        valid = sb("valid", [P, NT])
        empty = sb("empty", [P, ROW])

        pr = sb("pr", [P, NT, E])
        s9 = sb("s9", [P, 6, NT])
        oh = [sb(f"oh{k}", [P, NT, E]) for k in range(2)]
        scr = sb("scr", [P, NT, E])
        scr2 = sb("scr2", [P, NT, E])
        member = sb("member", [P, NT, E])
        pre = sb("pre", [P, NT + 1, E])
        tiles_k = sb("tiles_k", [P, E, NT])
        tiles_e = sb("tiles_e", [P, E])
        start_k = sb("start_k", [P, E, E])
        start_e = sb("start_e", [P, E])
        slot_f = sb("slot_f", [P, 2, NT])
        slot_i = sb("slot_i", [P, 2, NT], I32)
        te_k = sb("te_k", [P, SLOT_TILES, E - 1])
        te = sb("te", [P, SLOT_TILES])
        tile_expert = sb("tile_expert", [P, SLOT_TILES], I32)
        gates = sb("gates", [P, NT, E])
        b1t = sb("b1t", [P, 2, KE])

        PS = ctx.enter_context(nc.psum_tensor("PS", [P, 8, 512], F32))

        S = {n: sem(n) for n in (
            "l_tok", "l_pt0", "l_pt1", "l_pt2", "l_pt3", "l_vec", "l_qkv", "l_mid", "l_ff1", "l_ff2", "l_rows",
            "l_moe", "l_moe_late", "slots_empty", "acc_dummies",
            "c_pool", "c_int", "c_dve", "c_pe", "wxd",
            "tok", "h", "cls", "v2a", "v2", "rstd2_ln", "rstd2", "x0", "xna", "xnb", "xn",
            "xi", "qk", "qkev", "kx0", "kx1", "v", "vev", "scores", "mx", "sh", "ex", "T", "pT", "PV", "rc", "att",
            "aT", "attn",
            "o", "ctx", "x1", "z", "u", "e", "xs", "p9", "r",
            "x2", "f1", "fh", "f2", "ffb", "x3", "hp",
            "logit", "shifted", "exp", "rowT", "rowev", "row2", "route", "member", "cum", "gates", "gTt", "gTev", "hrow", "hrowev", "acc_set0", "acc_set1",
            "slot_no", "row_ends", "tile_expert", "scattered",
            "xin0", "xin1", "xin2", "xin3", "xt", "xtev", "l1", "zev", "hid", "b1t", "hrelu", "l2", "yev", "acc_add", "out_done",
        )}

        n0 = Norm(sem, "n0", hT, S["h"], 1, (4, 5), (6, 7))
        n0.var_used = S["v2"]
        n1 = Norm(sem, "n1", x0T, S["x1"], 1, (6,), (7,))
        n2 = Norm(sem, "n2", x0T, S["x2"], 1, (0, 1), (2, 3))
        n3 = Norm(sem, "n3", hT, S["hp"], 1, (0, 1), (2, 3))

        def chunk(c):
            return slice(c * CT, (c + 1) * CT)

        def over_k(ap, n):
            return ap.unsqueeze(1).broadcast_to([P, KD, n])

        def attention_steps(eng, step):
            step(0, 0, 0)
            with eng.Fori(0, IMG // CI - 1) as c:
                for j in range(CI):
                    step(c * CI + (1 + j), (1 + j) % CI, c * (CI // 2) + (2 + j) // 2)
            for i in range(IMG - 3, IMG):
                step(i, i % CI, (i + 1) // 2)

        def expert_steps(eng, step):
            for i in range(2):
                step(i, i, 0)
            with eng.Fori(0, SLOT_TILES // XR - 1) as r:
                for j in range(XR):
                    step(r * XR + (2 + j), (2 + j) % XR, r + (2 + j) // XR)
            for i in range(SLOT_TILES - 2, SLOT_TILES):
                step(i, i % XR, i // XR)

        block = ctx.enter_context(nc.Block())

        @block.sync
        def _(sp):
            sp.dma_start(wtok, tok_w).then_inc(S["l_tok"], 16)
            for c in range(2):
                sp.dma_start(pt[c % 2], patches[c]).then_inc(S[f"l_pt{c}"], 16)
            sp.dma_start(vecs[:, :], vec).then_inc(S["l_vec"], 16)
            sp.dma_start(wqkv, qkv_w).then_inc(S["l_qkv"], 16)
            sp.dma_start(vb_rows[:, :], v_b.broadcast_to([P, D])).then_inc(S["l_rows"], 16)
            sp.dma_start(gb_rows[:, :], gate_b.broadcast_to([P, E])).then_inc(S["l_rows"], 16)
            sp.dma_start(b2_rows[:, :], moe_b2).then_inc(S["l_rows"], 16)
            sp.dma_start(gate_t[:, :, :], gate_w).then_inc(S["l_rows"], 16)
            for c in range(2, NCH):
                sp.wait_ge(S["tok"], c - 1)
                sp.dma_start(pt[c % 2], patches[c]).then_inc(S[f"l_pt{c}"], 16)
            sp.dma_start(wout, out_w).then_inc(S["l_mid"], 16)
            sp.dma_start(wctx, ctx_w).then_inc(S["l_mid"], 16)
            sp.dma_start(wx[:, :, :], x_w).then_inc(S["l_mid"], 16)
            sp.dma_start(wff1, ff1_w).then_inc(S["l_ff1"], 16)
            sp.dma_start(wff2, ff2_w).then_inc(S["l_ff2"], 16)
            for e in range(E - 3):
                sp.dma_start(W[:, e * WE:(e + 1) * WE], moe_w[e]).then_inc(S["l_moe"], 16)
            sp.wait_ge(S["scores"], 2 * IMG)
            sp.dma_start(W[:, (E - 3) * WE:(E - 2) * WE], moe_w[E - 3]).then_inc(S["l_moe"], 16)
            sp.wait_ge(S["z"], NCH)
            sp.dma_start(W[:, (E - 1) * WE:E * WE], moe_w[E - 1]).then_inc(S["l_moe_late"], 16)
            sp.wait_ge(S["f2"], KD * NCH)
            sp.dma_start(W[:, (E - 2) * WE:(E - 1) * WE], moe_w[E - 2]).then_inc(S["l_moe_late"], 16)

            for t in range(NT):
                n = P if t < NT - 1 else LAST
                sp.wait_ge(S["hrowev"], t + 1)
                sp.dma_start(acc[t * P:t * P + n, :], hrow[0:n, t % 2, :]).then_inc(S[f"acc_set{t % 2}"], 16)

            sp.wait_ge(S["scattered"], 16 * 2 * NT)

            def load_tile(i, ring):
                if not isinstance(i, int) or i >= XR:
                    sp.wait_ge(S["acc_add"], 16 * (i - (XR - 1)))
                sp.dma_start(xin[:, ring, :], slots[bass.ds(i * P, P), :]).then_inc(S[f"xin{ring}"], 16)

            for i in range(XR):
                load_tile(i, i)
            with sp.Fori(1, SLOT_TILES // XR) as r:
                for j in range(XR):
                    load_tile(r * XR + j, j)

            sp.wait_ge(S["acc_add"], 16 * SLOT_TILES)
            sp.dma_start(out, acc[0:TOK, :]).then_inc(S["out_done"], 16)
            sp.wait_ge(S["out_done"], 16)

        @block.gpsimd
        def _(pool):
            done = [0]

            def link(ins):
                done[0] += 1
                ins.then_inc(S["c_pool"], 1)
                pool.wait_ge(S["c_pool"], done[0])

            pool.memset(maskb[:, :, :], 0.0)
            pool.memset(below[:, :], 1.0)
            pool.memset(head_of[:, :], 1.0)
            pool.memset(before[:, :, :], 1.0)
            pool.memset(empty[:, :], 0.0)
            link(pool.memset(ident[:, :], 0.0))
            pool.affine_select(out=ident[:, :], in_=ident[:, :], compare_op=ALU.not_equal, fill=1.0, base=0,
                               pattern=[[-1, P]], channel_multiplier=1)
            pool.affine_select(out=maskb[:, :, :], in_=maskb[:, :, :], compare_op=ALU.is_ge, fill=NEG, base=0,
                               pattern=[[0, HB], [-1, SEQ]], channel_multiplier=1)
            pool.affine_select(out=below[:, :], in_=below[:, :], compare_op=ALU.is_gt, fill=0.0, base=0,
                               pattern=[[1, P]], channel_multiplier=-1)
            pool.affine_select(out=before[:, :, :], in_=before[:, :, :], compare_op=ALU.is_gt, fill=0.0, base=0,
                               pattern=[[1, E], [-1, E]], channel_multiplier=0)
            link(pool.affine_select(out=head_of[:, :], in_=head_of[:, :], compare_op=ALU.is_ge, fill=0.0, base=0,
                                    pattern=[[-HD, HG]], channel_multiplier=1))
            pool.affine_select(out=head_of[:, :], in_=head_of[:, :], compare_op=ALU.is_ge, fill=0.0, base=HD - 1,
                               pattern=[[HD, HG]], channel_multiplier=-1)
            link(pool.iota(empty[:, D + 1:D + 2].bitcast(I32), pattern=[[0, 1]], base=TOK, channel_multiplier=1))
            pool.iota(iw[:, 0:NT], pattern=[[P, NT]], base=0, channel_multiplier=0)
            pool.iota(iw[:, NT:2 * NT], pattern=[[P, NT]], base=0, channel_multiplier=1)
            pool.iota(iw[:, 2 * NT:2 * NT + SLOT_TILES], pattern=[[1, SLOT_TILES]], base=0, channel_multiplier=0)
            pool.iota(iw[:, 2 * NT + SLOT_TILES:], pattern=[[-1, E]], base=E,
                      channel_multiplier=0).then_inc(S["c_int"], 1)

            def pair_in(p, pp):
                pool.wait_ge(S["xn"], 2 * p + 2)
                if not isinstance(p, int) or p >= 2:
                    pool.wait_ge(S["v"], 2 * p - 2)
                pool.tensor_copy(xi[:, pp, :, :], nT[:, :, bass.ds(p * (2 * SEQ), 2 * SEQ)]).then_inc(S["xi"], 2)

            def keys_out(n, pos, p):
                pool.wait_ge(S["qkev"], 2 * p + 2)
                if not isinstance(n, int) or n >= 2:
                    pool.wait_ge(S["scores"], 2 * n - 2)
                half = pos % 2 * SEQ
                pool.tensor_tensor(kx[pos % 2][:, 1, :, :],
                                   qk[:, pos // 2, 2 * KD - 1, half:half + SEQ].unsqueeze(1).broadcast_to([P, HG, SEQ]),
                                   head_of[:, :].unsqueeze(2).broadcast_to([P, HG, SEQ]),
                                   ALU.mult).then_inc(S["kx1"], 1)

            pool.wait_ge(S["tok"], NCH)
            pair_in(0, 0)
            pair_in(1, 1)
            keys_out(0, 0, 0)

            def step(i, pos, p):
                if pos % 2 == 1 and (not isinstance(i, int) or i + 3 < IMG):
                    pair_in(p + 1, (pos + 3) // 2 % 2)
                if not isinstance(i, int) or i + 1 < IMG:
                    keys_out(i + 1, (pos + 1) % CI, p)

            attention_steps(pool, step)

            def r_of(n, c):
                pool.wait_ge(S["p9"], n)
                pool.wait_ge(S["xs"], n)
                pool.tensor_tensor(rT[:, :, chunk(c)], pe[:, c % 2, :, :], xsT[:, :, chunk(c)],
                                   ALU.subtract).then_inc(S["r"], 1)

            for c in range(NCH):
                r_of(c + 1, c)
            with pool.Fori(1, ITERS) as t:
                for c in range(NCH):
                    r_of(t * NCH + (c + 1), c)

            for t in range(SLOT_TILES):
                pool.dma_start(slots[t * P:(t + 1) * P, :], empty[:, :]).then_inc(S["slots_empty"], 16)
            pool.dma_start(acc[TOK:TOK + P, :], empty[:, 0:D]).then_inc(S["acc_dummies"], 16)
            pool.wait_ge(S["slots_empty"], 16 * SLOT_TILES)
            pool.wait_ge(S["slot_no"], 1)
            for k in range(2):
                pool.wait_ge(S["row_ends"], 1)
                if k == 0:
                    pool.wait_ge(S["rowev"], NT)
                else:
                    pool.wait_ge(S["row2"], 1)
                for t in range(NT):
                    n = P if t < NT - 1 else LAST
                    pool.indirect_dma_start(
                        out=slots, out_offset=bass.IndirectOffsetOnAxis(ap=slot_i[0:n, k, t:t + 1], axis=0),
                        in_=rows[k][0:n, t, :], in_offset=None,
                    ).then_inc(S["scattered"], 16)

            pool.wait_ge(S["acc_set0"], 16 * -(-NT // 2))
            pool.wait_ge(S["acc_set1"], 16 * (NT // 2))

            pool.wait_ge(S["acc_dummies"], 16)

            for i in range(SLOT_TILES):
                pool.wait_ge(S["yev"], i + 1)
                if i > 0:
                    pool.wait_ge(S["acc_add"], 16 * i)
                pool.indirect_dma_start(
                    out=acc, out_offset=bass.IndirectOffsetOnAxis(
                        ap=xin[:, i % XR, D + 1:D + 2].bitcast(I32), axis=0),
                    in_=yt[:, i % 2, :], in_offset=None, compute_op=ALU.add,
                ).then_inc(S["acc_add"], 16)

        @block.tensor
        def _(pe_):
            mm = pe_.matmul

            def norm_mean(n, c):
                pe_.wait_ge(n.ready, n.per_chunk * (c + 1))
                if c >= len(n.mean_banks):
                    pe_.wait_ge(n.centered, c - len(n.mean_banks) + 1)
                bank = n.mean_banks[c % len(n.mean_banks)]
                for k in range(KD):
                    last = mm(PS[:, bank, 0:CT], mean_m[:, :], n.source[:, k, chunk(c)], start=k == 0,
                              stop=k == KD - 1)
                last.then_inc(n.mean, 1)

            def norm_var(n, c):
                pe_.wait_ge(n.squared, c + 1)
                if c >= len(n.var_banks):
                    pe_.wait_ge(n.var_used, c - len(n.var_banks) + 1)
                bank = n.var_banks[c % len(n.var_banks)]
                for k in range(KD):
                    last = mm(PS[:, bank, 0:CT], mean_m[:, :], sq[:, c % 2, k, :], start=k == 0, stop=k == KD - 1)
                last.then_inc(n.var, 1)

            pe_.wait_ge(S["l_tok"], 16)
            pe_.wait_ge(S["c_dve"], 1)

            def embed(c):
                pe_.wait_ge(S[f"l_pt{c}"], 16)
                if c >= 2:
                    pe_.wait_ge(S["h"], c - 1)
                for m in range(KD):
                    for k in range(KPATCH):
                        last = mm(PS[:, 2 * (c % 2) + m, 0:CP], wtok[:, k, m * P:(m + 1) * P], pt[c % 2][:, k, :],
                                  start=k == 0, stop=k == KPATCH - 1)
                last.then_inc(S["tok"], 1)

            pe_.wait_ge(S["cls"], 1)
            for s in range(NCH + 2):
                if s < NCH:
                    embed(s)
                if 0 <= s - 1 < NCH:
                    norm_mean(n0, s - 1)
                if 0 <= s - 2 < NCH:
                    norm_var(n0, s - 2)

            QK_BANK, V_BANK, T_BANK = 6, 7, 4

            def half_in(n, pos):
                pe_.wait_ge(S["xi"], n + 1)
                if not isinstance(n, int) or n >= 1:
                    pe_.wait_ge(S["qkev"], n)
                for i in range(KD):
                    m = pos % 2 * KD + i
                    for k in range(KD):
                        last = mm(PS[:, QK_BANK, i * 2 * SEQ:(i + 1) * 2 * SEQ], wqkv[:, k, m * P:(m + 1) * P],
                                  xi[:, pos // 2, k, :], start=k == 0, stop=k == KD - 1)
                last.then_inc(S["qk"], 1)

            def values(n, pos):
                if not isinstance(n, int) or n >= 2:
                    pe_.wait_ge(S["att"], n - 1)
                for k in range(KD):
                    last = mm(PS[0:SEQ, V_BANK, 0:D], xi[:, pos // 2, k, pos % 2 * SEQ:(pos % 2 + 1) * SEQ],
                              wqkv[:, k, 2 * D:3 * D], start=k == 0, stop=k == KD - 1)
                last.then_inc(S["v"], 1)

            def scores(n, pos, g):
                pe_.wait_ge(S["kx0"] if g == 0 else S["kx1"], n + 1)
                if not isinstance(n, int) or n >= 1:
                    pe_.wait_ge(S["sh"], 2 * n + g - 1)
                for b in range(2):
                    bank = PS[0:SEQ, 2 * g + b, 0:HB * SEQ]
                    mm(bank, identb[0:SEQ, 0:SEQ], maskb[0:SEQ, :, :].rearrange("p h s -> p (h s)"), start=True,
                       stop=False)
                    last = mm(bank, qk[:, pos // 2, g, pos % 2 * SEQ:(pos % 2 + 1) * SEQ],
                              kx[pos % 2][:, g, HB * b:HB * b + HB, :].rearrange("p h s -> p (h s)"), start=False,
                              stop=True)
                last.then_inc(S["scores"], 1)

            def transposes(n, g):
                pe_.wait_ge(S["ex"], 2 * n + g + 1)
                if g == 1 or not isinstance(n, int) or n >= 1:
                    pe_.wait_ge(S["pT"], 2 * n + g)
                if g == 1 and (not isinstance(n, int) or n >= 1):
                    pe_.wait_ge(S["attn"], n)
                for h in range(HG):
                    last = pe_.transpose(PS[0:SEQ, T_BANK + h // HB, (h % HB) * SEQ:(h % HB + 1) * SEQ],
                                         ex[g][0:SEQ, h, :], ident[0:SEQ, 0:SEQ])
                last.then_inc(S["T"], 1)

            def weighted(n, par, g, last_image):
                pe_.wait_ge(S["pT"], 2 * n + g + 1)
                pe_.wait_ge(S["vev"], n + 1 if last_image else n + 2)
                for h in range(HG):
                    a = (g * HG + h) * (HD + 1)
                    last = mm(PS[0:SEQ, V_BANK, a:a + HD + 1],
                              pT[g][0:SEQ, h // HB, (h % HB) * SEQ:(h % HB + 1) * SEQ],
                              va[par][0:SEQ, g * HG + h, :], start=True, stop=True)
                last.then_inc(S["PV"], 1)

            def output_transposed(n):
                pe_.wait_ge(S["att"], n + 1)
                pe_.wait_ge(S["pT"], 2 * n + 2)
                for m in range(KD):
                    a = HB * SEQ + m * SEQ
                    last = pe_.transpose(PS[:, T_BANK + 1, a:a + SEQ],
                                         att[0:SEQ, m * HG:(m + 1) * HG, :].rearrange("p h d -> p (h d)"),
                                         ident[0:SEQ, 0:SEQ])
                last.then_inc(S["aT"], 1)

            pe_.wait_ge(S["l_qkv"], 16)
            pe_.wait_ge(n0.centered, NCH)
            pe_.wait_ge(S["v2"], NCH)
            half_in(0, 0)
            half_in(1, 1)
            values(0, 0)
            half_in(2, 2)
            for g in range(KD):
                scores(0, 0, g)

            def step(i, pos, p):
                more = not isinstance(i, int) or i + 1 < IMG
                after = (pos + 1) % CI
                if not isinstance(i, int) or i + 3 < IMG:
                    half_in(i + 3, (pos + 3) % CI)
                transposes(i, 0)
                if more:
                    if isinstance(i, int) and i == 0:
                        pe_.wait_ge(S["vev"], 1)
                    values(i + 1, after)
                if not isinstance(i, int) or i > 0:
                    output_transposed(i - 1)
                for g in range(KD):
                    if g > 0:
                        transposes(i, g)
                    if more:
                        scores(i + 1, after, g)
                    weighted(i, pos % 2, g, not more)

            attention_steps(pe_, step)
            output_transposed(IMG - 1)

            def project(c):
                pe_.wait_ge(S["attn"], CI * (c + 1))
                if c >= 1:
                    pe_.wait_ge(S["ctx"], c)
                for m in range(KD):
                    for k in range(KD):
                        last = mm(PS[:, 4 + m, 0:CT], wout[:, k, m * P:(m + 1) * P], nT[:, k, chunk(c)],
                                  start=k == 0, stop=k == KD - 1)
                last.then_inc(S["o"], 1)

            def drive(c, w, rhs, begin):
                for m in range(KD):
                    for k in range(KD):
                        last = mm(PS[:, 2 * c + m, 0:CT], w[:, k, m * P:(m + 1) * P], rhs[:, k, chunk(c)],
                                  start=begin and k == 0, stop=not begin and k == KD - 1, skip_group_check=True)
                return last

            def context(c):
                pe_.wait_ge(S["ctx"], c + 1)
                drive(c, wctx, nT, True).then_inc(S["z"], 1)

            pe_.wait_ge(S["l_mid"], 16 * 3)
            pe_.wait_ge(S["attn"], IMG)
            pe_.wait_ge(S["sh"], 2 * IMG)
            project(0)
            project(1)
            norm_mean(n1, 0)
            context(0)
            project(2)
            norm_mean(n1, 1)
            norm_var(n1, 0)
            context(1)
            project(3)
            norm_mean(n1, 2)
            norm_var(n1, 1)
            norm_mean(n1, 3)
            norm_var(n1, 2)
            pe_.wait_ge(S["ctx"], NCH)
            context(2)
            norm_var(n1, 3)
            pe_.wait_ge(n1.centered, NCH)
            pe_.wait_ge(n1.rstd, NCH)
            context(3)

            for c in range(NCH):
                pe_.wait_ge(n1.done, c + 1)
                drive(c, wx, xsT, False).then_inc(S["z"], 1)
            pe_.wait_ge(S["wxd"], 1)
            with pe_.Fori(0, ITERS - 1) as t:
                for c in range(NCH):
                    pe_.wait_ge(S["e"], t * NCH + (c + 1))
                    drive(c, wxd, eT, False).then_inc(S["z"], 1)

            def ff_in(c, m):
                i = c * KF + m
                if m == 0:
                    pe_.wait_ge(n2.done, c + 1)
                if i >= 2:
                    pe_.wait_ge(S["fh"], i - 1)
                for k in range(KD):
                    last = mm(PS[:, 4 + i % 2, 0:CT], wff1[:, k, m * P:(m + 1) * P], xsT[:, k, chunk(c)],
                              start=k == 0, stop=k == KD - 1)
                last.then_inc(S["f1"], 1)

            def ff_out(c, m):
                if m == 0:
                    pe_.wait_ge(S["fh"], KF * (c + 1))
                if c >= 1:
                    pe_.wait_ge(S["ffb"], KD * (c - 1) + m + 1)
                for k in range(KF):
                    last = mm(PS[:, 6 + m, 0:CT], wff2[:, k, m * P:(m + 1) * P], fh[c % 2][:, k, :], start=k == 0,
                              stop=k == KF - 1)
                last.then_inc(S["f2"], 1)

            norm_mean(n2, 0)
            norm_mean(n2, 1)
            pe_.wait_ge(S["u"], ITERS * NCH)
            norm_mean(n2, 2)
            norm_var(n2, 0)
            norm_mean(n2, 3)
            for c in range(1, NCH):
                norm_var(n2, c)
            pe_.wait_ge(S["l_ff1"], 16)
            pe_.wait_ge(S["l_ff2"], 16)
            for c in range(2):
                for m in range(KF):
                    ff_in(c, m)
            for m in range(KD):
                ff_out(0, m)
            for c in range(2, NCH):
                for m in range(KF):
                    if m == KF // 2:
                        norm_mean(n3, c - 2)
                    ff_in(c, m)
                norm_var(n3, c - 2)
                for m in range(KD):
                    ff_out(c - 1, m)
            norm_mean(n3, 2)
            ff_out(3, 0)
            norm_var(n3, 2)
            ff_out(3, 1)

            def route_tile(t):
                pe_.wait_ge(n3.done, min((t * P + P - 1) // CT + 1, NCH))
                for k in range(KD):
                    last = mm(PS[:, 4, t * E:(t + 1) * E], nT[:, k, t * P:(t + 1) * P], gate_t[:, k, :],
                              start=k == 0, stop=k == KD - 1)
                last.then_inc(S["logit"], 1)

            def row_tile(t):
                if t >= 3:
                    pe_.wait_ge(S["rowev"], t - 2)
                for k in range(KD):
                    last = pe_.transpose(PS[:, 5 + t % 3, k * P:(k + 1) * P], nT[:, k, t * P:(t + 1) * P],
                                         ident[:, :])
                last.then_inc(S["rowT"], 1)

            pe_.wait_ge(S["l_rows"], 16 * 4)
            pe_.wait_ge(S["fh"], KF * NCH)
            ready = 3 * CT // P
            norm_mean(n3, 3)
            for t in range(3):
                route_tile(t)
            pe_.wait_ge(S["ffb"], KD * NCH)
            norm_var(n3, 3)
            for t in range(3, ready):
                route_tile(t)
            for t in range(ready):
                row_tile(t)
            for t in range(ready, NT):
                route_tile(t)
            for t in range(ready, NT):
                row_tile(t)
            pe_.wait_ge(S["member"], 1)
            pe_.wait_ge(n3.centered, NCH)
            pe_.wait_ge(n3.rstd, NCH)
            mem = member[:, :, :].rearrange("p t e -> p (t e)")
            mm(PS[:, 0, 0:NT * E], below[:, :], mem, start=True, stop=True)
            mm(PS[:, 1, 0:NT * E], ones[:, :], mem, start=True, stop=True).then_inc(S["cum"], 1)

            pe_.wait_ge(S["gates"], 1)
            for t in range(NT):
                n = P if t < NT - 1 else LAST
                last = pe_.transpose(PS[0:E, 2 + t // 4 % 2 if t < 8 else 4, (t % 4) * P:(t % 4) * P + n],
                                     gates[0:n, t, :], ident[0:n, 0:n])
            last.then_inc(S["gTt"], 1)
            pe_.wait_ge(S["gTev"], 1)
            pe_.wait_ge(S["rowev"], NT)
            for t in range(NT):
                n = P if t < NT - 1 else LAST
                bank = 6 + t % 2
                if t >= 2:
                    pe_.wait_ge(S["hrowev"], t - 1)
                for k in range(KD):
                    to = PS[0:n, bank, k * P:(k + 1) * P]
                    mm(to, gT[0:E, t * P:t * P + n], b2_rows[:, k * P:(k + 1) * P], start=True, stop=False)
                    last = mm(to, hT[:, k, t * P:t * P + n], ident[:, :], start=False, stop=True)
                last.then_inc(S["hrow"], 1)

            def input_tile(i, ring, lap):
                pe_.wait_ge(S[f"xin{ring}"], 16 * (lap + 1))
                if not isinstance(i, int) or i >= 1:
                    pe_.wait_ge(S["xtev"], i)
                for k in range(KD):
                    last = pe_.transpose(PS[:, 5, k * P:(k + 1) * P], xin[:, ring, k * P:(k + 1) * P], ident[:, :])
                last.then_inc(S["xt"], 1)

            def expert_of(i):
                return pe_.value_load(tile_expert[0:1, bass.ds(i, 1)], min_val=0, max_val=E - 1)

            def layer1(i, ring):
                w = expert_of(i) * WE
                pe_.wait_ge(S["xtev"], i + 1)
                if not isinstance(i, int) or i >= 1:
                    pe_.wait_ge(S["zev"], i)
                for h in range(EH // 512):
                    for k in range(KD):
                        last = mm(PS[:, h, :], xt[:, ring % 2, k, :], W[:, bass.ds(w + (k * EH + h * 512), 512)],
                                  start=k == 0, stop=k == KD - 1)
                last.then_inc(S["l1"], 1)

            def hidden_transposed(i):
                pe_.wait_ge(S["zev"], i + 1)
                if not isinstance(i, int) or i >= 1:
                    pe_.wait_ge(S["hrelu"], i)
                for m in range(KE):
                    last = pe_.transpose(PS[:, 2 + m // 4, (m % 4) * P:(m % 4 + 1) * P], zs[:, m * P:(m + 1) * P],
                                         ident[:, :])
                last.then_inc(S["hid"], 1)

            def layer2(i):
                w = expert_of(i) * WE
                pe_.wait_ge(S["hrelu"], i + 1)
                if not isinstance(i, int) or i >= 1:
                    pe_.wait_ge(S["yev"], i)
                for m in range(KE):
                    last = mm(PS[:, 4, 0:D], hid[:, m, :], W[:, bass.ds(w + (KD * EH + m * D), D)],
                              start=m == 0, stop=m == KE - 1)
                last.then_inc(S["l2"], 1)

            pe_.wait_ge(S["l_moe"], 16 * (E - 2))
            pe_.wait_ge(S["l_moe_late"], 16 * 2)
            pe_.wait_ge(S["tile_expert"], 1)
            input_tile(0, 0, 0)
            input_tile(1, 1, 0)
            layer1(0, 0)

            def expert_step(i, ring, lap):
                hidden_transposed(i)
                if not isinstance(i, int) or i + 1 < SLOT_TILES:
                    layer1(i + 1, (ring + 1) % XR)
                if not isinstance(i, int) or i + 2 < SLOT_TILES:
                    input_tile(i + 2, (ring + 2) % XR, lap + (ring + 2) // XR)
                layer2(i)

            expert_steps(pe_, expert_step)

        @block.scalar
        def _(act):
            f = act.activation

            def norm_square(n, c):
                act.wait_ge(n.centered, c + 1)
                f(sq[:, c % 2, :, :], xc[:, c % 2, :, :], ACT.Square).then_inc(n.squared, 1)

            def norm_rstd(n, c):
                act.wait_ge(n.var, c + 1)
                if c >= 2:
                    act.wait_ge(n.done, c - 1)
                f(rs[:, c % 2, :], PS[:, n.var_banks[c % len(n.var_banks)], 0:CT], ACT.Ln,
                  bias=eps[:, 0:1]).then_inc(n.logged, 1)
                act.wait_ge(n.logged, c + 1)
                f(rs[:, c % 2, :], rs[:, c % 2, :], ACT.Exp, scale=-0.5).then_inc(n.rstd, 1)

            act.preload_act_table_set("natural_log_exp_and_others")
            act.wait_ge(S["l_vec"], 16)
            act.wait_ge(S["c_dve"], 1)
            for s in range(NCH + 2):
                if s < NCH:
                    act.wait_ge(S["tok"], s + 1)
                    for m in range(KD):
                        to = hT[:, m, chunk(s)].rearrange("p (i t) -> p i t", i=CI)[:, :, 1:SEQ]
                        last = f(to, PS[:, 2 * (s % 2) + m, 0:CP].rearrange("p (i t) -> p i t", i=CI), ACT.Identity,
                                 bias=vcol("tok_b", m))
                    last.then_inc(S["h"], 1)
                if 0 <= s - 1 < NCH:
                    norm_square(n0, s - 1)
                if 0 <= s - 2 < NCH:
                    c = s - 2
                    norm_rstd(n0, c)
                    act.wait_ge(S["v2"], c + 1)
                    f(sq[:, c % 2, 0, :], sq[:, c % 2, 0, :], ACT.Ln, bias=eps[:, 0:1]).then_inc(S["rstd2_ln"], 1)
                    act.wait_ge(S["rstd2_ln"], c + 1)
                    f(sq[:, c % 2, 0, :], sq[:, c % 2, 0, :], ACT.Exp, scale=-0.5).then_inc(S["rstd2"], 1)

            def probabilities(n, g):
                act.wait_ge(S["sh"], 2 * n + g + 1)
                if not isinstance(n, int) or n >= 1:
                    act.wait_ge(S["T"], 2 * n + g - 1)
                f(ex[g][0:SEQ, :, :], sh[g][0:SEQ, :, :], ACT.Exp, scale=float(HD) ** -0.5).then_inc(S["ex"], 1)

            def copy_transposed(n, g):
                act.wait_ge(S["T"], 2 * n + g + 1)
                if g == 0 and (not isinstance(n, int) or n >= 1):
                    act.wait_ge(S["aT"], n)
                if not isinstance(n, int) or n >= 1:
                    act.wait_ge(S["PV"], 2 * n + g - 1)
                f(pT[g][0:SEQ, :, :], PS[0:SEQ, 4:6, 0:HB * SEQ], ACT.Copy).then_inc(S["pT"], 1)

            def copy_output(n):
                act.wait_ge(S["aT"], n + 1)
                f(nT[:, :, bass.ds(n * SEQ, SEQ)],
                  PS[:, 5, HB * SEQ:(HB + KD) * SEQ].rearrange("p (k s) -> p k s", k=KD), ACT.Copy
                  ).then_inc(S["attn"], 1)

            for g in range(KD):
                probabilities(0, g)

            def step(i, pos, p):
                copy_transposed(i, 0)
                if not isinstance(i, int) or i > 0:
                    copy_output(i - 1)
                copy_transposed(i, 1)
                if not isinstance(i, int) or i + 1 < IMG:
                    for g in range(KD):
                        probabilities(i + 1, g)

            attention_steps(act, step)
            copy_output(IMG - 1)

            def project_out(c):
                act.wait_ge(S["o"], c + 1)
                for m in range(KD):
                    last = f(nT[:, m, chunk(c)], PS[:, 4 + m, 0:CT], ACT.Identity, bias=vcol("out_b", m))
                last.then_inc(S["ctx"], 1)

            project_out(0)
            project_out(1)
            norm_square(n1, 0)
            project_out(2)
            norm_square(n1, 1)
            norm_rstd(n1, 0)
            project_out(3)
            norm_square(n1, 2)
            norm_rstd(n1, 1)
            norm_square(n1, 3)
            norm_rstd(n1, 2)
            norm_rstd(n1, 3)

            def tanh(n, c, first):
                act.wait_ge(S["z"], n + NCH)
                if first and c < 2:
                    act.wait_ge(n1.done, NCH)
                else:
                    act.wait_ge(S["e"], n - 2)
                for m in range(KD):
                    last = f(u[:, c % 2, m, :], PS[:, 2 * c + m, 0:CT], ACT.Tanh, bias=vcol("b_inl", m))
                last.then_inc(S["u"], 1)

            def decay(n, c, first):
                act.wait_ge(S["e"], n)
                if not (first and c < 2):
                    act.wait_ge(S["r"], n - 2)
                f(pe[:, c % 2, :, :], eT[:, :, chunk(c)], ACT.Copy, scale=1.0 - DT).then_inc(S["p9"], 1)

            def iteration(n, first):
                for c in range(NCH):
                    tanh(n + (c + 1), c, first)
                    if c >= 1:
                        decay(n + c, c - 1, first)
                decay(n + NCH, NCH - 1, first)

            iteration(0, True)
            with act.Fori(1, ITERS) as t:
                iteration(t * NCH, False)

            act.preload_act_table_set("natural_log_exp_and_others")
            norm_square(n2, 0)
            norm_square(n2, 1)
            norm_rstd(n2, 0)
            norm_square(n2, 2)
            norm_rstd(n2, 1)
            norm_square(n2, 3)
            norm_rstd(n2, 2)
            norm_rstd(n2, 3)

            def gelu(c, m):
                i = c * KF + m
                act.wait_ge(S["f1"], i + 1)
                if c >= 2 and m == 0:
                    act.wait_ge(S["f2"], KD * (c - 1))
                f(fh[c % 2][:, m, :], PS[:, 4 + i % 2, 0:CT], ACT.Gelu, bias=vcol("ff_b1", m)).then_inc(S["fh"], 1)

            def ff_bias(c):
                for m in range(KD):
                    act.wait_ge(S["f2"], KD * c + m + 1)
                    if c >= 1 and m == 0:
                        act.wait_ge(S["x3"], c)
                    f(ffb_buf[:, m, :], PS[:, 6 + m, 0:CT], ACT.Identity, bias=vcol("ff_b2", m)
                      ).then_inc(S["ffb"], 1)

            for c in range(2):
                for m in range(KF):
                    gelu(c, m)
            ff_bias(0)
            for c in range(2, NCH):
                for m in range(KF):
                    gelu(c, m)
                    if m == KF - 2:
                        norm_square(n3, c - 2)
                act.preload_act_table_set("natural_log_exp_and_others")
                norm_rstd(n3, c - 2)
                ff_bias(c - 1)
            norm_square(n3, 2)
            norm_rstd(n3, 2)
            ff_bias(3)
            norm_square(n3, 3)
            norm_rstd(n3, 3)

            act.wait_ge(S["hp"], NCH)
            act.wait_ge(S["f2"], KD * NCH)
            for t in range(NT):
                if t == 3 * CT // P:
                    act.wait_ge(S["shifted"], 1)
                    f(pr[:, :, :], pr[:, :, :], ACT.Exp).then_inc(S["exp"], 1)
                act.wait_ge(S["rowT"], t + 1)
                f(rows[0][:, t, 0:D], PS[:, 5 + t % 3, 0:D], ACT.Copy).then_inc(S["rowev"], 1)
            act.wait_ge(S["rowev"], NT)
            f(rows[1][:, :, 0:D], rows[0][:, :, 0:D], ACT.Copy).then_inc(S["row2"], 1)
            act.wait_ge(S["gTt"], 1)
            for b, bank in enumerate((2, 3, 4)):
                n = min(4 * P, TOK - b * 4 * P)
                last = f(gT[0:E, b * 4 * P:b * 4 * P + n], PS[0:E, bank, 0:n], ACT.Copy)
            last.then_inc(S["gTev"], 1)
            for t in range(NT):
                n = P if t < NT - 1 else LAST
                act.wait_ge(S["hrow"], t + 1)
                if t >= 2:
                    act.wait_ge(S[f"acc_set{t % 2}"], 16 * (t // 2))
                f(hrow[0:n, t % 2, :], PS[0:n, 6 + t % 2, 0:D], ACT.Copy).then_inc(S["hrowev"], 1)

            def relu(i, ring, lap):
                e = act.value_load(tile_expert[0:1, bass.ds(i, 1)], min_val=0, max_val=E - 1)
                f(b1t[:, ring % 2, :], vecs[:, bass.ds(e * KE + vec_at["moe_b1"], KE)], ACT.Copy
                  ).then_inc(S["b1t"], 1)
                act.wait_ge(S["b1t"], i + 1)
                act.wait_ge(S["hid"], i + 1)
                if not isinstance(i, int) or i > 0:
                    act.wait_ge(S["l2"], i)
                for m in range(KE):
                    last = f(hid[:, m, :], PS[:, 2 + m // 4, (m % 4) * P:(m % 4 + 1) * P], ACT.Relu,
                             bias=b1t[:, ring % 2, m:m + 1])
                last.then_inc(S["hrelu"], 1)

            act.wait_ge(S["tile_expert"], 1)
            expert_steps(act, relu)

        @block.vector
        def _(dve):
            tt, ts = dve.tensor_tensor, dve.tensor_scalar

            dve.memset(mean_m[:, :], 1.0 / D)
            dve.memset(ones[:, :], 1.0)
            dve.memset(eps[:, :], EPS).then_inc(S["c_dve"], 1)
            dve.wait_ge(S["l_vec"], 16)
            for m in range(KD):
                to = hT[:, m, :].rearrange("p (i t) -> p i t", i=IMG)[:, :, 0]
                last = dve.tensor_copy(to, vcol("cls", m).broadcast_to([P, IMG]))
            last.then_inc(S["cls"], 1)

            def norm_center(n, c):
                dve.wait_ge(n.mean, c + 1)
                tt(xc[:, c % 2, :, :], n.source[:, :, chunk(c)],
                   over_k(PS[:, n.mean_banks[c % len(n.mean_banks)], 0:CT], CT), ALU.subtract
                   ).then_inc(n.centered, 1)

            def norm_out(n, c, dst, affine=None):
                dve.wait_ge(n.rstd, c + 1)
                ins = tt(dst[:, :, chunk(c)], xc[:, c % 2, :, :], over_k(rs[:, c % 2, :], CT), ALU.mult)
                if affine is None:
                    ins.then_inc(n.done, 1)
                    return
                ins.then_inc(n.scaled, 1)
                dve.wait_ge(n.scaled, c + 1)
                for m in range(KD):
                    ins = ts(dst[:, m, chunk(c)], dst[:, m, chunk(c)], vcol(affine[0], m), vcol(affine[1], m),
                             ALU.mult, ALU.add)
                ins.then_inc(n.done, 1)

            for s in range(1, NCH + 2):
                if s - 1 < NCH:
                    norm_center(n0, s - 1)
                if s == 1:
                    dve.wait_ge(S["c_int"], 1)
                    dve.tensor_copy(fw[:, :], iw[:, :])
                    dve.tensor_copy(identb[:, :], ident[:, :]).then_inc(S["c_dve"], 1)
                    dve.wait_ge(S["c_dve"], 2)
                    ts(valid[:, :], token_no, float(TOK), None, ALU.is_lt).then_inc(S["c_dve"], 1)
                if s >= 2:
                    c = s - 2
                    var, r = PS[:, n0.var_banks[c % 2], 0:CT], rs[:, c % 2, :]
                    dve.wait_ge(n0.rstd, c + 1)
                    tt(sq[:, c % 2, 0, :], r, r, ALU.mult).then_inc(S["v2a"], 1)
                    dve.wait_ge(S["v2a"], c + 1)
                    tt(sq[:, c % 2, 0, :], sq[:, c % 2, 0, :], var, ALU.mult).then_inc(S["v2"], 1)
                    tt(x0T[:, :, chunk(c)], xc[:, c % 2, :, :], over_k(r, CT), ALU.mult).then_inc(n0.done, 1)
                    dve.wait_ge(n0.done, c + 1)
                    dve.wait_ge(S["rstd2"], c + 1)
                    tt(nT[:, :, chunk(c)], x0T[:, :, chunk(c)], over_k(sq[:, c % 2, 0, :], CT), ALU.mult
                       ).then_inc(S["xna"], 1)
                    dve.wait_ge(S["xna"], c + 1)
                    for m in range(KD):
                        last = ts(nT[:, m, chunk(c)], nT[:, m, chunk(c)], vcol("g_attn", m), vcol("b_attn", m),
                                  ALU.mult, ALU.add)
                    last.then_inc(S["xn"], CI)

            def half_out(n, pos):
                dve.wait_ge(S["qk"], n + 1)
                if not isinstance(n, int) or n >= 4:
                    dve.wait_ge(S["scores"], 2 * n - 4 - pos % 2 * 2)
                m = pos % 2 * KD
                tt(qk[:, pos // 2, m:m + KD, :], PS[:, 6, 0:KD * 2 * SEQ].rearrange("p (m s) -> p m s", m=KD),
                   vcol("qk_b", m, KD).unsqueeze(2).broadcast_to([P, KD, 2 * SEQ]), ALU.add
                   ).then_inc(S["qkev"], 1)

            def keys_out(n, pos, p):
                dve.wait_ge(S["qkev"], 2 * p + 2)
                if not isinstance(n, int) or n >= 2:
                    dve.wait_ge(S["scores"], 2 * n - 2)
                half = pos % 2 * SEQ
                tt(kx[pos % 2][:, 0, :, :],
                   qk[:, pos // 2, KD, half:half + SEQ].unsqueeze(1).broadcast_to([P, HG, SEQ]),
                   head_of[:, :].unsqueeze(2).broadcast_to([P, HG, SEQ]), ALU.mult).then_inc(S["kx0"], 1)

            def values_out(n, par):
                dve.wait_ge(S["v"], n + 1)
                tt(va[par][0:SEQ, :, 0:HD], PS[0:SEQ, 7, 0:D].rearrange("p (h d) -> p h d", h=H),
                   vb_rows[0:SEQ, :].rearrange("p (h d) -> p h d", h=H), ALU.add).then_inc(S["vev"], 1)

            def less_max(n, g):
                dve.wait_ge(S["scores"], 2 * n + g + 1)
                score = PS[0:SEQ, 2 * g:2 * g + 2, 0:HB * SEQ].rearrange("p b (h s) -> p b h s", h=HB)
                dve.tensor_reduce(mx[0:SEQ, g, :], score, AX_X, ALU.max).then_inc(S["mx"], 1)
                dve.wait_ge(S["mx"], 2 * n + g + 1)
                if not isinstance(n, int) or n >= 1:
                    dve.wait_ge(S["ex"], 2 * n + g - 1)
                tt(sh[g][0:SEQ, :, :].rearrange("p (b h) s -> p b h s", b=2), score,
                   mx[0:SEQ, g, :].rearrange("p (b h) -> p b h", b=2).unsqueeze(3).broadcast_to([SEQ, 2, HB, SEQ]),
                   ALU.subtract).then_inc(S["sh"], 1)

            def normalize(n):
                dve.wait_ge(S["PV"], 2 * n + 2)
                o = PS[0:SEQ, 7, 0:H * (HD + 1)].rearrange("p (h d) -> p h d", h=H)
                dve.reciprocal(rc[0:SEQ, :], o[:, :, HD]).then_inc(S["rc"], 1)
                dve.wait_ge(S["rc"], n + 1)
                if not isinstance(n, int) or n >= 1:
                    dve.wait_ge(S["aT"], n)
                tt(att[0:SEQ, :, :], o[:, :, 0:HD], rc[0:SEQ, :].unsqueeze(2).broadcast_to([SEQ, H, HD]), ALU.mult
                   ).then_inc(S["att"], 1)

            for i in range(2):
                dve.memset(va[i][0:SEQ, :, HD:HD + 1], 1.0)
            dve.wait_ge(S["l_rows"], 16 * 4)
            half_out(0, 0)
            half_out(1, 1)
            keys_out(0, 0, 0)
            values_out(0, 0)
            half_out(2, 2)
            for g in range(KD):
                less_max(0, g)

            def step(i, pos, p):
                after = (pos + 1) % CI
                if not isinstance(i, int) or i > 0:
                    normalize(i - 1)
                if not isinstance(i, int) or i + 1 < IMG:
                    keys_out(i + 1, after, p)
                if not isinstance(i, int) or i + 3 < IMG:
                    half_out(i + 3, (pos + 3) % CI)
                if not isinstance(i, int) or i + 1 < IMG:
                    values_out(i + 1, after % 2)
                    for g in range(KD):
                        less_max(i + 1, g)

            attention_steps(dve, step)
            normalize(IMG - 1)

            def add_attention(c):
                dve.wait_ge(S["ctx"], c + 1)
                tt(x0T[:, :, chunk(c)], x0T[:, :, chunk(c)], nT[:, :, chunk(c)], ALU.add).then_inc(S["x1"], 1)

            dve.wait_ge(S["l_mid"], 16 * 3)
            ts(wxd[:, :, :], wx[:, :, :], DT * DT, None, ALU.mult).then_inc(S["wxd"], 1)
            add_attention(0)
            add_attention(1)
            norm_center(n1, 0)
            add_attention(2)
            norm_center(n1, 1)
            norm_out(n1, 0, xsT, ("g1", "b1"))
            add_attention(3)
            norm_center(n1, 2)
            norm_out(n1, 1, xsT, ("g1", "b1"))
            norm_center(n1, 3)
            norm_out(n1, 2, xsT, ("g1", "b1"))
            norm_out(n1, 3, xsT, ("g1", "b1"))

            def advance(n, c, first):
                dve.wait_ge(S["u"], n)
                if first:
                    tt(eT[:, :, chunk(c)], u[:, c % 2, :, :], xsT[:, :, chunk(c)], ALU.subtract).then_inc(S["e"], 1)
                else:
                    dve.wait_ge(S["r"], n - NCH)
                    tt(eT[:, :, chunk(c)], u[:, c % 2, :, :], rT[:, :, chunk(c)], ALU.add).then_inc(S["e"], 1)
                dve.wait_ge(S["e"], n)
                dve.scalar_tensor_tensor(out=xsT[:, :, chunk(c)], in0=eT[:, :, chunk(c)], scalar=DT * DT,
                                         in1=xsT[:, :, chunk(c)], op0=ALU.mult, op1=ALU.add).then_inc(S["xs"], 1)

            for c in range(NCH):
                advance(c + 1, c, True)
            with dve.Fori(1, ITERS) as t:
                for c in range(NCH):
                    advance(t * NCH + (c + 1), c, False)

            dve.wait_ge(S["r"], ITERS * NCH)
            for c in range(NCH):
                dve.wait_ge(S["xs"], (ITERS - 1) * NCH + c + 1)
                tt(x0T[:, :, chunk(c)], x0T[:, :, chunk(c)], xsT[:, :, chunk(c)], ALU.add).then_inc(S["x2"], 1)
            norm_center(n2, 0)
            norm_center(n2, 1)
            norm_out(n2, 0, xsT, ("g2", "b2"))
            norm_center(n2, 2)
            norm_out(n2, 1, xsT, ("g2", "b2"))
            norm_center(n2, 3)
            norm_out(n2, 2, xsT, ("g2", "b2"))
            norm_out(n2, 3, xsT, ("g2", "b2"))

            def residual(c):
                dve.wait_ge(S["ffb"], KD * (c + 1))
                tt(x0T[:, :, chunk(c)], x0T[:, :, chunk(c)], ffb_buf[:, :, :], ALU.add).then_inc(S["x3"], 1)
                dve.wait_ge(S["x3"], c + 1)
                tt(hT[:, :, chunk(c)], hT[:, :, chunk(c)], x0T[:, :, chunk(c)], ALU.add).then_inc(S["hp"], 1)

            dve.wait_ge(S["z"], NCH)
            dve.memset(nT[:, :, TOK:TP], 0.0)
            residual(0)
            for c in range(2, NCH):
                norm_center(n3, c - 2)
                norm_out(n3, c - 2, nT)
                residual(c - 1)
            norm_center(n3, 2)
            norm_out(n3, 2, nT)
            residual(3)
            norm_center(n3, 3)
            norm_out(n3, 3, nT)

            done = [0]

            def link(ins):
                done[0] += 1
                ins.then_inc(S["route"], 1)
                dve.wait_ge(S["route"], done[0])

            def over_e(ap):
                return ap.unsqueeze(2).broadcast_to([P, NT, E])

            dve.wait_ge(S["logit"], NT)
            reduce = dve.tensor_reduce
            tok_i = iw[:, NT:2 * NT]
            for k in range(2):
                dve.tensor_copy(rows[k][:, :, D + 1].bitcast(I32), tok_i)
            link(tt(pr[:, :, :], PS[:, 4, 0:NT * E].rearrange("p (t e) -> p t e", t=NT),
                    gb_rows[:, :].unsqueeze(1).broadcast_to([P, NT, E]), ALU.add))
            link(reduce(s9[:, 0, :], pr[:, :, :], AX_X, ALU.max))
            tt(pr[:, :, :], pr[:, :, :], over_e(s9[:, 0, :]), ALU.subtract).then_inc(S["shifted"], 1)
            dve.wait_ge(S["exp"], 1)
            link(reduce(s9[:, 1, :], pr[:, :, :], AX_X, ALU.add))
            link(dve.reciprocal(s9[:, 2, :], s9[:, 1, :]))
            link(tt(pr[:, :, :], pr[:, :, :], over_e(s9[:, 2, :]), ALU.mult))

            for k in range(2):
                top = s9[:, 3 + k, :]
                link(reduce(top, pr[:, :, :], AX_X, ALU.max))
                link(tt(scr[:, :, :], pr[:, :, :], over_e(top), ALU.is_equal))
                link(tt(scr[:, :, :], scr[:, :, :], rank.unsqueeze(1).broadcast_to([P, NT, E]), ALU.mult))
                link(reduce(s9[:, 5, :], scr[:, :, :], AX_X, ALU.max))
                link(tt(oh[k][:, :, :], scr[:, :, :], over_e(s9[:, 5, :]), ALU.is_equal))
                if k == 0:
                    link(dve.scalar_tensor_tensor(out=pr[:, :, :], in0=oh[0][:, :, :], scalar=-2.0, in1=pr[:, :, :],
                                                  op0=ALU.mult, op1=ALU.add))
            link(tt(scr[:, :, :], oh[0][:, :, :], oh[1][:, :, :], ALU.add))
            tt(member[:, :, :], scr[:, :, :], over_e(valid[:, :]), ALU.mult).then_inc(S["member"], 1)

            for k in range(2):
                last = dve.tensor_copy(rows[k][:, :, D], s9[:, 3 + k, :])
            last.then_inc(S["row_ends"], 1)
            dve.wait_ge(S["member"], 1)
            link(tt(scr[:, :, :], oh[0][:, :, :], over_e(s9[:, 3, :]), ALU.mult))
            link(tt(scr2[:, :, :], oh[1][:, :, :], over_e(s9[:, 4, :]), ALU.mult))
            tt(gates[:, :, :], scr[:, :, :], scr2[:, :, :], ALU.add).then_inc(S["gates"], 1)

            dve.wait_ge(S["cum"], 1)
            count = PS[:, 1, 0:NT * E].rearrange("p (t e) -> p t e", t=NT)
            link(dve.memset(pre[:, 0, :], 0.0))
            for t in range(NT):
                link(tt(pre[:, t + 1, :], count[:, t, :], pre[:, t, :], ALU.add))
            link(tt(tiles_k[:, :, :], pre[:, NT, :].unsqueeze(2).broadcast_to([P, E, NT]),
                    multiples.unsqueeze(1).broadcast_to([P, E, NT]), ALU.is_gt))
            link(reduce(tiles_e[:, :], tiles_k[:, :, :], AX_X, ALU.add))
            link(tt(start_k[:, :, :], before[:, :, :], tiles_e[:, :].unsqueeze(1).broadcast_to([P, E, E]), ALU.mult))
            link(reduce(start_e[:, :], start_k[:, :, :], AX_X, ALU.add))
            link(tt(scr[:, :, :], PS[:, 0, 0:NT * E].rearrange("p (t e) -> p t e", t=NT), pre[:, 0:NT, :], ALU.add))
            link(ts(start_k[:, 0, :], start_e[:, :], float(P), None, ALU.mult))
            link(tt(scr[:, :, :], scr[:, :, :], start_k[:, 0, :].unsqueeze(1).broadcast_to([P, NT, E]), ALU.add))
            for k in range(2):
                link(tt(scr2[:, :, :], scr[:, :, :], oh[k][:, :, :], ALU.mult))
                link(reduce(slot_f[:, k, :], scr2[:, :, :], AX_X, ALU.add))
            dve.tensor_copy(slot_i[:, :, :], slot_f[:, :, :]).then_inc(S["slot_no"], 1)
            link(tt(te_k[:, :, :], start_e[:, 1:E].unsqueeze(1).broadcast_to([P, SLOT_TILES, E - 1]),
                    tile_no.unsqueeze(2).broadcast_to([P, SLOT_TILES, E - 1]), ALU.is_le))
            link(reduce(te[:, :], te_k[:, :, :], AX_X, ALU.add))
            dve.tensor_copy(tile_expert[:, :], te[:, :]).then_inc(S["tile_expert"], 1)

            def input_out(i, ring):
                dve.wait_ge(S["xt"], i + 1)
                if not isinstance(i, int) or i >= 2:
                    dve.wait_ge(S["l1"], i - 1)
                dve.tensor_copy(xt[:, ring % 2, :, :], PS[:, 5, 0:D].rearrange("p (k t) -> p k t", k=KD)
                                ).then_inc(S["xtev"], 1)

            def hidden_out(i):
                dve.wait_ge(S["l1"], i + 1)
                if not isinstance(i, int) or i >= 1:
                    dve.wait_ge(S["hid"], i)
                dve.tensor_copy(zs.rearrange("p (b n) -> p b n", b=2), PS[:, 0:2, :]).then_inc(S["zev"], 1)

            def gated(i, ring):
                dve.wait_ge(S["l2"], i + 1)
                if not isinstance(i, int) or i >= 2:
                    dve.wait_ge(S["acc_add"], 16 * (i - 1))
                ts(yt[:, ring % 2, :], PS[:, 4, 0:D], xin[:, ring, D:D + 1], None, ALU.mult).then_inc(S["yev"], 1)

            input_out(0, 0)
            input_out(1, 1)
            hidden_out(0)

            def expert_step(i, ring, lap):
                if not isinstance(i, int) or i + 1 < SLOT_TILES:
                    hidden_out(i + 1)
                if not isinstance(i, int) or i + 2 < SLOT_TILES:
                    input_out(i + 2, (ring + 2) % XR)
                gated(i, ring)

            expert_steps(dve, expert_step)


def by_partition(w):
    return w.reshape(w.shape[0] // P, P, -1).transpose(1, 0, 2)


def columns(b):
    return b.reshape(-1, P).T


def layout(np, a):
    x = a["x"].reshape(IMG, 3, 8, 16, 8, 16).transpose(0, 2, 4, 3, 5, 1).reshape(NCH, CP, KPATCH, P)
    w1 = a["L0_ffn_w1"].reshape(E, KD, P, EH).transpose(0, 2, 1, 3).reshape(E, P, KD * EH)
    w2 = a["L0_ffn_w2"].reshape(E, KE, P, D).transpose(0, 2, 1, 3).reshape(E, P, KE * D)
    qkv_b = a["L0_attn_qkv_b"]
    by_name = {
        "tok_b": a["L0_tok_b"], "cls": a["cls_tok"].reshape(D), "g_attn": a["L0_attn_g_attn"],
        "b_attn": a["L0_attn_b_attn"], "g1": a["L0_attn_g1"], "b1": a["L0_attn_b1"], "g2": a["L0_attn_g2"],
        "b2": a["L0_attn_b2"], "b_inl": a["L0_attn_b_inl"], "qk_b": qkv_b[0:2 * D], "out_b": a["L0_attn_out_b"],
        "ff_b1": a["L0_attn_ff_b1"], "ff_b2": a["L0_attn_ff_b2"], "moe_b1": a["L0_ffn_b1"].reshape(E * EH),
    }
    return {
        "patches": x.transpose(0, 3, 2, 1), "tok_w": by_partition(a["L0_tok_W"].T),
        "qkv_w": by_partition(a["L0_attn_qkv_w"]), "out_w": by_partition(a["L0_attn_out_w"]),
        "ctx_w": by_partition(a["L0_attn_w_ctx"]), "x_w": by_partition(a["L0_attn_w_x"]),
        "ff1_w": by_partition(a["L0_attn_ff_w1"]), "ff2_w": by_partition(a["L0_attn_ff_w2"]),
        "moe_w": np.concatenate([w1, w2], axis=2), "gate_w": by_partition(a["L0_ffn_gate_w"].T),
        "vec": np.concatenate([columns(by_name[n]) for n, _ in VEC], axis=1),
        "v_b": qkv_b[2 * D:3 * D].reshape(1, D), "gate_b": a["L0_ffn_gate_b"].reshape(1, E),
        "moe_b2": a["L0_ffn_b2"],
    }


def kernel(**inputs):
    import numpy as np
    import concourse.bacc as bacc
    from concourse.bass_utils import run_bass_kernel_spmd

    nc = bacc.Bacc("TRN2", target_bir_lowering=False, num_devices=1)
    arrays, args = {}, {}
    for name, a in layout(np, {n: np.asarray(v) for n, v in inputs.items()}).items():
        a = np.ascontiguousarray(a)
        arrays[name] = a
        args[name] = nc.dram_tensor(name, a.shape, F32, kind="ExternalInput").ap()
    out = nc.dram_tensor("out", (TOK, D), F32, kind="ExternalOutput").ap()
    vit_block(nc, out=out, **args)
    result = run_bass_kernel_spmd(nc, [arrays], core_ids=[0])
    return result.results[0]["out"].reshape(IMG, SEQ, D)
```

```python
from contextlib import ExitStack

import concourse.bass as bass
from concourse import mybir

F32 = mybir.dt.float32
I32 = mybir.dt.int32
ALU = mybir.AluOpType
ACT = mybir.ActivationFunctionType
AX_X = mybir.AxisListType.X

P = 128
IMG = 16
PATCHES = 64
SEQ = PATCHES + 1
TOK = IMG * SEQ
D = 256
KD = D // P
KPATCH = 768 // P
NCH = 4
CI = IMG // NCH
CT = CI * SEQ
CP = CI * PATCHES
H = 16
HD = D // H
HG = H // KD
HB = 4
FF = 1024
KF = FF // P
ITERS = 8
DT = 0.1
EPS = 1e-5
E = 8
EH = 1024
KE = EH // P
WE = KD * EH + KE * D
NT = -(-TOK // P)
LAST = TOK - (NT - 1) * P
TP = NT * P
SLOT_TILES = (2 * TOK + E * (P - 1)) // P
CAP = NT * P
ALL_TILES = (E - 1) * NT + SLOT_TILES - (TOK // P)
ROUTED = ((0, 2 * CT // P), (2 * CT // P, 3 * CT // P), (3 * CT // P, NT))
ROUTED_IN = (2, 2, 0)
XR = 4
PROJECTED = (0, 2, 0, 4)
NEG = -3.0e38

VEC = (("tok_b", KD), ("cls", KD), ("g_attn", KD), ("b_attn", KD), ("g1", KD), ("b1", KD), ("g2", KD), ("b2", KD),
       ("b_inl", KD), ("qk_b", 2 * KD), ("out_b", KD), ("ff_b1", KF), ("ff_b2", KD), ("moe_b1", E * KE))
NVEC = sum(n for _, n in VEC)


class Norm:

    def __init__(self, sem, name, source, ready, per_chunk, mean_banks, var_banks):
        self.source = source
        self.ready = ready
        self.per_chunk = per_chunk
        self.mean_banks = mean_banks
        self.var_banks = var_banks
        self.mean = sem(f"{name}_mean")
        self.centered = sem(f"{name}_centered")
        self.squared = sem(f"{name}_squared")
        self.var = sem(f"{name}_var")
        self.logged = sem(f"{name}_logged")
        self.rstd = sem(f"{name}_rstd")
        self.var_used = self.rstd
        self.scaled = sem(f"{name}_scaled")
        self.done = sem(f"{name}_done")


def vit_block(nc, patches, tok_w, qkv_w, out_w, ctx_w, x_w, ff1_w, ff2_w, moe_w, gate_w, vec, v_b, gate_b, moe_b2,
              out):
    slots = nc.dram_tensor("slots", (ALL_TILES * P, 2), F32, kind="Internal").ap()
    tokens = nc.dram_tensor("tokens", (TOK + P, D), F32, kind="Internal").ap()

    with ExitStack() as ctx:
        def sb(name, shape, dt=F32):
            return ctx.enter_context(nc.sbuf_tensor(name, shape, dt))

        def sem(name):
            return ctx.enter_context(nc.semaphore(name))

        def carve(flat, at, *dims):
            n = 1
            for d in dims:
                n *= d
            names = "abcd"[:len(dims)]
            view = flat[:, at:at + n].rearrange(f"p ({' '.join(names)}) -> p {' '.join(names)}",
                                                **dict(zip(names, dims)))
            return view, at + n

        W = sb("W", [P, E * WE])
        at = (E - 1) * WE
        wtok, at = carve(W, at, KPATCH, D)
        wqkv, at = carve(W, at, KD, 3 * D)
        wout, at = carve(W, at, KD, D)
        wctx, at = carve(W, at, KD, D)
        at = (E - 2) * WE
        wff1, at = carve(W, at, KD, FF)
        wff2, at = carve(W, at, KF, D)
        qk, at = carve(W, (E - 3) * WE, 2, 2 * KD, 2 * SEQ)
        rs2, at = carve(W, at, 2, CT)
        wx = sb("wx", [P, KD, D])
        wxd = sb("wxd", [P, KD, D])
        gate_t = sb("gate_t", [P, KD, E])
        vecs = sb("vecs", [P, NVEC])
        vec_at, at = {}, 0
        for name, n in VEC:
            vec_at[name] = at
            at += n

        def vcol(name, m=0, n=1):
            return vecs[:, vec_at[name] + m:vec_at[name] + m + n]

        vb_rows = sb("vb_rows", [P, D])
        gb_rows = sb("gb_rows", [P, E])
        b2_rows = sb("b2_rows", [E, D])

        streams = sb("streams", [P, KD * TOK + KD * TP])
        hT, at = carve(streams, 0, KD, TOK)
        nT, at = carve(streams, at, KD, TP)
        arena = sb("arena", [P, 4 * KD * TOK])
        x0T, _ = carve(arena, 0, KD, TOK)
        xsT, _ = carve(arena, KD * TOK, KD, TOK)
        eT, _ = carve(arena, 2 * KD * TOK, KD, TOK)
        rT, _ = carve(arena, 3 * KD * TOK, KD, TOK)
        xc = sb("xc", [P, 2, KD, CT])
        sq = sb("sq", [P, 2, KD, CT])
        rs = sb("rs", [P, 2, CT])
        pe, u = xc, sq

        pt = [carve(arena, (2 + i) * KD * TOK, KPATCH, CP)[0] for i in range(2)]
        kx = [carve(arena, (2 * KD + i) * TOK, KD, HG, SEQ)[0] for i in range(2)]
        ex, pT = [], []
        at = 3 * KD * TOK
        for i in range(2):
            view, at = carve(arena, at, HG, SEQ)
            ex.append(view)
        for i in range(2):
            view, at = carve(arena, at, 2, HB * SEQ)
            pT.append(view)
        fh = [carve(arena, (2 + i) * KD * TOK, KF, CT)[0] for i in range(2)]
        at = KD * TOK
        sh, va = [], []
        for i in range(2):
            view, at = carve(arena, at, HG, SEQ)
            sh.append(view)
        for i in range(2):
            view, at = carve(arena, at, H, HD + 1)
            va.append(view)
        att, at = carve(arena, at, H, HD)
        assert at <= 2 * KD * TOK
        xi = sb("xi", [P, 2, KD, 2 * SEQ])
        ffb_buf = xi[:, :, :, :].rearrange("p a b s -> p (a b s)").rearrange("p (k t) -> p k t", k=KD)
        mx = sb("mx", [P, 2, HG])
        rc = sb("rc", [P, H])

        rows = [carve(arena, KD * TOK + t * D, D)[0] for t in range(NT - 1)]
        rows.append(sq[:, 0, 0, 0:D])
        at = 2 * KD * TOK
        xin, at = carve(arena, at, XR, D)
        xt, at = carve(arena, at, 2, KD, P)
        hid, at = carve(arena, at, KE, P)
        gT, at = carve(arena, at, TOK)
        assert at <= 4 * KD * TOK
        w1 = [carve(arena, 0, KD, EH)[0], carve(streams, 0, KD, EH)[0]]
        y_flat = xc[:, :, :, :].rearrange("p a b c -> p (a b c)")
        hrow, at = carve(y_flat, 0, 2, D)
        yt, at = carve(y_flat, at, 2, D)

        ident = sb("ident", [P, P])
        mask = sb("mask", [P, SEQ])
        mean_m = sb("mean_m", [P, P])
        ones = sb("ones", [P, P])
        below = sb("below", [P, P])
        head_of = sb("head_of", [P, HG])
        eps = sb("eps", [P, 1])
        before = sb("before", [P, E, E])
        iw = sb("iw", [P, 2 * NT + SLOT_TILES + 2 * E], I32)
        fw = sb("fw", [P, 2 * NT + SLOT_TILES + 2 * E])
        multiples, at = carve(fw, 0, NT)
        token_no, at = carve(fw, at, NT)
        tile_no, at = carve(fw, at, SLOT_TILES)
        rank, at = carve(fw, at, E)
        region, at = carve(fw, at, E)
        valid = sb("valid", [P, NT])
        zero = sb("zero", [P, D])
        empty = sb("empty", [ALL_TILES, P, 2])
        pairs = sb("pairs", [P, 2, NT, 2])
        info = sb("info", [P, SLOT_TILES, 2])

        pr = sb("pr", [P, NT, E])
        s9 = sb("s9", [P, 6, NT])
        oh = [sb(f"oh{k}", [P, NT, E]) for k in range(2)]
        scr = sb("scr", [P, NT, E])
        scr2 = sb("scr2", [P, NT, E])
        member = sb("member", [P, NT, E])
        pre = sb("pre", [P, NT + 1, E])
        tiles_k = sb("tiles_k", [P, E, NT])
        tiles_e = sb("tiles_e", [P, E])
        start_k = sb("start_k", [P, E, E])
        past_e = sb("past_e", [P, E - 1])
        start_e = sb("start_e", [P, E])
        slot_f = sb("slot_f", [P, 2, NT])
        slot_i = sb("slot_i", [P, 2, NT], I32)
        te_k = sb("te_k", [P, SLOT_TILES, E - 1])
        te = sb("te", [P, SLOT_TILES])
        tile_expert = sb("tile_expert", [P, SLOT_TILES], I32)
        tb = sb("tb", [P, SLOT_TILES])
        tile_base = sb("tile_base", [P, SLOT_TILES], I32)
        gates = sb("gates", [P, NT, E])
        b1t = sb("b1t", [P, 2, KE])

        PS = ctx.enter_context(nc.psum_tensor("PS", [P, 8, 512], F32))

        S = {n: sem(n) for n in (
            "l_first", "l_second", "l_pt1", "l_pt2", "l_pt3", "l_vec", "l_qkv", "l_mid", "l_ff1", "l_ff2", "l_rows",
            "l_moe", "l_moe_late", "slots_empty", "acc_dummies",
            "c_pool", "c_int", "c_dve", "c_pe", "wxd",
            "tok", "h", "cls", "v2a", "v2", "rstd2_ln", "rstd2", "x0", "xna", "xnb", "xn",
            "xi", "qk", "qkev", "kx0", "kx1", "v", "vev", "scores", "masked", "mx", "sh", "ex", "T", "pT", "PV", "rc", "att",
            "aT", "attn",
            "o", "ctx", "x1", "z", "u", "e", "xs", "p9", "r",
            "x2", "f1", "fh", "f2", "ffb", "x3", "hp",
            "logit", "shifted", "exp", "rowT", "rowev", "route", "member", "cum", "gates", "gTt", "gTev", "hrow", "hrowev", "acc_set0", "acc_set1",
            "slot_no", "pairs", "numbers", "tokens_a", "tokens_b", "info0", "info1", "info2", "info3", "tile_expert", "scattered",
            "xin0", "xin1", "xin2", "xin3", "xt", "xtev", "l1", "w1", "b1t", "hrelu", "l2", "yev", "acc_add",
        )}

        n0 = Norm(sem, "n0", hT, S["h"], 1, (4,), (5, 1, 5, 4))
        n0.var_used = S["v2"]
        n1 = Norm(sem, "n1", x0T, S["x1"], 1, (6,), (7,))
        n2 = Norm(sem, "n2", x0T, S["x2"], 1, (0, 1), (2, 3))
        n3 = Norm(sem, "n3", hT, S["hp"], 1, (0,), (1,))

        def chunk(c):
            return slice(c * CT, (c + 1) * CT)

        def over_k(ap, n):
            return ap.unsqueeze(1).broadcast_to([P, KD, n])

        def attention_steps(eng, step):
            step(0, 0, 0)
            with eng.Fori(0, IMG // CI - 1) as c:
                for j in range(CI):
                    step(c * CI + (1 + j), (1 + j) % CI, c * (CI // 2) + (2 + j) // 2)
            for i in range(IMG - 3, IMG):
                step(i, i % CI, (i + 1) // 2)

        def expert_steps(eng, step):
            step(0, 0, 0)
            with eng.Fori(0, SLOT_TILES // XR - 1) as r:
                for j in range(XR):
                    step(r * XR + (1 + j), (1 + j) % XR, r + (1 + j) // XR)
            for i in range(SLOT_TILES - 3, SLOT_TILES):
                step(i, i % XR, i // XR)

        block = ctx.enter_context(nc.Block())

        @block.sync
        def _(sp):
            half = KPATCH // 2
            for i, signal in enumerate(("l_first", "l_second")):
                sp.dma_start(wtok[:, i * half:(i + 1) * half, :], tok_w[:, i * half:(i + 1) * half, :]
                             ).then_inc(S[signal], 16)
                sp.dma_start(pt[0][:, i * half:(i + 1) * half, :], patches[0][:, i * half:(i + 1) * half, :]
                             ).then_inc(S[signal], 16)
            sp.dma_start(pt[1], patches[1]).then_inc(S["l_pt1"], 16)
            sp.dma_start(vecs[:, :], vec).then_inc(S["l_vec"], 16)
            sp.dma_start(wqkv, qkv_w).then_inc(S["l_qkv"], 16)
            sp.dma_start(vb_rows[:, :], v_b.broadcast_to([P, D])).then_inc(S["l_rows"], 16)
            sp.dma_start(gb_rows[:, :], gate_b.broadcast_to([P, E])).then_inc(S["l_rows"], 16)
            sp.dma_start(b2_rows[:, :], moe_b2).then_inc(S["l_rows"], 16)
            sp.dma_start(gate_t[:, :, :], gate_w).then_inc(S["l_rows"], 16)
            for c in range(2, NCH):
                sp.wait_ge(S["tok"], c - 1)
                sp.dma_start(pt[c % 2], patches[c]).then_inc(S[f"l_pt{c}"], 16)
            sp.dma_start(wout, out_w).then_inc(S["l_mid"], 16)
            sp.dma_start(wctx, ctx_w).then_inc(S["l_mid"], 16)
            sp.dma_start(wx[:, :, :], x_w).then_inc(S["l_mid"], 16)
            sp.dma_start(wff1, ff1_w).then_inc(S["l_ff1"], 16)
            sp.dma_start(wff2, ff2_w).then_inc(S["l_ff2"], 16)
            for e in range(E - 3):
                sp.dma_start(W[:, e * WE:(e + 1) * WE], moe_w[e]).then_inc(S["l_moe"], 16)
            sp.wait_ge(S["scores"], 2 * IMG)
            sp.dma_start(W[:, (E - 3) * WE:(E - 2) * WE], moe_w[E - 3]).then_inc(S["l_moe"], 16)
            sp.wait_ge(S["z"], 2 * NCH)
            sp.dma_start(W[:, (E - 1) * WE:E * WE], moe_w[E - 1]).then_inc(S["l_moe_late"], 16)

            def token_rows(t, signal):
                sp.wait_ge(S["rowev"], t + 1)
                sp.dma_start(tokens[t * P:(t + 1) * P, :], rows[t]).then_inc(S[signal], 16)

            for t in range(*ROUTED[0]):
                token_rows(t, "tokens_a")
            sp.wait_ge(S["f2"], KD * NCH)
            sp.dma_start(W[:, (E - 2) * WE:(E - 1) * WE], moe_w[E - 2]).then_inc(S["l_moe_late"], 16)
            for t in range(ROUTED[0][1], NT):
                token_rows(t, "tokens_b")

            sp.wait_ge(S["tile_expert"], 1)
            sp.wait_ge(S["scattered"], 16 * 2 * NT)
            for i in range(SLOT_TILES):
                base = sp.value_load(tile_base[0:1, i:i + 1], min_val=0, max_val=(ALL_TILES - 1) * P)
                if i >= XR:
                    sp.wait_ge(S[f"info{i % XR}"], 16 * (i // XR))
                sp.dma_start(info[:, i, :], slots[bass.ds(base, P), :]).then_inc(S[f"info{i % XR}"], 16)

            sp.wait_ge(S["acc_add"], 16 * SLOT_TILES)

        @block.gpsimd
        def _(pool):
            done = [0]

            def link(ins):
                done[0] += 1
                ins.then_inc(S["c_pool"], 1)
                pool.wait_ge(S["c_pool"], done[0])

            pool.memset(mask[:, :], 0.0)
            pool.memset(below[:, :], 1.0)
            pool.memset(head_of[:, :], 1.0)
            pool.memset(before[:, :, :], 1.0)
            pool.memset(empty[:, :, :], 0.0)
            pool.memset(zero[:, :], 0.0)
            link(pool.memset(ident[:, :], 0.0))
            pool.affine_select(out=ident[:, :], in_=ident[:, :], compare_op=ALU.not_equal, fill=1.0, base=0,
                               pattern=[[-1, P]], channel_multiplier=1)
            pool.affine_select(out=mask[:, :], in_=mask[:, :], compare_op=ALU.is_ge, fill=NEG, base=0,
                               pattern=[[-1, SEQ]], channel_multiplier=1)
            pool.affine_select(out=below[:, :], in_=below[:, :], compare_op=ALU.is_gt, fill=0.0, base=0,
                               pattern=[[1, P]], channel_multiplier=-1)
            pool.affine_select(out=before[:, :, :], in_=before[:, :, :], compare_op=ALU.is_gt, fill=0.0, base=0,
                               pattern=[[1, E], [-1, E]], channel_multiplier=0)
            link(pool.affine_select(out=head_of[:, :], in_=head_of[:, :], compare_op=ALU.is_ge, fill=0.0, base=0,
                                    pattern=[[-HD, HG]], channel_multiplier=1))
            pool.affine_select(out=head_of[:, :], in_=head_of[:, :], compare_op=ALU.is_ge, fill=0.0, base=HD - 1,
                               pattern=[[HD, HG]], channel_multiplier=-1)
            link(pool.iota(empty[:, :, 1].bitcast(I32), pattern=[[1, P]], base=TOK, channel_multiplier=0))
            pool.dma_start(slots.rearrange("(t p) c -> t (p c)", p=P),
                           empty[:, :, :].rearrange("t p c -> t (p c)")).then_inc(S["slots_empty"], 16)
            pool.dma_start(out[TOK:TOK + P, :], zero[:, :]).then_inc(S["acc_dummies"], 16)
            pool.dma_start(tokens[CAP:TOK + P, :], zero[0:TOK + P - CAP, :]).then_inc(S["acc_dummies"], 16)
            pool.iota(iw[:, 0:NT], pattern=[[P, NT]], base=0, channel_multiplier=0)
            pool.iota(iw[:, NT:2 * NT], pattern=[[P, NT]], base=0, channel_multiplier=1)
            pool.iota(iw[:, 2 * NT:2 * NT + SLOT_TILES], pattern=[[1, SLOT_TILES]], base=0, channel_multiplier=0)
            pool.iota(iw[:, 2 * NT + SLOT_TILES:2 * NT + SLOT_TILES + E], pattern=[[-1, E]], base=E,
                      channel_multiplier=0)
            pool.iota(iw[:, 2 * NT + SLOT_TILES + E:], pattern=[[CAP, E]], base=0,
                      channel_multiplier=0).then_inc(S["c_int"], 1)

            def pair_in(p, pp):
                pool.wait_ge(S["xn"], 2 * p + 2)
                if not isinstance(p, int) or p >= 2:
                    pool.wait_ge(S["v"], 2 * p - 2)
                pool.tensor_copy(xi[:, pp, :, :], nT[:, :, bass.ds(p * (2 * SEQ), 2 * SEQ)]).then_inc(S["xi"], 2)

            def keys_out(n, pos, p):
                pool.wait_ge(S["qkev"], 2 * p + 2)
                if not isinstance(n, int) or n >= 2:
                    pool.wait_ge(S["scores"], 2 * n - 2)
                half = pos % 2 * SEQ
                pool.tensor_tensor(kx[pos % 2][:, 1, :, :],
                                   qk[:, pos // 2, 2 * KD - 1, half:half + SEQ].unsqueeze(1).broadcast_to([P, HG, SEQ]),
                                   head_of[:, :].unsqueeze(2).broadcast_to([P, HG, SEQ]),
                                   ALU.mult).then_inc(S["kx1"], 1)

            def affine(c):
                pool.wait_ge(S["xna"], c + 1)
                for m in range(KD):
                    part = nT[:, m, chunk(c)]
                    last = pool.tensor_scalar(part, part, vcol("g_attn", m), vcol("b_attn", m), ALU.mult, ALU.add)
                last.then_inc(S["xn"], CI)

            pool.wait_ge(S["l_vec"], 16)
            affine(0)
            pair_in(0, 0)
            pair_in(1, 1)
            affine(1)
            pool.wait_ge(S["tok"], NCH)
            keys_out(0, 0, 0)

            def step(i, pos, p):
                if pos % 2 == 1 and (not isinstance(i, int) or i + 3 < IMG):
                    pair_in(p + 1, (pos + 3) // 2 % 2)
                if not isinstance(i, int) or i + 1 < IMG:
                    keys_out(i + 1, (pos + 1) % CI, p)

            attention_steps(pool, step)

            def r_of(n, c):
                pool.wait_ge(S["p9"], n)
                pool.wait_ge(S["xs"], n)
                pool.tensor_tensor(rT[:, :, chunk(c)], pe[:, c % 2, :, :], xsT[:, :, chunk(c)],
                                   ALU.subtract).then_inc(S["r"], 1)

            for c in range(NCH):
                r_of(c + 1, c)
            with pool.Fori(1, ITERS - 1) as t:
                for c in range(NCH):
                    r_of(t * NCH + (c + 1), c)

            pool.wait_ge(S["slots_empty"], 16)
            pool.wait_ge(S["numbers"], 1)
            for batch, (first, behind) in enumerate(ROUTED):
                pool.wait_ge(S["pairs"], batch + 1)
                pool.wait_ge(S["slot_no"], batch + 1)
                for t in range(first, behind):
                    n = P if t < NT - 1 else LAST
                    for k in range(2):
                        pool.indirect_dma_start(
                            out=slots, out_offset=bass.IndirectOffsetOnAxis(ap=slot_i[0:n, k, t:t + 1], axis=0),
                            in_=pairs[0:n, k, t, :], in_offset=None,
                        ).then_inc(S["scattered"], 16)

            def gather(i):
                pool.wait_ge(S[f"info{i % XR}"], 16 * (i // XR + 1))
                if i >= XR:
                    pool.wait_ge(S["xt"], i - XR + 1)
                pool.indirect_dma_start(
                    out=xin[:, i % XR, :], out_offset=None, in_=tokens,
                    in_offset=bass.IndirectOffsetOnAxis(ap=info[:, i, 1:2].bitcast(I32), axis=0),
                ).then_inc(S[f"xin{i % XR}"], 16)

            def add_rows(i):
                pool.wait_ge(S["yev"], i + 1)
                if i > 0:
                    pool.wait_ge(S["acc_add"], 16 * i)
                pool.indirect_dma_start(
                    out=out, out_offset=bass.IndirectOffsetOnAxis(ap=info[:, i, 1:2].bitcast(I32), axis=0),
                    in_=yt[:, i % 2, :], in_offset=None, compute_op=ALU.add,
                ).then_inc(S["acc_add"], 16)

            pool.wait_ge(S["acc_dummies"], 16 * 2)
            pool.wait_ge(S["tokens_a"], 16 * ROUTED[0][1])
            pool.wait_ge(S["tokens_b"], 16 * (NT - ROUTED[0][1]))
            pool.wait_ge(S["fh"], KF * NCH)
            pool.wait_ge(S["f2"], KD * NCH)
            for i in range(XR - 1):
                gather(i)
            pool.wait_ge(S["acc_set0"], 16 * -(-NT // 2))
            pool.wait_ge(S["acc_set1"], 16 * (NT // 2))
            for i in range(SLOT_TILES):
                if i + XR - 1 < SLOT_TILES:
                    gather(i + XR - 1)
                add_rows(i)

        @block.tensor
        def _(pe_):
            mm = pe_.matmul

            def norm_mean(n, c):
                pe_.wait_ge(n.ready, n.per_chunk * (c + 1))
                if c >= len(n.mean_banks):
                    pe_.wait_ge(n.centered, c - len(n.mean_banks) + 1)
                bank = n.mean_banks[c % len(n.mean_banks)]
                for k in range(KD):
                    last = mm(PS[:, bank, 0:CT], mean_m[:, :], n.source[:, k, chunk(c)], start=k == 0,
                              stop=k == KD - 1)
                last.then_inc(n.mean, 1)

            def norm_var(n, c):
                pe_.wait_ge(n.squared, c + 1)
                if c >= len(n.var_banks):
                    pe_.wait_ge(n.var_used, c - len(n.var_banks) + 1)
                bank = n.var_banks[c % len(n.var_banks)]
                for k in range(KD):
                    last = mm(PS[:, bank, 0:CT], mean_m[:, :], sq[:, c % 2, k, :], start=k == 0, stop=k == KD - 1)
                last.then_inc(n.var, 1)

            def embed(c):
                if c >= 1:
                    pe_.wait_ge(S[f"l_pt{c}"], 16)
                if c >= 2:
                    pe_.wait_ge(S["h"], c - 1)
                half = KPATCH // 2
                for part, signal in enumerate(("l_first", "l_second")):
                    if c == 0:
                        pe_.wait_ge(S[signal], 16 * 2)
                    for m in range(KD):
                        for k in range(part * half, (part + 1) * half):
                            last = mm(PS[:, 2 * (c % 2) + m, 0:CP], wtok[:, k, m * P:(m + 1) * P], pt[c % 2][:, k, :],
                                      start=k == 0, stop=k == KPATCH - 1)
                last.then_inc(S["tok"], 1)

            for s in range(NCH):
                embed(s)
                if s == 0:
                    pe_.wait_ge(S["c_dve"], 1)
                    pe_.wait_ge(S["cls"], 1)
                if s >= 1:
                    norm_mean(n0, s - 1)
                if s >= 2:
                    norm_var(n0, s - 2)

            QK_BANK, V_BANK, T_BANK = 6, 7, 4

            def half_in(n, pos):
                pe_.wait_ge(S["xi"], n + 1)
                if not isinstance(n, int) or n >= 1:
                    pe_.wait_ge(S["qkev"], n)
                for i in range(KD):
                    m = pos % 2 * KD + i
                    for k in range(KD):
                        last = mm(PS[:, QK_BANK, i * 2 * SEQ:(i + 1) * 2 * SEQ], wqkv[:, k, m * P:(m + 1) * P],
                                  xi[:, pos // 2, k, :], start=k == 0, stop=k == KD - 1)
                last.then_inc(S["qk"], 1)

            def values(n, pos):
                if not isinstance(n, int) or n >= 2:
                    pe_.wait_ge(S["att"], n - 1)
                for k in range(KD):
                    last = mm(PS[0:SEQ, V_BANK, 0:D], xi[:, pos // 2, k, pos % 2 * SEQ:(pos % 2 + 1) * SEQ],
                              wqkv[:, k, 2 * D:3 * D], start=k == 0, stop=k == KD - 1)
                last.then_inc(S["v"], 1)

            def scores(n, pos, g):
                pe_.wait_ge(S["kx0"] if g == 0 else S["kx1"], n + 1)
                if not isinstance(n, int) or n >= 1:
                    pe_.wait_ge(S["masked"], 2 * n + g - 1)
                for b in range(2):
                    bank = PS[0:SEQ, 2 * g + b, 0:HB * SEQ]
                    last = mm(bank, qk[:, pos // 2, g, pos % 2 * SEQ:(pos % 2 + 1) * SEQ],
                              kx[pos % 2][:, g, HB * b:HB * b + HB, :].rearrange("p h s -> p (h s)"), start=True,
                              stop=True)
                last.then_inc(S["scores"], 1)

            def transposes(n, g):
                pe_.wait_ge(S["ex"], 2 * n + g + 1)
                if g == 1 or not isinstance(n, int) or n >= 1:
                    pe_.wait_ge(S["pT"], 2 * n + g)
                if g == 1 and (not isinstance(n, int) or n >= 1):
                    pe_.wait_ge(S["attn"], n)
                for h in range(HG):
                    last = pe_.transpose(PS[0:SEQ, T_BANK + h // HB, (h % HB) * SEQ:(h % HB + 1) * SEQ],
                                         ex[g][0:SEQ, h, :], ident[0:SEQ, 0:SEQ])
                last.then_inc(S["T"], 1)

            def weighted(n, par, g, last_image):
                pe_.wait_ge(S["pT"], 2 * n + g + 1)
                pe_.wait_ge(S["vev"], n + 1 if last_image else n + 2)
                for h in range(HG):
                    a = (g * HG + h) * (HD + 1)
                    last = mm(PS[0:SEQ, V_BANK, a:a + HD + 1],
                              pT[g][0:SEQ, h // HB, (h % HB) * SEQ:(h % HB + 1) * SEQ],
                              va[par][0:SEQ, g * HG + h, :], start=True, stop=True)
                last.then_inc(S["PV"], 1)

            def output_transposed(n):
                pe_.wait_ge(S["att"], n + 1)
                pe_.wait_ge(S["pT"], 2 * n + 2)
                for m in range(KD):
                    a = HB * SEQ + m * SEQ
                    last = pe_.transpose(PS[:, T_BANK + 1, a:a + SEQ],
                                         att[0:SEQ, m * HG:(m + 1) * HG, :].rearrange("p h d -> p (h d)"),
                                         ident[0:SEQ, 0:SEQ])
                last.then_inc(S["aT"], 1)

            pe_.wait_ge(S["l_qkv"], 16)
            half_in(0, 0)
            norm_mean(n0, 3)
            pe_.wait_ge(S["v2"], 1)
            norm_var(n0, 2)
            half_in(1, 1)
            values(0, 0)
            norm_var(n0, 3)
            half_in(2, 2)
            pe_.wait_ge(S["v2"], 2)
            scores(0, 0, 0)
            scores(0, 0, 1)

            def project(c):
                pe_.wait_ge(S["attn"], CI * (c + 1))
                if c == 0:
                    pe_.wait_ge(S["l_mid"], 16 * 3)
                    pe_.wait_ge(S["masked"], 2 * IMG)
                if c == 2:
                    pe_.wait_ge(S["ctx"], 1)
                for m in range(KD):
                    for k in range(KD):
                        last = mm(PS[:, PROJECTED[c] + m, 0:CT], wout[:, k, m * P:(m + 1) * P], nT[:, k, chunk(c)],
                                  start=k == 0, stop=k == KD - 1)
                last.then_inc(S["o"], 1)

            def step(i, pos, p):
                more = not isinstance(i, int) or i + 1 < IMG
                after = (pos + 1) % CI
                if not isinstance(i, int) or i + 3 < IMG:
                    half_in(i + 3, (pos + 3) % CI)
                if isinstance(i, int) and i == 0:
                    pe_.wait_ge(S["vev"], 1)
                    values(i + 1, after)
                    pe_.wait_ge(S["v2"], NCH)
                transposes(i, 0)
                if not more:
                    project(0)
                if more and not (isinstance(i, int) and i == 0):
                    values(i + 1, after)
                if not isinstance(i, int) or i > 0:
                    output_transposed(i - 1)
                for g in range(KD):
                    if g > 0:
                        transposes(i, g)
                        if not more:
                            project(1)
                    if more:
                        scores(i + 1, after, g)
                    weighted(i, pos % 2, g, not more)

            attention_steps(pe_, step)
            norm_mean(n1, 0)
            output_transposed(IMG - 1)

            def drive(c, w, rhs, begin):
                for m in range(KD):
                    for k in range(KD):
                        last = mm(PS[:, 2 * c + m, 0:CT], w[:, k, m * P:(m + 1) * P], rhs[:, k, chunk(c)],
                                  start=begin and k == 0, stop=not begin and k == KD - 1, skip_group_check=True)
                return last

            def context(c):
                pe_.wait_ge(S["ctx"], (3, 2, NCH, NCH)[c])
                drive(c, wctx, nT, True).then_inc(S["z"], 1)

            def first_drive(c):
                pe_.wait_ge(n1.done, c + 1)
                drive(c, wx, xsT, False).then_inc(S["z"], 1)

            project(2)
            norm_mean(n1, 1)
            project(3)
            norm_var(n1, 0)
            norm_mean(n1, 2)
            norm_var(n1, 1)
            context(0)
            norm_mean(n1, 3)
            context(1)
            norm_var(n1, 2)
            context(2)
            norm_var(n1, 3)

            first_drive(0)
            first_drive(1)
            pe_.wait_ge(n1.centered, NCH)
            pe_.wait_ge(n1.rstd, NCH)
            context(3)
            first_drive(2)
            first_drive(3)
            pe_.wait_ge(S["wxd"], 1)
            with pe_.Fori(0, ITERS - 1) as t:
                for c in range(NCH):
                    pe_.wait_ge(S["e"], t * NCH + (c + 1))
                    drive(c, wxd, eT, False).then_inc(S["z"], 1)

            def ff_in(c, m):
                i = c * KF + m
                if m == 0:
                    pe_.wait_ge(n2.done, c + 1)
                if i >= 2:
                    pe_.wait_ge(S["fh"], i - 1)
                for k in range(KD):
                    last = mm(PS[:, 4 + i % 2, 0:CT], wff1[:, k, m * P:(m + 1) * P], xsT[:, k, chunk(c)],
                              start=k == 0, stop=k == KD - 1)
                last.then_inc(S["f1"], 1)

            def ff_out(c, m):
                if m == 0:
                    pe_.wait_ge(S["fh"], KF * (c + 1))
                if c >= 1:
                    pe_.wait_ge(S["ffb"], KD * (c - 1) + m + 1)
                for k in range(KF):
                    last = mm(PS[:, 6 + m, 0:CT], wff2[:, k, m * P:(m + 1) * P], fh[c % 2][:, k, :], start=k == 0,
                              stop=k == KF - 1)
                last.then_inc(S["f2"], 1)

            norm_mean(n2, 0)
            norm_mean(n2, 1)
            pe_.wait_ge(S["u"], (ITERS - 1) * NCH + 2)
            norm_var(n2, 0)
            norm_mean(n2, 2)
            norm_var(n2, 1)
            norm_mean(n2, 3)
            norm_var(n2, 2)
            pe_.wait_ge(S["l_ff1"], 16)
            pe_.wait_ge(S["l_ff2"], 16)
            pe_.wait_ge(S["u"], ITERS * NCH)
            for m in range(2):
                ff_in(0, m)
            for c in range(2):
                for m in range(2 if c == 0 else 0, KF):
                    ff_in(c, m)
                if c == 0:
                    norm_var(n2, 3)
            for m in range(KD):
                ff_out(0, m)
            for c in range(2, NCH):
                for m in range(KF):
                    if m == KF // 2:
                        norm_mean(n3, c - 2)
                    ff_in(c, m)
                norm_var(n3, c - 2)
                ff_out(c - 1, 0)
                if c < NCH - 1:
                    ff_out(c - 1, 1)

            def route_tile(t, bank):
                pe_.wait_ge(n3.done, min((t * P + P - 1) // CT + 1, NCH))
                for k in range(KD):
                    last = mm(PS[:, bank, t * E:(t + 1) * E], nT[:, k, t * P:(t + 1) * P], gate_t[:, k, :],
                              start=k == 0, stop=k == KD - 1)
                last.then_inc(S["logit"], 1)

            def row_tile(t):
                if t >= 2:
                    pe_.wait_ge(S["rowev"], t - 1)
                for k in range(KD):
                    last = pe_.transpose(PS[:, 3 + t % 2 * 2, k * P:(k + 1) * P], nT[:, k, t * P:(t + 1) * P],
                                         ident[:, :])
                last.then_inc(S["rowT"], 1)

            def ranks_and_counts(batch):
                pe_.wait_ge(S["member"], batch + 1)
                first, behind = ROUTED[batch]
                mem = member[:, first:behind, :].rearrange("p t e -> p (t e)")
                bank = ROUTED_IN[batch]
                mm(PS[:, bank, (NT + first) * E:(NT + behind) * E], below[:, :], mem, start=True, stop=True)
                mm(PS[:, bank, (2 * NT + first) * E:(2 * NT + behind) * E], ones[:, :], mem, start=True, stop=True
                   ).then_inc(S["cum"], 1)

            pe_.wait_ge(S["l_rows"], 16 * 4)
            for t in range(*ROUTED[0]):
                route_tile(t, ROUTED_IN[0])
            ff_out(2, 1)
            pe_.wait_ge(S["fh"], KF * NCH)
            for t in range(*ROUTED[0]):
                row_tile(t)
            ff_out(3, 0)
            norm_mean(n3, 2)
            ranks_and_counts(0)
            ff_out(3, 1)
            norm_var(n3, 2)
            norm_mean(n3, 3)

            def gates_transposed(batch):
                pe_.wait_ge(S["gates"], batch + 1)
                if batch >= 1:
                    pe_.wait_ge(S["gTev"], batch)
                first, behind = ROUTED[batch]
                for t in range(first, behind):
                    n = P if t < NT - 1 else LAST
                    last = pe_.transpose(PS[0:E, 4, (t - first) * P:(t - first) * P + n],
                                         gates[0:n, t, :], ident[0:n, 0:n])
                last.then_inc(S["gTt"], 1)

            def residual_row(t):
                n = P if t < NT - 1 else LAST
                bank = 6 + t % 2
                if t >= 2:
                    pe_.wait_ge(S["hrowev"], t - 1)
                for k in range(KD):
                    to = PS[0:n, bank, k * P:(k + 1) * P]
                    mm(to, gT[0:E, t * P:t * P + n], b2_rows[:, k * P:(k + 1) * P], start=True, stop=False)
                    last = mm(to, hT[:, k, t * P:t * P + n], ident[:, :], start=False, stop=True)
                last.then_inc(S["hrow"], 1)

            pe_.wait_ge(S["slot_no"], 1)
            for t in range(*ROUTED[1]):
                route_tile(t, ROUTED_IN[1])
            gates_transposed(0)
            pe_.wait_ge(S["ffb"], KD * NCH)
            pe_.wait_ge(S["gTev"], 1)
            residual_row(0)
            norm_var(n3, 3)
            for t in range(*ROUTED[1]):
                row_tile(t)
            for t in range(1, ROUTED[0][1]):
                residual_row(t)
            ranks_and_counts(1)
            for t in range(*ROUTED[2]):
                route_tile(t, ROUTED_IN[2])
            for t in range(*ROUTED[2]):
                row_tile(t)
            ranks_and_counts(2)
            for batch in (1, 2):
                gates_transposed(batch)
                pe_.wait_ge(S["gTev"], batch + 1)
                for t in range(*ROUTED[batch]):
                    residual_row(t)
            pe_.wait_ge(S["rowev"], NT)

            def input_tile(i, ring, lap):
                pe_.wait_ge(S[f"xin{ring}"], 16 * (lap + 1))
                if not isinstance(i, int) or i >= 1:
                    pe_.wait_ge(S["xtev"], i)
                for k in range(KD):
                    last = pe_.transpose(PS[:, 5, k * P:(k + 1) * P], xin[:, ring, k * P:(k + 1) * P], ident[:, :])
                last.then_inc(S["xt"], 1)

            def expert_of(i):
                return pe_.value_load(tile_expert[0:1, bass.ds(i, 1)], min_val=0, max_val=E - 1)

            def layer1(i, ring):
                par = ring % 2
                pe_.wait_ge(S["xtev"], i + 1)
                pe_.wait_ge(S["w1"], i + 1)
                if not isinstance(i, int) or i >= 2:
                    pe_.wait_ge(S["hrelu"], i - 1)
                for m in range(KE):
                    to = PS[:, 2 * par + m // 4, (m % 4) * P:(m % 4 + 1) * P]
                    for k in range(KD):
                        last = mm(to, w1[par][:, k, m * P:(m + 1) * P], xt[:, par, k, :], start=k == 0, stop=k == KD - 1)
                last.then_inc(S["l1"], 1)

            def layer2(i):
                w = expert_of(i) * WE
                pe_.wait_ge(S["hrelu"], i + 1)
                if not isinstance(i, int) or i >= 1:
                    pe_.wait_ge(S["yev"], i)
                for m in range(KE):
                    last = mm(PS[:, 4, 0:D], hid[:, m, :], W[:, bass.ds(w + (KD * EH + m * D), D)],
                              start=m == 0, stop=m == KE - 1)
                last.then_inc(S["l2"], 1)

            pe_.wait_ge(S["l_moe"], 16 * (E - 2))
            pe_.wait_ge(S["l_moe_late"], 16 * 2)
            pe_.wait_ge(S["tile_expert"], 1)
            input_tile(0, 0, 0)
            input_tile(1, 1, 0)
            layer1(0, 0)

            def expert_step(i, ring, lap):
                if not isinstance(i, int) or i + 1 < SLOT_TILES:
                    layer1(i + 1, (ring + 1) % XR)
                if not isinstance(i, int) or i + 2 < SLOT_TILES:
                    input_tile(i + 2, (ring + 2) % XR, lap + (ring + 2) // XR)
                layer2(i)

            expert_steps(pe_, expert_step)

        @block.scalar
        def _(act):
            f = act.activation

            def norm_square(n, c):
                act.wait_ge(n.centered, c + 1)
                f(sq[:, c % 2, :, :], xc[:, c % 2, :, :], ACT.Square).then_inc(n.squared, 1)

            def norm_rstd(n, c):
                act.wait_ge(n.var, c + 1)
                if c >= 2:
                    act.wait_ge(n.done, c - 1)
                f(rs[:, c % 2, :], PS[:, n.var_banks[c % len(n.var_banks)], 0:CT], ACT.Ln,
                  bias=eps[:, 0:1]).then_inc(n.logged, 1)
                act.wait_ge(n.logged, c + 1)
                f(rs[:, c % 2, :], rs[:, c % 2, :], ACT.Exp, scale=-0.5).then_inc(n.rstd, 1)

            act.preload_act_table_set("natural_log_exp_and_others")
            act.wait_ge(S["l_vec"], 16)
            act.wait_ge(S["c_dve"], 1)
            def patches_out(c):
                act.wait_ge(S["tok"], c + 1)
                for m in range(KD):
                    to = hT[:, m, chunk(c)].rearrange("p (i t) -> p i t", i=CI)[:, :, 1:SEQ]
                    last = f(to, PS[:, 2 * (c % 2) + m, 0:CP].rearrange("p (i t) -> p i t", i=CI), ACT.Identity,
                             bias=vcol("tok_b", m))
                last.then_inc(S["h"], 1)

            def second_rstd(c):
                act.wait_ge(S["v2"], c + 1)
                f(rs2[:, c % 2, :], rs2[:, c % 2, :], ACT.Ln, bias=eps[:, 0:1]).then_inc(S["rstd2_ln"], 1)
                act.wait_ge(S["rstd2_ln"], c + 1)
                f(rs2[:, c % 2, :], rs2[:, c % 2, :], ACT.Exp, scale=-0.5).then_inc(S["rstd2"], 1)

            patches_out(0)
            patches_out(1)
            norm_square(n0, 0)
            patches_out(2)
            norm_square(n0, 1)
            norm_rstd(n0, 0)
            second_rstd(0)
            patches_out(3)
            norm_square(n0, 2)
            norm_rstd(n0, 1)
            second_rstd(1)
            norm_square(n0, 3)
            norm_rstd(n0, 2)

            def affine(c):
                act.wait_ge(S["xna"], c + 1)
                for m in range(KD):
                    part = nT[:, m, chunk(c)]
                    last = f(part, part, ACT.Identity, bias=vcol("b_attn", m), scale=vcol("g_attn", m))
                last.then_inc(S["xn"], CI)

            def probabilities(n, g):
                act.wait_ge(S["sh"], 2 * n + g + 1)
                if not isinstance(n, int) or n >= 1:
                    act.wait_ge(S["T"], 2 * n + g - 1)
                f(ex[g][0:SEQ, :, :], sh[g][0:SEQ, :, :], ACT.Exp, scale=float(HD) ** -0.5).then_inc(S["ex"], 1)

            def keys_out(n, pos, p):
                act.wait_ge(S["qkev"], 2 * p + 2)
                if not isinstance(n, int) or n >= 2:
                    act.wait_ge(S["scores"], 2 * n - 2)
                half = pos % 2 * SEQ
                for h in range(HG):
                    last = f(kx[pos % 2][:, 0, h, :], qk[:, pos // 2, KD, half:half + SEQ], ACT.Copy,
                             scale=head_of[:, h:h + 1])
                last.then_inc(S["kx0"], 1)

            def copy_transposed(n, g):
                act.wait_ge(S["T"], 2 * n + g + 1)
                if g == 0 and (not isinstance(n, int) or n >= 1):
                    act.wait_ge(S["aT"], n)
                if not isinstance(n, int) or n >= 1:
                    act.wait_ge(S["PV"], 2 * n + g - 1)
                f(pT[g][0:SEQ, :, :], PS[0:SEQ, 4:6, 0:HB * SEQ], ACT.Copy).then_inc(S["pT"], 1)

            def copy_output(n):
                act.wait_ge(S["aT"], n + 1)
                f(nT[:, :, bass.ds(n * SEQ, SEQ)],
                  PS[:, 5, HB * SEQ:(HB + KD) * SEQ].rearrange("p (k s) -> p k s", k=KD), ACT.Copy
                  ).then_inc(S["attn"], 1)

            keys_out(0, 0, 0)
            second_rstd(2)
            norm_rstd(n0, 3)
            keys_out(1, 1, 0)
            probabilities(0, 0)
            second_rstd(3)

            def project_out(c):
                act.wait_ge(S["o"], c + 1)
                for m in range(KD):
                    last = f(nT[:, m, chunk(c)], PS[:, PROJECTED[c] + m, 0:CT], ACT.Identity, bias=vcol("out_b", m))
                last.then_inc(S["ctx"], 1)

            def step(i, pos, p):
                copy_transposed(i, 0)
                if not isinstance(i, int) or i > 0:
                    copy_output(i - 1)
                probabilities(i, 1)
                if isinstance(i, int) and i == IMG - 1:
                    project_out(0)
                copy_transposed(i, 1)
                if isinstance(i, int) and i == 0:
                    affine(2)
                    affine(3)
                if not isinstance(i, int) or i + 1 < IMG:
                    probabilities(i + 1, 0)
                if not isinstance(i, int) or i + 2 < IMG:
                    keys_out(i + 2, (pos + 2) % CI, p if pos % 2 else p + 1)

            attention_steps(act, step)
            project_out(1)
            copy_output(IMG - 1)

            norm_square(n1, 0)
            project_out(2)
            norm_square(n1, 1)
            project_out(3)
            norm_rstd(n1, 0)
            norm_rstd(n1, 1)
            for c in range(2, NCH):
                norm_square(n1, c)
                norm_rstd(n1, c)

            def tanh(n, c, first):
                act.wait_ge(S["z"], n + NCH)
                if first and c < 2:
                    act.wait_ge(n1.done, NCH)
                else:
                    act.wait_ge(S["e"], n - 2)
                for m in range(KD):
                    last = f(u[:, c % 2, m, :], PS[:, 2 * c + m, 0:CT], ACT.Tanh, bias=vcol("b_inl", m))
                last.then_inc(S["u"], 1)

            def decay(n, c, first):
                act.wait_ge(S["e"], n)
                if not (first and c < 2):
                    act.wait_ge(S["r"], n - 2)
                f(pe[:, c % 2, :, :], eT[:, :, chunk(c)], ACT.Copy, scale=1.0 - DT).then_inc(S["p9"], 1)

            def iteration(n, first):
                for c in range(NCH):
                    tanh(n + (c + 1), c, first)
                    if c >= 1:
                        decay(n + c, c - 1, first)
                decay(n + NCH, NCH - 1, first)

            iteration(0, True)
            with act.Fori(1, ITERS - 1) as t:
                iteration(t * NCH, False)
            for c in range(NCH):
                tanh((ITERS - 1) * NCH + c + 1, c, False)

            act.preload_act_table_set("natural_log_exp_and_others")
            norm_square(n2, 0)
            norm_square(n2, 1)
            norm_rstd(n2, 0)
            norm_rstd(n2, 1)
            norm_square(n2, 2)
            norm_rstd(n2, 2)
            norm_square(n2, 3)

            def gelu(c, m):
                i = c * KF + m
                act.wait_ge(S["f1"], i + 1)
                if c >= 2 and m == 0:
                    act.wait_ge(S["f2"], KD * (c - 1))
                f(fh[c % 2][:, m, :], PS[:, 4 + i % 2, 0:CT], ACT.Gelu, bias=vcol("ff_b1", m)).then_inc(S["fh"], 1)

            def ff_bias(c, ms=range(KD)):
                for m in ms:
                    act.wait_ge(S["f2"], KD * c + m + 1)
                    if c >= 1 and m == 0:
                        act.wait_ge(S["x3"], c)
                    f(ffb_buf[:, m, :], PS[:, 6 + m, 0:CT], ACT.Identity, bias=vcol("ff_b2", m)
                      ).then_inc(S["ffb"], 1)

            for c in range(2):
                for m in range(KF):
                    gelu(c, m)
            ff_bias(0)
            for c in range(2, NCH):
                for m in range(KF):
                    gelu(c, m)
                    if m == KF - 2:
                        norm_square(n3, c - 2)
                act.preload_act_table_set("natural_log_exp_and_others")
                if c == 2:
                    norm_rstd(n2, 3)
                norm_rstd(n3, c - 2)
                if c < NCH - 1:
                    ff_bias(c - 1)

            def row_out(t):
                act.wait_ge(S["rowT"], t + 1)
                f(rows[t], PS[:, 3 + t % 2 * 2, 0:D], ACT.Copy).then_inc(S["rowev"], 1)

            def exponentials(batch):
                act.wait_ge(S["shifted"], batch + 1)
                part = pr[:, ROUTED[batch][0]:ROUTED[batch][1], :]
                f(part, part, ACT.Exp).then_inc(S["exp"], 1)

            def gates_out(batch):
                act.wait_ge(S["gTt"], batch + 1)
                act.wait_ge(S["f2"], KD * NCH)
                a, b = ROUTED[batch][0] * P, min(ROUTED[batch][1] * P, TOK)
                f(gT[0:E, a:b], PS[0:E, 4, 0:b - a], ACT.Copy).then_inc(S["gTev"], 1)

            def residual_row_out(t):
                n = P if t < NT - 1 else LAST
                act.wait_ge(S["hrow"], t + 1)
                if t >= 2:
                    act.wait_ge(S[f"acc_set{t % 2}"], 16 * (t // 2))
                else:
                    act.wait_ge(n3.done, 3)
                f(hrow[0:n, t % 2, :], PS[0:n, 6 + t % 2, 0:D], ACT.Copy).then_inc(S["hrowev"], 1)
                act.wait_ge(S["hrowev"], t + 1)
                act.dma_start(out[t * P:t * P + n, :], hrow[0:n, t % 2, :]).then_inc(S[f"acc_set{t % 2}"], 16)

            exponentials(0)
            ff_bias(2)
            for t in range(*ROUTED[0]):
                row_out(t)
            ff_bias(3, (0,))
            norm_square(n3, 2)
            ff_bias(3, (1,))
            norm_rstd(n3, 2)
            gates_out(0)
            norm_square(n3, 3)
            exponentials(1)
            residual_row_out(0)
            norm_rstd(n3, 3)
            for t in range(*ROUTED[1]):
                row_out(t)
            for t in range(1, ROUTED[0][1]):
                residual_row_out(t)
            exponentials(2)
            for t in range(*ROUTED[2]):
                row_out(t)
            for batch in (1, 2):
                gates_out(batch)
                for t in range(*ROUTED[batch]):
                    residual_row_out(t)

            def expert_of(i):
                return act.value_load(tile_expert[0:1, bass.ds(i, 1)], min_val=0, max_val=E - 1)

            def relu(i, ring):
                e = expert_of(i)
                f(b1t[:, ring % 2, :], vecs[:, bass.ds(e * KE + vec_at["moe_b1"], KE)], ACT.Copy
                  ).then_inc(S["b1t"], 1)
                act.wait_ge(S["b1t"], i + 1)
                act.wait_ge(S["l1"], i + 1)
                if not isinstance(i, int) or i > 0:
                    act.wait_ge(S["l2"], i)
                for m in range(KE):
                    last = f(hid[:, m, :], PS[:, 2 * (ring % 2) + m // 4, (m % 4) * P:(m % 4 + 1) * P], ACT.Relu,
                             bias=b1t[:, ring % 2, m:m + 1])
                last.then_inc(S["hrelu"], 1)

            act.wait_ge(S["tile_expert"], 1)
            def expert_step(i, ring, lap):
                relu(i, ring)

            expert_steps(act, expert_step)

        @block.vector
        def _(dve):
            tt, ts = dve.tensor_tensor, dve.tensor_scalar

            dve.memset(mean_m[:, :], 1.0 / D)
            dve.memset(ones[:, :], 1.0)
            dve.memset(eps[:, :], EPS).then_inc(S["c_dve"], 1)
            dve.wait_ge(S["l_vec"], 16)
            for m in range(KD):
                to = hT[:, m, :].rearrange("p (i t) -> p i t", i=IMG)[:, :, 0]
                last = dve.tensor_copy(to, vcol("cls", m).broadcast_to([P, IMG]))
            last.then_inc(S["cls"], 1)

            def norm_center(n, c):
                dve.wait_ge(n.mean, c + 1)
                tt(xc[:, c % 2, :, :], n.source[:, :, chunk(c)],
                   over_k(PS[:, n.mean_banks[c % len(n.mean_banks)], 0:CT], CT), ALU.subtract
                   ).then_inc(n.centered, 1)

            def norm_out(n, c, dst, affine=None):
                dve.wait_ge(n.rstd, c + 1)
                ins = tt(dst[:, :, chunk(c)], xc[:, c % 2, :, :], over_k(rs[:, c % 2, :], CT), ALU.mult)
                if affine is None:
                    ins.then_inc(n.done, 1)
                    return
                ins.then_inc(n.scaled, 1)
                dve.wait_ge(n.scaled, c + 1)
                for m in range(KD):
                    ins = ts(dst[:, m, chunk(c)], dst[:, m, chunk(c)], vcol(affine[0], m), vcol(affine[1], m),
                             ALU.mult, ALU.add)
                ins.then_inc(n.done, 1)

            def second_var(c):
                var, r, v2 = PS[:, n0.var_banks[c], 0:CT], rs[:, c % 2, :], rs2[:, c % 2, :]
                dve.wait_ge(n0.rstd, c + 1)
                tt(v2, r, r, ALU.mult).then_inc(S["v2a"], 1)
                dve.wait_ge(S["v2a"], c + 1)
                tt(v2, v2, var, ALU.mult).then_inc(S["v2"], 1)

            def first_out(c):
                tt(x0T[:, :, chunk(c)], xc[:, c % 2, :, :], over_k(rs[:, c % 2, :], CT), ALU.mult
                   ).then_inc(n0.done, 1)

            def second_out(c):
                dve.wait_ge(n0.done, c + 1)
                dve.wait_ge(S["rstd2"], c + 1)
                tt(nT[:, :, chunk(c)], x0T[:, :, chunk(c)], over_k(rs2[:, c % 2, :], CT), ALU.mult
                   ).then_inc(S["xna"], 1)

            norm_center(n0, 0)
            dve.wait_ge(S["c_int"], 1)
            dve.tensor_copy(fw[:, :], iw[:, :]).then_inc(S["c_dve"], 1)
            for k in range(2):
                last = dve.tensor_copy(pairs[:, k, :, 1].bitcast(I32), iw[:, NT:2 * NT])
            last.then_inc(S["numbers"], 1)
            dve.wait_ge(S["c_dve"], 2)
            ts(valid[:, :], token_no, float(TOK), None, ALU.is_lt).then_inc(S["c_dve"], 1)
            norm_center(n0, 1)
            second_var(0)
            first_out(0)
            second_out(0)
            norm_center(n0, 2)

            def half_out(n, pos):
                dve.wait_ge(S["qk"], n + 1)
                if not isinstance(n, int) or n >= 4:
                    dve.wait_ge(S["scores"], 2 * n - 4 - pos % 2 * 2)
                m = pos % 2 * KD
                tt(qk[:, pos // 2, m:m + KD, :], PS[:, 6, 0:KD * 2 * SEQ].rearrange("p (m s) -> p m s", m=KD),
                   vcol("qk_b", m, KD).unsqueeze(2).broadcast_to([P, KD, 2 * SEQ]), ALU.add
                   ).then_inc(S["qkev"], 1)

            def values_out(n, par):
                dve.wait_ge(S["v"], n + 1)
                tt(va[par][0:SEQ, :, 0:HD], PS[0:SEQ, 7, 0:D].rearrange("p (h d) -> p h d", h=H),
                   vb_rows[0:SEQ, :].rearrange("p (h d) -> p h d", h=H), ALU.add).then_inc(S["vev"], 1)

            def masked_max(n, g):
                dve.wait_ge(S["scores"], 2 * n + g + 1)
                if not isinstance(n, int) or n >= 1:
                    dve.wait_ge(S["ex"], 2 * n + g - 1)
                to = sh[g][0:SEQ, :, :]
                tt(to.rearrange("p (b h) s -> p b h s", b=2),
                   PS[0:SEQ, 2 * g:2 * g + 2, 0:HB * SEQ].rearrange("p b (h s) -> p b h s", h=HB),
                   mask[0:SEQ, :].unsqueeze(1).unsqueeze(1).broadcast_to([SEQ, 2, HB, SEQ]), ALU.add
                   ).then_inc(S["masked"], 1)
                dve.wait_ge(S["masked"], 2 * n + g + 1)
                dve.tensor_reduce(mx[0:SEQ, g, :], to, AX_X, ALU.max).then_inc(S["mx"], 1)

            def less_max(n, g):
                dve.wait_ge(S["mx"], 2 * n + g + 1)
                to = sh[g][0:SEQ, :, :]
                tt(to, to, mx[0:SEQ, g, :].unsqueeze(2).broadcast_to([SEQ, HG, SEQ]), ALU.subtract
                   ).then_inc(S["sh"], 1)

            def normalize(n):
                dve.wait_ge(S["PV"], 2 * n + 2)
                o = PS[0:SEQ, 7, 0:H * (HD + 1)].rearrange("p (h d) -> p h d", h=H)
                dve.reciprocal(rc[0:SEQ, :], o[:, :, HD]).then_inc(S["rc"], 1)
                dve.wait_ge(S["rc"], n + 1)
                if not isinstance(n, int) or n >= 1:
                    dve.wait_ge(S["aT"], n)
                tt(att[0:SEQ, :, :], o[:, :, 0:HD], rc[0:SEQ, :].unsqueeze(2).broadcast_to([SEQ, H, HD]), ALU.mult
                   ).then_inc(S["att"], 1)

            for i in range(2):
                dve.memset(va[i][0:SEQ, :, HD:HD + 1], 1.0)
            dve.wait_ge(S["l_rows"], 16 * 4)
            half_out(0, 0)
            second_var(1)
            first_out(1)
            dve.wait_ge(n0.done, 2)
            norm_center(n0, 3)
            second_out(1)
            half_out(1, 1)
            values_out(0, 0)
            second_var(2)
            first_out(2)
            half_out(2, 2)
            masked_max(0, 0)
            less_max(0, 0)
            second_var(3)
            masked_max(0, 1)
            values_out(1, 1)

            def step(i, pos, p):
                after = (pos + 1) % CI
                if not isinstance(i, int) or i > 0:
                    normalize(i - 1)
                less_max(i, 1)
                if isinstance(i, int) and i == 0:
                    first_out(3)
                    second_out(2)
                    second_out(3)
                if not isinstance(i, int) or i + 3 < IMG:
                    half_out(i + 3, (pos + 3) % CI)
                if not isinstance(i, int) or i + 1 < IMG:
                    if not isinstance(i, int) or i > 0:
                        values_out(i + 1, after % 2)
                    masked_max(i + 1, 0)
                    less_max(i + 1, 0)
                    masked_max(i + 1, 1)

            attention_steps(dve, step)

            def add_attention(c):
                dve.wait_ge(S["ctx"], c + 1)
                tt(x0T[:, :, chunk(c)], x0T[:, :, chunk(c)], nT[:, :, chunk(c)], ALU.add).then_inc(S["x1"], 1)

            dve.wait_ge(S["l_mid"], 16 * 3)
            ts(wxd[:, :, :], wx[:, :, :], DT * DT, None, ALU.mult).then_inc(S["wxd"], 1)
            add_attention(0)
            normalize(IMG - 1)
            add_attention(1)
            norm_center(n1, 0)
            add_attention(2)
            norm_center(n1, 1)
            dve.wait_ge(S["aT"], IMG)
            norm_out(n1, 0, xsT, ("g1", "b1"))
            add_attention(3)
            norm_center(n1, 2)
            norm_out(n1, 1, xsT, ("g1", "b1"))
            norm_center(n1, 3)
            norm_out(n1, 2, xsT, ("g1", "b1"))
            norm_out(n1, 3, xsT, ("g1", "b1"))

            def advance(n, c, first):
                dve.wait_ge(S["u"], n)
                if first:
                    tt(eT[:, :, chunk(c)], u[:, c % 2, :, :], xsT[:, :, chunk(c)], ALU.subtract).then_inc(S["e"], 1)
                else:
                    dve.wait_ge(S["r"], n - NCH)
                    tt(eT[:, :, chunk(c)], u[:, c % 2, :, :], rT[:, :, chunk(c)], ALU.add).then_inc(S["e"], 1)
                dve.wait_ge(S["e"], n)
                dve.scalar_tensor_tensor(out=xsT[:, :, chunk(c)], in0=eT[:, :, chunk(c)], scalar=DT * DT,
                                         in1=xsT[:, :, chunk(c)], op0=ALU.mult, op1=ALU.add).then_inc(S["xs"], 1)

            for c in range(NCH):
                advance(c + 1, c, True)
            with dve.Fori(1, ITERS - 1) as t:
                for c in range(NCH):
                    advance(t * NCH + (c + 1), c, False)

            def last_advance(c):
                n = (ITERS - 1) * NCH + c + 1
                advance(n, c, False)
                dve.wait_ge(S["xs"], n)
                tt(x0T[:, :, chunk(c)], x0T[:, :, chunk(c)], xsT[:, :, chunk(c)], ALU.add).then_inc(S["x2"], 1)

            for c in range(3):
                last_advance(c)
            norm_center(n2, 0)
            last_advance(3)
            norm_center(n2, 1)
            norm_out(n2, 0, xsT, ("g2", "b2"))
            norm_center(n2, 2)
            norm_out(n2, 1, xsT, ("g2", "b2"))
            norm_center(n2, 3)
            norm_out(n2, 2, xsT, ("g2", "b2"))

            def residual(c):
                dve.wait_ge(S["ffb"], KD * (c + 1))
                tt(x0T[:, :, chunk(c)], x0T[:, :, chunk(c)], ffb_buf[:, :, :], ALU.add).then_inc(S["x3"], 1)
                dve.wait_ge(S["x3"], c + 1)
                tt(hT[:, :, chunk(c)], hT[:, :, chunk(c)], x0T[:, :, chunk(c)], ALU.add).then_inc(S["hp"], 1)

            dve.wait_ge(S["z"], NCH)
            dve.memset(nT[:, :, TOK:TP], 0.0)
            residual(0)
            norm_center(n3, 0)
            norm_out(n2, 3, xsT, ("g2", "b2"))
            norm_out(n3, 0, nT)
            residual(1)
            norm_center(n3, 1)
            norm_out(n3, 1, nT)

            done = [0]
            reduce = dve.tensor_reduce

            def link(ins):
                done[0] += 1
                ins.then_inc(S["route"], 1)
                dve.wait_ge(S["route"], done[0])

            def choose(batch):
                first, behind = ROUTED[batch]
                n = behind - first
                b = slice(first, behind)
                p, s_ = pr[:, b, :], scr[:, b, :]

                def over_e(ap):
                    return ap.unsqueeze(2).broadcast_to([P, n, E])

                dve.wait_ge(S["logit"], behind)
                link(tt(p, PS[:, ROUTED_IN[batch], first * E:behind * E].rearrange("p (t e) -> p t e", t=n),
                        gb_rows[:, :].unsqueeze(1).broadcast_to([P, n, E]), ALU.add))
                link(reduce(s9[:, 0, b], p, AX_X, ALU.max))
                tt(p, p, over_e(s9[:, 0, b]), ALU.subtract).then_inc(S["shifted"], 1)
                dve.wait_ge(S["exp"], batch + 1)
                link(reduce(s9[:, 1, b], p, AX_X, ALU.add))
                link(dve.reciprocal(s9[:, 2, b], s9[:, 1, b]))
                link(tt(p, p, over_e(s9[:, 2, b]), ALU.mult))
                for k in range(2):
                    top = s9[:, 3 + k, b]
                    link(reduce(top, p, AX_X, ALU.max))
                    link(tt(s_, p, over_e(top), ALU.is_equal))
                    link(tt(s_, s_, rank.unsqueeze(1).broadcast_to([P, n, E]), ALU.mult))
                    link(reduce(s9[:, 5, b], s_, AX_X, ALU.max))
                    link(tt(oh[k][:, b, :], s_, over_e(s9[:, 5, b]), ALU.is_equal))
                    if k == 0:
                        link(dve.scalar_tensor_tensor(out=p, in0=oh[0][:, b, :], scalar=-2.0, in1=p, op0=ALU.mult,
                                                      op1=ALU.add))
                link(tt(s_, oh[0][:, b, :], oh[1][:, b, :], ALU.add))
                tt(member[:, b, :], s_, over_e(valid[:, b]), ALU.mult).then_inc(S["member"], 1)
                for k in range(2):
                    last = dve.tensor_copy(pairs[:, k, b, 0], s9[:, 3 + k, b])
                last.then_inc(S["pairs"], 1)

            def place(batch):
                first, behind = ROUTED[batch]
                n = behind - first
                b = slice(first, behind)
                s_, s2 = scr[:, b, :], scr2[:, b, :]
                bank = ROUTED_IN[batch]
                dve.wait_ge(S["member"], batch + 1)
                dve.wait_ge(S["cum"], batch + 1)
                if batch == 0:
                    link(dve.tensor_copy(pre[:, 0, :], region))
                for t in range(first, behind):
                    link(tt(pre[:, t + 1, :], PS[:, bank, (2 * NT + t) * E:(2 * NT + t + 1) * E], pre[:, t, :], ALU.add))
                link(tt(s_, PS[:, bank, (NT + first) * E:(NT + behind) * E].rearrange("p (t e) -> p t e", t=n),
                        pre[:, b, :], ALU.add))
                for k in range(2):
                    link(tt(s2, s_, oh[k][:, b, :], ALU.mult))
                    link(reduce(slot_f[:, k, b], s2, AX_X, ALU.add))
                dve.tensor_copy(slot_i[:, :, b], slot_f[:, :, b]).then_inc(S["slot_no"], 1)

            def gates_by_expert(batch):
                b = slice(*ROUTED[batch])
                n = ROUTED[batch][1] - ROUTED[batch][0]
                link(tt(scr[:, b, :], oh[0][:, b, :], s9[:, 3, b].unsqueeze(2).broadcast_to([P, n, E]), ALU.mult))
                link(tt(scr2[:, b, :], oh[1][:, b, :], s9[:, 4, b].unsqueeze(2).broadcast_to([P, n, E]), ALU.mult))
                tt(gates[:, b, :], scr[:, b, :], scr2[:, b, :], ALU.add).then_inc(S["gates"], 1)

            choose(0)
            residual(2)
            norm_center(n3, 2)
            place(0)
            gates_by_expert(0)
            residual(3)
            norm_out(n3, 2, nT)
            norm_center(n3, 3)
            choose(1)
            norm_out(n3, 3, nT)
            place(1)
            choose(2)
            gates_by_expert(1)
            place(2)
            gates_by_expert(2)

            link(tt(scr[:, 0, :], pre[:, NT, :], region, ALU.subtract))
            link(tt(tiles_k[:, :, :], scr[:, 0, :].unsqueeze(2).broadcast_to([P, E, NT]),
                    multiples.unsqueeze(1).broadcast_to([P, E, NT]), ALU.is_gt))
            link(reduce(tiles_e[:, :], tiles_k[:, :, :], AX_X, ALU.add))
            link(tt(start_k[:, :, :], before[:, :, :], tiles_e[:, :].unsqueeze(1).broadcast_to([P, E, E]), ALU.mult))
            link(reduce(start_e[:, :], start_k[:, :, :], AX_X, ALU.add))
            link(tt(te_k[:, :, :], start_e[:, 1:E].unsqueeze(1).broadcast_to([P, SLOT_TILES, E - 1]),
                    tile_no.unsqueeze(2).broadcast_to([P, SLOT_TILES, E - 1]), ALU.is_le))
            link(reduce(te[:, :], te_k[:, :, :], AX_X, ALU.add))
            link(ts(past_e[:, :], tiles_e[:, 0:E - 1], -float(P), float(CAP), ALU.mult, ALU.add))
            link(tt(te_k[:, :, :], te_k[:, :, :], past_e[:, :].unsqueeze(1).broadcast_to([P, SLOT_TILES, E - 1]),
                    ALU.mult))
            link(reduce(tb[:, :], te_k[:, :, :], AX_X, ALU.add))
            link(dve.scalar_tensor_tensor(out=tb[:, :], in0=tile_no, scalar=float(P), in1=tb[:, :], op0=ALU.mult,
                                          op1=ALU.add))
            dve.tensor_copy(tile_base[:, :], tb[:, :])
            dve.tensor_copy(tile_expert[:, :], te[:, :]).then_inc(S["tile_expert"], 1)

            def input_out(i, ring):
                dve.wait_ge(S["xt"], i + 1)
                if not isinstance(i, int) or i >= 2:
                    dve.wait_ge(S["l1"], i - 1)
                dve.tensor_copy(xt[:, ring % 2, :, :], PS[:, 5, 0:D].rearrange("p (k t) -> p k t", k=KD)
                                ).then_inc(S["xtev"], 1)

            def weights_in(i, ring):
                w = dve.value_load(tile_expert[0:1, bass.ds(i, 1)], min_val=0, max_val=E - 1) * WE
                if not isinstance(i, int) or i >= 2:
                    dve.wait_ge(S["l1"], i - 1)
                dve.tensor_copy(w1[ring % 2], W[:, bass.ds(w, KD * EH)].rearrange("p (k n) -> p k n", k=KD)
                                ).then_inc(S["w1"], 1)

            def gated(i, ring):
                gate = info[:, i, 0:1] if isinstance(i, int) else info[:, bass.ds(i, 1), 0].rearrange("p o -> p o")
                dve.wait_ge(S["l2"], i + 1)
                if not isinstance(i, int) or i >= 2:
                    dve.wait_ge(S["acc_add"], 16 * (i - 1))
                ts(yt[:, ring % 2, :], PS[:, 4, 0:D], gate, None, ALU.mult).then_inc(S["yev"], 1)

            dve.wait_ge(S["tile_expert"], 1)
            dve.wait_ge(S["l_moe"], 16 * (E - 2))
            dve.wait_ge(S["l_moe_late"], 16 * 2)
            weights_in(0, 0)
            dve.wait_ge(S["hrow"], NT)
            weights_in(1, 1)
            input_out(0, 0)
            input_out(1, 1)

            def expert_step(i, ring, lap):
                if not isinstance(i, int) or i + 2 < SLOT_TILES:
                    input_out(i + 2, (ring + 2) % XR)
                if isinstance(i, int) and i == 0:
                    weights_in(2, 2)
                if not isinstance(i, int) or i + 3 < SLOT_TILES:
                    weights_in(i + 3, (ring + 3) % XR)
                gated(i, ring)

            expert_steps(dve, expert_step)


def by_partition(w):
    return w.reshape(w.shape[0] // P, P, -1).transpose(1, 0, 2)


def columns(b):
    return b.reshape(-1, P).T


def layout(np, a):
    x = a["x"].reshape(IMG, 3, 8, 16, 8, 16).transpose(0, 2, 4, 3, 5, 1).reshape(NCH, CP, KPATCH, P)
    w1 = a["L0_ffn_w1"].reshape(E, KD, P, EH).transpose(0, 2, 1, 3).reshape(E, P, KD * EH)
    w2 = a["L0_ffn_w2"].reshape(E, KE, P, D).transpose(0, 2, 1, 3).reshape(E, P, KE * D)
    qkv_b = a["L0_attn_qkv_b"]
    by_name = {
        "tok_b": a["L0_tok_b"], "cls": a["cls_tok"].reshape(D), "g_attn": a["L0_attn_g_attn"],
        "b_attn": a["L0_attn_b_attn"], "g1": a["L0_attn_g1"], "b1": a["L0_attn_b1"], "g2": a["L0_attn_g2"],
        "b2": a["L0_attn_b2"], "b_inl": a["L0_attn_b_inl"], "qk_b": qkv_b[0:2 * D], "out_b": a["L0_attn_out_b"],
        "ff_b1": a["L0_attn_ff_b1"], "ff_b2": a["L0_attn_ff_b2"], "moe_b1": a["L0_ffn_b1"].reshape(E * EH),
    }
    return {
        "patches": x.transpose(0, 3, 2, 1), "tok_w": by_partition(a["L0_tok_W"].T),
        "qkv_w": by_partition(a["L0_attn_qkv_w"]), "out_w": by_partition(a["L0_attn_out_w"]),
        "ctx_w": by_partition(a["L0_attn_w_ctx"]), "x_w": by_partition(a["L0_attn_w_x"]),
        "ff1_w": by_partition(a["L0_attn_ff_w1"]), "ff2_w": by_partition(a["L0_attn_ff_w2"]),
        "moe_w": np.concatenate([w1, w2], axis=2), "gate_w": by_partition(a["L0_ffn_gate_w"].T),
        "vec": np.concatenate([columns(by_name[n]) for n, _ in VEC], axis=1),
        "v_b": qkv_b[2 * D:3 * D].reshape(1, D), "gate_b": a["L0_ffn_gate_b"].reshape(1, E),
        "moe_b2": a["L0_ffn_b2"],
    }


def kernel(**inputs):
    import numpy as np
    import concourse.bacc as bacc
    from concourse.bass_utils import run_bass_kernel_spmd

    nc = bacc.Bacc("TRN2", target_bir_lowering=False, num_devices=1)
    arrays, args = {}, {}
    for name, a in layout(np, {n: np.asarray(v) for n, v in inputs.items()}).items():
        a = np.ascontiguousarray(a)
        arrays[name] = a
        args[name] = nc.dram_tensor(name, a.shape, F32, kind="ExternalInput").ap()
    out = nc.dram_tensor("out", (TOK + P, D), F32, kind="ExternalOutput").ap()
    vit_block(nc, out=out, **args)
    result = run_bass_kernel_spmd(nc, [arrays], core_ids=[0])
    return result.results[0]["out"][:TOK].reshape(IMG, SEQ, D)
```

```python
from contextlib import ExitStack

import concourse.bass as bass
from concourse import mybir

F32 = mybir.dt.float32
I32 = mybir.dt.int32
ALU = mybir.AluOpType
ACT = mybir.ActivationFunctionType
AX_X = mybir.AxisListType.X

P = 128
IMG = 16
PATCHES = 64
SEQ = PATCHES + 1
TOK = IMG * SEQ
D = 256
KD = D // P
KPATCH = 768 // P
NCH = 4
CI = IMG // NCH
CT = CI * SEQ
CP = CI * PATCHES
H = 16
HD = D // H
HG = H // KD
HB = 4
FF = 1024
KF = FF // P
ITERS = 8
DT = 0.1
EPS = 1e-5
E = 8
EH = 1024
KE = EH // P
WE = KD * EH + KE * D
NT = -(-TOK // P)
LAST = TOK - (NT - 1) * P
TP = NT * P
SLOT_TILES = (2 * TOK + E * (P - 1)) // P
CAP = NT * P
ALL_TILES = (E - 1) * NT + SLOT_TILES - (TOK // P)
ROUTED = ((0, 2 * CT // P), (2 * CT // P, 3 * CT // P), (3 * CT // P, NT))
ROUTED_IN = (2, 2, 0)
XR = 4
PROJECTED = (0, 2, 0, 4)
NEG = -3.0e38

VEC = (("tok_b", KD), ("cls", KD), ("g_attn", KD), ("b_attn", KD), ("g1", KD), ("b1", KD), ("g2", KD), ("b2", KD),
       ("b_inl", KD), ("qk_b", 2 * KD), ("out_b", KD), ("ff_b1", KF), ("ff_b2", KD), ("moe_b1", E * KE))
NVEC = sum(n for _, n in VEC)


class Norm:

    def __init__(self, sem, name, source, ready, per_chunk, mean_banks, var_banks):
        self.source = source
        self.ready = ready
        self.per_chunk = per_chunk
        self.mean_banks = mean_banks
        self.var_banks = var_banks
        self.mean = sem(f"{name}_mean")
        self.centered = sem(f"{name}_centered")
        self.squared = sem(f"{name}_squared")
        self.var = sem(f"{name}_var")
        self.logged = sem(f"{name}_logged")
        self.rstd = sem(f"{name}_rstd")
        self.var_used = self.rstd
        self.scaled = sem(f"{name}_scaled")
        self.done = sem(f"{name}_done")


def vit_block(nc, patches, tok_w, qkv_w, out_w, ctx_w, x_w, ff1_w, ff2_w, moe_w, gate_w, vec, v_b, gate_b, moe_b2,
              out):
    slots = nc.dram_tensor("slots", (ALL_TILES * P, 2), F32, kind="Internal").ap()
    tokens = nc.dram_tensor("tokens", (TOK + P, D), F32, kind="Internal").ap()

    with ExitStack() as ctx:
        def sb(name, shape, dt=F32):
            return ctx.enter_context(nc.sbuf_tensor(name, shape, dt))

        def sem(name):
            return ctx.enter_context(nc.semaphore(name))

        def carve(flat, at, *dims):
            n = 1
            for d in dims:
                n *= d
            names = "abcd"[:len(dims)]
            view = flat[:, at:at + n].rearrange(f"p ({' '.join(names)}) -> p {' '.join(names)}",
                                                **dict(zip(names, dims)))
            return view, at + n

        W = sb("W", [P, E * WE])
        at = (E - 1) * WE
        wtok, at = carve(W, at, KPATCH, D)
        wqkv, at = carve(W, at, KD, 3 * D)
        wout, at = carve(W, at, KD, D)
        wctx, at = carve(W, at, KD, D)
        at = (E - 2) * WE
        wff1, at = carve(W, at, KD, FF)
        wff2, at = carve(W, at, KF, D)
        qk, at = carve(W, (E - 3) * WE, 2, 2 * KD, 2 * SEQ)
        rs2, at = carve(W, at, 2, CT)
        wx = sb("wx", [P, KD, D])
        wxd = sb("wxd", [P, KD, D])
        gate_t = sb("gate_t", [P, KD, E])
        vecs = sb("vecs", [P, NVEC])
        vec_at, at = {}, 0
        for name, n in VEC:
            vec_at[name] = at
            at += n

        def vcol(name, m=0, n=1):
            return vecs[:, vec_at[name] + m:vec_at[name] + m + n]

        vb_rows = sb("vb_rows", [P, D])
        gb_rows = sb("gb_rows", [P, E])
        b2_rows = sb("b2_rows", [E, D])

        streams = sb("streams", [P, KD * TOK + KD * TP])
        hT, at = carve(streams, 0, KD, TOK)
        nT, at = carve(streams, at, KD, TP)
        arena = sb("arena", [P, 4 * KD * TOK])
        x0T, _ = carve(arena, 0, KD, TOK)
        xsT, _ = carve(arena, KD * TOK, KD, TOK)
        eT, _ = carve(arena, 2 * KD * TOK, KD, TOK)
        rT, _ = carve(arena, 3 * KD * TOK, KD, TOK)
        xc = sb("xc", [P, 2, KD, CT])
        sq = sb("sq", [P, 2, KD, CT])
        rs = sb("rs", [P, 2, CT])
        pe, u = xc, sq

        pt = [carve(arena, (2 + i) * KD * TOK, KPATCH, CP)[0] for i in range(2)]
        kx = [carve(arena, (2 * KD + i) * TOK, KD, HG, SEQ)[0] for i in range(2)]
        ex, pT = [], []
        at = 3 * KD * TOK
        for i in range(2):
            view, at = carve(arena, at, HG, SEQ)
            ex.append(view)
        for i in range(2):
            view, at = carve(arena, at, 2, HB * SEQ)
            pT.append(view)
        fh = [carve(arena, (2 + i) * KD * TOK, KF, CT)[0] for i in range(2)]
        at = KD * TOK
        sh, va = [], []
        for i in range(2):
            view, at = carve(arena, at, HG, SEQ)
            sh.append(view)
        for i in range(2):
            view, at = carve(arena, at, H, HD + 1)
            va.append(view)
        att, at = carve(arena, at, H, HD)
        assert at <= 2 * KD * TOK
        xi = sb("xi", [P, 2, KD, 2 * SEQ])
        ffb_buf = xi[:, :, :, :].rearrange("p a b s -> p (a b s)").rearrange("p (k t) -> p k t", k=KD)
        mx = sb("mx", [P, 2, HG])
        rc = sb("rc", [P, H])

        rows = [carve(arena, KD * TOK + t * D, D)[0] for t in range(NT - 1)]
        rows.append(sq[:, 0, 0, 0:D])
        at = 2 * KD * TOK
        xin, at = carve(arena, at, XR, D)
        xt, at = carve(arena, at, 2, KD, P)
        hid, at = carve(arena, at, KE, P)
        gT, at = carve(arena, at, TOK)
        assert at <= 4 * KD * TOK
        w1 = [carve(arena, 0, KD, EH)[0], carve(streams, 0, KD, EH)[0]]
        y_flat = xc[:, :, :, :].rearrange("p a b c -> p (a b c)")
        hrow, at = carve(y_flat, 0, 2, D)
        yt, at = carve(y_flat, at, 2, D)

        ident = sb("ident", [P, P])
        mask = sb("mask", [P, SEQ])
        mean_m = sb("mean_m", [P, P])
        ones = sb("ones", [P, P])
        below = sb("below", [P, P])
        head_of = sb("head_of", [P, HG])
        eps = sb("eps", [P, 1])
        before = sb("before", [P, E, E])
        iw = sb("iw", [P, 2 * NT + SLOT_TILES + 2 * E], I32)
        fw = sb("fw", [P, 2 * NT + SLOT_TILES + 2 * E])
        multiples, at = carve(fw, 0, NT)
        token_no, at = carve(fw, at, NT)
        tile_no, at = carve(fw, at, SLOT_TILES)
        rank, at = carve(fw, at, E)
        region, at = carve(fw, at, E)
        valid = sb("valid", [P, NT])
        zero = sb("zero", [P, D])
        empty = sb("empty", [ALL_TILES, P, 2])
        pairs = sb("pairs", [P, 2, NT, 2])
        info = sb("info", [P, SLOT_TILES, 2])

        pr = sb("pr", [P, NT, E])
        s9 = sb("s9", [P, 6, NT])
        oh = [sb(f"oh{k}", [P, NT, E]) for k in range(2)]
        scr = sb("scr", [P, NT, E])
        scr2 = sb("scr2", [P, NT, E])
        member = sb("member", [P, NT, E])
        pre = sb("pre", [P, NT + 1, E])
        tiles_k = sb("tiles_k", [P, E, NT])
        tiles_e = sb("tiles_e", [P, E])
        start_k = sb("start_k", [P, E, E])
        past_e = sb("past_e", [P, E - 1])
        start_e = sb("start_e", [P, E])
        slot_f = sb("slot_f", [P, 2, NT])
        slot_i = sb("slot_i", [P, 2, NT], I32)
        te_k = sb("te_k", [P, SLOT_TILES, E - 1])
        te = sb("te", [P, SLOT_TILES])
        tile_expert = sb("tile_expert", [P, SLOT_TILES], I32)
        tb = sb("tb", [P, SLOT_TILES])
        tile_base = sb("tile_base", [P, SLOT_TILES], I32)
        gates = sb("gates", [P, NT, E])
        b1t = sb("b1t", [P, 2, KE])

        PS = ctx.enter_context(nc.psum_tensor("PS", [P, 8, 512], F32))

        S = {n: sem(n) for n in (
            "l_first", "l_second", "l_pt1", "l_pt2", "l_pt3", "l_vec", "l_qkv", "l_mid", "l_ff1", "l_ff2", "l_rows",
            "l_moe", "l_moe_late", "slots_empty", "acc_dummies",
            "c_pool", "c_int", "c_dve", "wxd",
            "embedded", "stream_set", "class_set", "rstd_squared", "second_var", "second_logged", "second_rstd",
            "second_scaled", "normed_images",
            "pair_in", "half_mm", "half_out", "keys0_out", "keys1_out", "values_mm", "values_out", "scores_mm",
            "masked", "max_taken", "less_max", "probabilities", "transposed", "transposed_out", "weighted",
            "sums_inverted", "normalized",
            "output_transposed", "output_out",
            "projected", "projected_out", "attention_added", "drive_mm", "tanh_done", "velocity", "state", "decayed",
            "decayed_less_state",
            "loop_added", "ff_in_mm", "gelu_done", "ff_out_mm", "ff_out_biased", "ff_added", "block_added",
            "logits_mm", "shifted", "exponentials", "row_transposed", "row_out", "route", "member", "ranks_mm",
            "gates", "gates_transposed", "gates_out", "residual_row_mm", "residual_row_out", "acc_set0", "acc_set1",
            "slot_no", "pairs", "numbers", "tokens_a", "tokens_b", "info0", "info1", "info2", "info3", "tile_expert",
            "scattered",
            "xin0", "xin1", "xin2", "xin3", "input_transposed", "input_out", "layer1_mm", "weights_in", "bias_in",
            "relu_done", "layer2_mm", "gated", "rows_added",
        )}

        n0 = Norm(sem, "n0", hT, S["stream_set"], 1, (4,), (5, 1, 5, 4))
        n0.var_used = S["second_var"]
        n1 = Norm(sem, "n1", x0T, S["attention_added"], 1, (6,), (7,))
        n2 = Norm(sem, "n2", x0T, S["loop_added"], 1, (0, 1), (2, 3))
        n3 = Norm(sem, "n3", hT, S["block_added"], 1, (0,), (1,))

        def chunk(c):
            return slice(c * CT, (c + 1) * CT)

        def over_k(ap, n):
            return ap.unsqueeze(1).broadcast_to([P, KD, n])

        def attention_steps(eng, step):
            step(0, 0, 0)
            with eng.Fori(0, IMG // CI - 1) as c:
                for j in range(CI):
                    step(c * CI + (1 + j), (1 + j) % CI, c * (CI // 2) + (2 + j) // 2)
            for i in range(IMG - 3, IMG):
                step(i, i % CI, (i + 1) // 2)

        def expert_steps(eng, step):
            step(0, 0, 0)
            with eng.Fori(0, SLOT_TILES // XR - 1) as r:
                for j in range(XR):
                    step(r * XR + (1 + j), (1 + j) % XR, r + (1 + j) // XR)
            for i in range(SLOT_TILES - 3, SLOT_TILES):
                step(i, i % XR, i // XR)

        block = ctx.enter_context(nc.Block())

        @block.sync
        def _(sp):
            half = KPATCH // 2
            for i, signal in enumerate(("l_first", "l_second")):
                sp.dma_start(wtok[:, i * half:(i + 1) * half, :], tok_w[:, i * half:(i + 1) * half, :]
                             ).then_inc(S[signal], 16)
                sp.dma_start(pt[0][:, i * half:(i + 1) * half, :], patches[0][:, i * half:(i + 1) * half, :]
                             ).then_inc(S[signal], 16)
            sp.dma_start(pt[1], patches[1]).then_inc(S["l_pt1"], 16)
            sp.dma_start(vecs[:, :], vec).then_inc(S["l_vec"], 16)
            sp.dma_start(wqkv, qkv_w).then_inc(S["l_qkv"], 16)
            sp.dma_start(vb_rows[:, :], v_b.broadcast_to([P, D])).then_inc(S["l_rows"], 16)
            sp.dma_start(gb_rows[:, :], gate_b.broadcast_to([P, E])).then_inc(S["l_rows"], 16)
            sp.dma_start(b2_rows[:, :], moe_b2).then_inc(S["l_rows"], 16)
            sp.dma_start(gate_t[:, :, :], gate_w).then_inc(S["l_rows"], 16)
            for c in range(2, NCH):
                sp.wait_ge(S["embedded"], c - 1)
                sp.dma_start(pt[c % 2], patches[c]).then_inc(S[f"l_pt{c}"], 16)
            sp.dma_start(wout, out_w).then_inc(S["l_mid"], 16)
            sp.dma_start(wctx, ctx_w).then_inc(S["l_mid"], 16)
            sp.dma_start(wx[:, :, :], x_w).then_inc(S["l_mid"], 16)
            sp.dma_start(wff1, ff1_w).then_inc(S["l_ff1"], 16)
            sp.dma_start(wff2, ff2_w).then_inc(S["l_ff2"], 16)
            for e in range(E - 3):
                sp.dma_start(W[:, e * WE:(e + 1) * WE], moe_w[e]).then_inc(S["l_moe"], 16)
            sp.wait_ge(S["scores_mm"], 2 * IMG)
            sp.dma_start(W[:, (E - 3) * WE:(E - 2) * WE], moe_w[E - 3]).then_inc(S["l_moe"], 16)
            sp.wait_ge(S["drive_mm"], 2 * NCH)
            sp.dma_start(W[:, (E - 1) * WE:E * WE], moe_w[E - 1]).then_inc(S["l_moe_late"], 16)

            def token_rows(t, signal):
                sp.wait_ge(S["row_out"], t + 1)
                sp.dma_start(tokens[t * P:(t + 1) * P, :], rows[t]).then_inc(S[signal], 16)

            for t in range(*ROUTED[0]):
                token_rows(t, "tokens_a")
            sp.wait_ge(S["ff_out_mm"], KD * NCH)
            sp.dma_start(W[:, (E - 2) * WE:(E - 1) * WE], moe_w[E - 2]).then_inc(S["l_moe_late"], 16)
            for t in range(ROUTED[0][1], NT):
                token_rows(t, "tokens_b")

            sp.wait_ge(S["tile_expert"], 1)
            sp.wait_ge(S["scattered"], 16 * 2 * NT)
            for i in range(SLOT_TILES):
                base = sp.value_load(tile_base[0:1, i:i + 1], min_val=0, max_val=(ALL_TILES - 1) * P)
                if i >= XR:
                    sp.wait_ge(S[f"info{i % XR}"], 16 * (i // XR))
                sp.dma_start(info[:, i, :], slots[bass.ds(base, P), :]).then_inc(S[f"info{i % XR}"], 16)

            sp.wait_ge(S["rows_added"], 16 * SLOT_TILES)

        @block.gpsimd
        def _(pool):
            done = [0]

            def link(ins):
                done[0] += 1
                ins.then_inc(S["c_pool"], 1)
                pool.wait_ge(S["c_pool"], done[0])

            pool.memset(mask[:, :], 0.0)
            pool.memset(below[:, :], 1.0)
            pool.memset(head_of[:, :], 1.0)
            pool.memset(before[:, :, :], 1.0)
            pool.memset(empty[:, :, :], 0.0)
            pool.memset(zero[:, :], 0.0)
            link(pool.memset(ident[:, :], 0.0))
            pool.affine_select(out=ident[:, :], in_=ident[:, :], compare_op=ALU.not_equal, fill=1.0, base=0,
                               pattern=[[-1, P]], channel_multiplier=1)
            pool.affine_select(out=mask[:, :], in_=mask[:, :], compare_op=ALU.is_ge, fill=NEG, base=0,
                               pattern=[[-1, SEQ]], channel_multiplier=1)
            pool.affine_select(out=below[:, :], in_=below[:, :], compare_op=ALU.is_gt, fill=0.0, base=0,
                               pattern=[[1, P]], channel_multiplier=-1)
            pool.affine_select(out=before[:, :, :], in_=before[:, :, :], compare_op=ALU.is_gt, fill=0.0, base=0,
                               pattern=[[1, E], [-1, E]], channel_multiplier=0)
            link(pool.affine_select(out=head_of[:, :], in_=head_of[:, :], compare_op=ALU.is_ge, fill=0.0, base=0,
                                    pattern=[[-HD, HG]], channel_multiplier=1))
            pool.affine_select(out=head_of[:, :], in_=head_of[:, :], compare_op=ALU.is_ge, fill=0.0, base=HD - 1,
                               pattern=[[HD, HG]], channel_multiplier=-1)
            link(pool.iota(empty[:, :, 1].bitcast(I32), pattern=[[1, P]], base=TOK, channel_multiplier=0))
            pool.dma_start(slots.rearrange("(t p) c -> t (p c)", p=P),
                           empty[:, :, :].rearrange("t p c -> t (p c)")).then_inc(S["slots_empty"], 16)
            pool.dma_start(out[TOK:TOK + P, :], zero[:, :]).then_inc(S["acc_dummies"], 16)
            pool.dma_start(tokens[CAP:TOK + P, :], zero[0:TOK + P - CAP, :]).then_inc(S["acc_dummies"], 16)
            pool.iota(iw[:, 0:NT], pattern=[[P, NT]], base=0, channel_multiplier=0)
            pool.iota(iw[:, NT:2 * NT], pattern=[[P, NT]], base=0, channel_multiplier=1)
            pool.iota(iw[:, 2 * NT:2 * NT + SLOT_TILES], pattern=[[1, SLOT_TILES]], base=0, channel_multiplier=0)
            pool.iota(iw[:, 2 * NT + SLOT_TILES:2 * NT + SLOT_TILES + E], pattern=[[-1, E]], base=E,
                      channel_multiplier=0)
            pool.iota(iw[:, 2 * NT + SLOT_TILES + E:], pattern=[[CAP, E]], base=0,
                      channel_multiplier=0).then_inc(S["c_int"], 1)

            def pair_in(p, pp):
                pool.wait_ge(S["normed_images"], 2 * p + 2)
                if not isinstance(p, int) or p >= 2:
                    pool.wait_ge(S["values_mm"], 2 * p - 2)
                pool.tensor_copy(xi[:, pp, :, :], nT[:, :, bass.ds(p * (2 * SEQ), 2 * SEQ)]).then_inc(S["pair_in"], 2)

            def keys_out(n, pos, p):
                pool.wait_ge(S["half_out"], 2 * p + 2)
                if not isinstance(n, int) or n >= 2:
                    pool.wait_ge(S["scores_mm"], 2 * n - 2)
                half = pos % 2 * SEQ
                pool.tensor_tensor(kx[pos % 2][:, 1, :, :],
                                   qk[:, pos // 2, 2 * KD - 1, half:half + SEQ].unsqueeze(1).broadcast_to([P, HG, SEQ]),
                                   head_of[:, :].unsqueeze(2).broadcast_to([P, HG, SEQ]),
                                   ALU.mult).then_inc(S["keys1_out"], 1)

            def affine(c):
                pool.wait_ge(S["second_scaled"], c + 1)
                for m in range(KD):
                    part = nT[:, m, chunk(c)]
                    last = pool.tensor_scalar(part, part, vcol("g_attn", m), vcol("b_attn", m), ALU.mult, ALU.add)
                last.then_inc(S["normed_images"], CI)

            pool.wait_ge(S["l_vec"], 16)
            affine(0)
            pair_in(0, 0)
            pair_in(1, 1)
            affine(1)
            pool.wait_ge(S["embedded"], NCH)
            keys_out(0, 0, 0)

            def step(i, pos, p):
                if pos % 2 == 1 and (not isinstance(i, int) or i + 3 < IMG):
                    pair_in(p + 1, (pos + 3) // 2 % 2)
                if not isinstance(i, int) or i + 1 < IMG:
                    keys_out(i + 1, (pos + 1) % CI, p)

            attention_steps(pool, step)

            def r_of(n, c):
                pool.wait_ge(S["decayed"], n)
                pool.wait_ge(S["state"], n)
                pool.tensor_tensor(rT[:, :, chunk(c)], pe[:, c % 2, :, :], xsT[:, :, chunk(c)],
                                   ALU.subtract).then_inc(S["decayed_less_state"], 1)

            for c in range(NCH):
                r_of(c + 1, c)
            with pool.Fori(1, ITERS - 1) as t:
                for c in range(NCH):
                    r_of(t * NCH + (c + 1), c)

            pool.wait_ge(S["slots_empty"], 16)
            pool.wait_ge(S["numbers"], 1)
            for batch, (first, behind) in enumerate(ROUTED):
                pool.wait_ge(S["pairs"], batch + 1)
                pool.wait_ge(S["slot_no"], batch + 1)
                for t in range(first, behind):
                    n = P if t < NT - 1 else LAST
                    for k in range(2):
                        pool.indirect_dma_start(
                            out=slots, out_offset=bass.IndirectOffsetOnAxis(ap=slot_i[0:n, k, t:t + 1], axis=0),
                            in_=pairs[0:n, k, t, :], in_offset=None,
                        ).then_inc(S["scattered"], 16)

            def gather(i):
                pool.wait_ge(S[f"info{i % XR}"], 16 * (i // XR + 1))
                if i >= XR:
                    pool.wait_ge(S["input_transposed"], i - XR + 1)
                pool.indirect_dma_start(
                    out=xin[:, i % XR, :], out_offset=None, in_=tokens,
                    in_offset=bass.IndirectOffsetOnAxis(ap=info[:, i, 1:2].bitcast(I32), axis=0),
                ).then_inc(S[f"xin{i % XR}"], 16)

            def add_rows(i):
                pool.wait_ge(S["gated"], i + 1)
                if i > 0:
                    pool.wait_ge(S["rows_added"], 16 * i)
                pool.indirect_dma_start(
                    out=out, out_offset=bass.IndirectOffsetOnAxis(ap=info[:, i, 1:2].bitcast(I32), axis=0),
                    in_=yt[:, i % 2, :], in_offset=None, compute_op=ALU.add,
                ).then_inc(S["rows_added"], 16)

            pool.wait_ge(S["acc_dummies"], 16 * 2)
            pool.wait_ge(S["tokens_a"], 16 * ROUTED[0][1])
            pool.wait_ge(S["tokens_b"], 16 * (NT - ROUTED[0][1]))
            pool.wait_ge(S["gelu_done"], KF * NCH)
            pool.wait_ge(S["ff_out_mm"], KD * NCH)
            for i in range(XR - 1):
                gather(i)
            pool.wait_ge(S["acc_set0"], 16 * -(-NT // 2))
            pool.wait_ge(S["acc_set1"], 16 * (NT // 2))
            for i in range(SLOT_TILES):
                if i + XR - 1 < SLOT_TILES:
                    gather(i + XR - 1)
                add_rows(i)

        @block.tensor
        def _(pe_):
            mm = pe_.matmul

            def norm_mean(n, c):
                pe_.wait_ge(n.ready, n.per_chunk * (c + 1))
                if c >= len(n.mean_banks):
                    pe_.wait_ge(n.centered, c - len(n.mean_banks) + 1)
                bank = n.mean_banks[c % len(n.mean_banks)]
                for k in range(KD):
                    last = mm(PS[:, bank, 0:CT], mean_m[:, :], n.source[:, k, chunk(c)], start=k == 0,
                              stop=k == KD - 1)
                last.then_inc(n.mean, 1)

            def norm_var(n, c):
                pe_.wait_ge(n.squared, c + 1)
                if c >= len(n.var_banks):
                    pe_.wait_ge(n.var_used, c - len(n.var_banks) + 1)
                bank = n.var_banks[c % len(n.var_banks)]
                for k in range(KD):
                    last = mm(PS[:, bank, 0:CT], mean_m[:, :], sq[:, c % 2, k, :], start=k == 0, stop=k == KD - 1)
                last.then_inc(n.var, 1)

            def embed(c):
                if c >= 1:
                    pe_.wait_ge(S[f"l_pt{c}"], 16)
                if c >= 2:
                    pe_.wait_ge(S["stream_set"], c - 1)
                half = KPATCH // 2
                for part, signal in enumerate(("l_first", "l_second")):
                    if c == 0:
                        pe_.wait_ge(S[signal], 16 * 2)
                    for m in range(KD):
                        for k in range(part * half, (part + 1) * half):
                            last = mm(PS[:, 2 * (c % 2) + m, 0:CP], wtok[:, k, m * P:(m + 1) * P], pt[c % 2][:, k, :],
                                      start=k == 0, stop=k == KPATCH - 1)
                last.then_inc(S["embedded"], 1)

            for s in range(NCH):
                embed(s)
                if s == 0:
                    pe_.wait_ge(S["c_dve"], 1)
                    pe_.wait_ge(S["class_set"], 1)
                if s >= 1:
                    norm_mean(n0, s - 1)
                if s >= 2:
                    norm_var(n0, s - 2)

            QK_BANK, V_BANK, T_BANK = 6, 7, 4

            def half_in(n, pos):
                pe_.wait_ge(S["pair_in"], n + 1)
                if not isinstance(n, int) or n >= 1:
                    pe_.wait_ge(S["half_out"], n)
                for i in range(KD):
                    m = pos % 2 * KD + i
                    for k in range(KD):
                        last = mm(PS[:, QK_BANK, i * 2 * SEQ:(i + 1) * 2 * SEQ], wqkv[:, k, m * P:(m + 1) * P],
                                  xi[:, pos // 2, k, :], start=k == 0, stop=k == KD - 1)
                last.then_inc(S["half_mm"], 1)

            def values(n, pos):
                if not isinstance(n, int) or n >= 2:
                    pe_.wait_ge(S["normalized"], n - 1)
                for k in range(KD):
                    last = mm(PS[0:SEQ, V_BANK, 0:D], xi[:, pos // 2, k, pos % 2 * SEQ:(pos % 2 + 1) * SEQ],
                              wqkv[:, k, 2 * D:3 * D], start=k == 0, stop=k == KD - 1)
                last.then_inc(S["values_mm"], 1)

            def scores(n, pos, g):
                pe_.wait_ge(S["keys0_out"] if g == 0 else S["keys1_out"], n + 1)
                if not isinstance(n, int) or n >= 1:
                    pe_.wait_ge(S["masked"], 2 * n + g - 1)
                for b in range(2):
                    bank = PS[0:SEQ, 2 * g + b, 0:HB * SEQ]
                    last = mm(bank, qk[:, pos // 2, g, pos % 2 * SEQ:(pos % 2 + 1) * SEQ],
                              kx[pos % 2][:, g, HB * b:HB * b + HB, :].rearrange("p h s -> p (h s)"), start=True,
                              stop=True)
                last.then_inc(S["scores_mm"], 1)

            def transposes(n, g):
                pe_.wait_ge(S["probabilities"], 2 * n + g + 1)
                if g == 1 or not isinstance(n, int) or n >= 1:
                    pe_.wait_ge(S["transposed_out"], 2 * n + g)
                if g == 1 and (not isinstance(n, int) or n >= 1):
                    pe_.wait_ge(S["output_out"], n)
                for h in range(HG):
                    last = pe_.transpose(PS[0:SEQ, T_BANK + h // HB, (h % HB) * SEQ:(h % HB + 1) * SEQ],
                                         ex[g][0:SEQ, h, :], ident[0:SEQ, 0:SEQ])
                last.then_inc(S["transposed"], 1)

            def weighted(n, par, g, last_image):
                pe_.wait_ge(S["transposed_out"], 2 * n + g + 1)
                pe_.wait_ge(S["values_out"], n + 1 if last_image else n + 2)
                for h in range(HG):
                    a = (g * HG + h) * (HD + 1)
                    last = mm(PS[0:SEQ, V_BANK, a:a + HD + 1],
                              pT[g][0:SEQ, h // HB, (h % HB) * SEQ:(h % HB + 1) * SEQ],
                              va[par][0:SEQ, g * HG + h, :], start=True, stop=True)
                last.then_inc(S["weighted"], 1)

            def output_transposed(n):
                pe_.wait_ge(S["normalized"], n + 1)
                pe_.wait_ge(S["transposed_out"], 2 * n + 2)
                for m in range(KD):
                    a = HB * SEQ + m * SEQ
                    last = pe_.transpose(PS[:, T_BANK + 1, a:a + SEQ],
                                         att[0:SEQ, m * HG:(m + 1) * HG, :].rearrange("p h d -> p (h d)"),
                                         ident[0:SEQ, 0:SEQ])
                last.then_inc(S["output_transposed"], 1)

            pe_.wait_ge(S["l_qkv"], 16)
            half_in(0, 0)
            norm_mean(n0, 3)
            pe_.wait_ge(S["second_var"], 1)
            norm_var(n0, 2)
            half_in(1, 1)
            values(0, 0)
            norm_var(n0, 3)
            half_in(2, 2)
            pe_.wait_ge(S["second_var"], 2)
            scores(0, 0, 0)
            scores(0, 0, 1)

            def project(c):
                pe_.wait_ge(S["output_out"], CI * (c + 1))
                if c == 0:
                    pe_.wait_ge(S["l_mid"], 16 * 3)
                    pe_.wait_ge(S["masked"], 2 * IMG)
                if c == 2:
                    pe_.wait_ge(S["projected_out"], 1)
                for m in range(KD):
                    for k in range(KD):
                        last = mm(PS[:, PROJECTED[c] + m, 0:CT], wout[:, k, m * P:(m + 1) * P], nT[:, k, chunk(c)],
                                  start=k == 0, stop=k == KD - 1)
                last.then_inc(S["projected"], 1)

            def step(i, pos, p):
                more = not isinstance(i, int) or i + 1 < IMG
                after = (pos + 1) % CI
                if not isinstance(i, int) or i + 3 < IMG:
                    half_in(i + 3, (pos + 3) % CI)
                if isinstance(i, int) and i == 0:
                    pe_.wait_ge(S["values_out"], 1)
                    values(i + 1, after)
                    pe_.wait_ge(S["second_var"], NCH)
                transposes(i, 0)
                if not more:
                    project(0)
                if more and not (isinstance(i, int) and i == 0):
                    values(i + 1, after)
                if not isinstance(i, int) or i > 0:
                    output_transposed(i - 1)
                for g in range(KD):
                    if g > 0:
                        transposes(i, g)
                        if not more:
                            project(1)
                    if more:
                        scores(i + 1, after, g)
                    weighted(i, pos % 2, g, not more)

            attention_steps(pe_, step)
            norm_mean(n1, 0)
            output_transposed(IMG - 1)

            def drive(c, w, rhs, begin):
                for m in range(KD):
                    for k in range(KD):
                        last = mm(PS[:, 2 * c + m, 0:CT], w[:, k, m * P:(m + 1) * P], rhs[:, k, chunk(c)],
                                  start=begin and k == 0, stop=not begin and k == KD - 1, skip_group_check=True)
                return last

            def context(c):
                pe_.wait_ge(S["projected_out"], (3, 2, NCH, NCH)[c])
                drive(c, wctx, nT, True).then_inc(S["drive_mm"], 1)

            def first_drive(c):
                pe_.wait_ge(n1.done, c + 1)
                drive(c, wx, xsT, False).then_inc(S["drive_mm"], 1)

            project(2)
            norm_mean(n1, 1)
            project(3)
            norm_var(n1, 0)
            norm_mean(n1, 2)
            norm_var(n1, 1)
            context(0)
            norm_mean(n1, 3)
            context(1)
            norm_var(n1, 2)
            context(2)
            norm_var(n1, 3)

            first_drive(0)
            first_drive(1)
            pe_.wait_ge(n1.centered, NCH)
            pe_.wait_ge(n1.rstd, NCH)
            context(3)
            first_drive(2)
            first_drive(3)
            pe_.wait_ge(S["wxd"], 1)
            with pe_.Fori(0, ITERS - 1) as t:
                for c in range(NCH):
                    pe_.wait_ge(S["velocity"], t * NCH + (c + 1))
                    drive(c, wxd, eT, False).then_inc(S["drive_mm"], 1)

            def ff_in(c, m):
                i = c * KF + m
                if m == 0:
                    pe_.wait_ge(n2.done, c + 1)
                if i >= 2:
                    pe_.wait_ge(S["gelu_done"], i - 1)
                for k in range(KD):
                    last = mm(PS[:, 4 + i % 2, 0:CT], wff1[:, k, m * P:(m + 1) * P], xsT[:, k, chunk(c)],
                              start=k == 0, stop=k == KD - 1)
                last.then_inc(S["ff_in_mm"], 1)

            def ff_out(c, m):
                if m == 0:
                    pe_.wait_ge(S["gelu_done"], KF * (c + 1))
                if c >= 1:
                    pe_.wait_ge(S["ff_out_biased"], KD * (c - 1) + m + 1)
                for k in range(KF):
                    last = mm(PS[:, 6 + m, 0:CT], wff2[:, k, m * P:(m + 1) * P], fh[c % 2][:, k, :], start=k == 0,
                              stop=k == KF - 1)
                last.then_inc(S["ff_out_mm"], 1)

            norm_mean(n2, 0)
            norm_mean(n2, 1)
            pe_.wait_ge(S["tanh_done"], (ITERS - 1) * NCH + 2)
            norm_var(n2, 0)
            norm_mean(n2, 2)
            norm_var(n2, 1)
            norm_mean(n2, 3)
            norm_var(n2, 2)
            pe_.wait_ge(S["l_ff1"], 16)
            pe_.wait_ge(S["l_ff2"], 16)
            pe_.wait_ge(S["tanh_done"], ITERS * NCH)
            for m in range(2):
                ff_in(0, m)
            for c in range(2):
                for m in range(2 if c == 0 else 0, KF):
                    ff_in(c, m)
                if c == 0:
                    norm_var(n2, 3)
            for m in range(KD):
                ff_out(0, m)
            for c in range(2, NCH):
                for m in range(KF):
                    if m == KF // 2:
                        norm_mean(n3, c - 2)
                    ff_in(c, m)
                norm_var(n3, c - 2)
                ff_out(c - 1, 0)
                if c < NCH - 1:
                    ff_out(c - 1, 1)

            def route_tile(t, bank):
                pe_.wait_ge(n3.done, min((t * P + P - 1) // CT + 1, NCH))
                for k in range(KD):
                    last = mm(PS[:, bank, t * E:(t + 1) * E], nT[:, k, t * P:(t + 1) * P], gate_t[:, k, :],
                              start=k == 0, stop=k == KD - 1)
                last.then_inc(S["logits_mm"], 1)

            def row_tile(t):
                if t >= 2:
                    pe_.wait_ge(S["row_out"], t - 1)
                for k in range(KD):
                    last = pe_.transpose(PS[:, 3 + t % 2 * 2, k * P:(k + 1) * P], nT[:, k, t * P:(t + 1) * P],
                                         ident[:, :])
                last.then_inc(S["row_transposed"], 1)

            def ranks_and_counts(batch):
                pe_.wait_ge(S["member"], batch + 1)
                first, behind = ROUTED[batch]
                mem = member[:, first:behind, :].rearrange("p t e -> p (t e)")
                bank = ROUTED_IN[batch]
                mm(PS[:, bank, (NT + first) * E:(NT + behind) * E], below[:, :], mem, start=True, stop=True)
                mm(PS[:, bank, (2 * NT + first) * E:(2 * NT + behind) * E], ones[:, :], mem, start=True, stop=True
                   ).then_inc(S["ranks_mm"], 1)

            pe_.wait_ge(S["l_rows"], 16 * 4)
            for t in range(*ROUTED[0]):
                route_tile(t, ROUTED_IN[0])
            ff_out(2, 1)
            pe_.wait_ge(S["gelu_done"], KF * NCH)
            for t in range(*ROUTED[0]):
                row_tile(t)
            ff_out(3, 0)
            norm_mean(n3, 2)
            ranks_and_counts(0)
            ff_out(3, 1)
            norm_var(n3, 2)
            norm_mean(n3, 3)

            def gates_transposed(batch):
                pe_.wait_ge(S["gates"], batch + 1)
                if batch >= 1:
                    pe_.wait_ge(S["gates_out"], batch)
                first, behind = ROUTED[batch]
                for t in range(first, behind):
                    n = P if t < NT - 1 else LAST
                    last = pe_.transpose(PS[0:E, 4, (t - first) * P:(t - first) * P + n],
                                         gates[0:n, t, :], ident[0:n, 0:n])
                last.then_inc(S["gates_transposed"], 1)

            def residual_row(t):
                n = P if t < NT - 1 else LAST
                bank = 6 + t % 2
                if t >= 2:
                    pe_.wait_ge(S["residual_row_out"], t - 1)
                for k in range(KD):
                    to = PS[0:n, bank, k * P:(k + 1) * P]
                    mm(to, gT[0:E, t * P:t * P + n], b2_rows[:, k * P:(k + 1) * P], start=True, stop=False)
                    last = mm(to, hT[:, k, t * P:t * P + n], ident[:, :], start=False, stop=True)
                last.then_inc(S["residual_row_mm"], 1)

            pe_.wait_ge(S["slot_no"], 1)
            for t in range(*ROUTED[1]):
                route_tile(t, ROUTED_IN[1])
            gates_transposed(0)
            pe_.wait_ge(S["ff_out_biased"], KD * NCH)
            pe_.wait_ge(S["gates_out"], 1)
            residual_row(0)
            norm_var(n3, 3)
            for t in range(*ROUTED[1]):
                row_tile(t)
            for t in range(1, ROUTED[0][1]):
                residual_row(t)
            ranks_and_counts(1)
            for t in range(*ROUTED[2]):
                route_tile(t, ROUTED_IN[2])
            for t in range(*ROUTED[2]):
                row_tile(t)
            ranks_and_counts(2)
            for batch in (1, 2):
                gates_transposed(batch)
                pe_.wait_ge(S["gates_out"], batch + 1)
                for t in range(*ROUTED[batch]):
                    residual_row(t)
            pe_.wait_ge(S["row_out"], NT)

            def input_tile(i, ring, lap):
                pe_.wait_ge(S[f"xin{ring}"], 16 * (lap + 1))
                if not isinstance(i, int) or i >= 1:
                    pe_.wait_ge(S["input_out"], i)
                for k in range(KD):
                    last = pe_.transpose(PS[:, 5, k * P:(k + 1) * P], xin[:, ring, k * P:(k + 1) * P], ident[:, :])
                last.then_inc(S["input_transposed"], 1)

            def expert_of(i):
                return pe_.value_load(tile_expert[0:1, bass.ds(i, 1)], min_val=0, max_val=E - 1)

            def layer1(i, ring):
                par = ring % 2
                pe_.wait_ge(S["input_out"], i + 1)
                pe_.wait_ge(S["weights_in"], i + 1)
                if not isinstance(i, int) or i >= 2:
                    pe_.wait_ge(S["relu_done"], i - 1)
                for m in range(KE):
                    to = PS[:, 2 * par + m // 4, (m % 4) * P:(m % 4 + 1) * P]
                    for k in range(KD):
                        last = mm(to, w1[par][:, k, m * P:(m + 1) * P], xt[:, par, k, :], start=k == 0, stop=k == KD - 1)
                last.then_inc(S["layer1_mm"], 1)

            def layer2(i):
                w = expert_of(i) * WE
                pe_.wait_ge(S["relu_done"], i + 1)
                if not isinstance(i, int) or i >= 1:
                    pe_.wait_ge(S["gated"], i)
                for m in range(KE):
                    last = mm(PS[:, 4, 0:D], hid[:, m, :], W[:, bass.ds(w + (KD * EH + m * D), D)],
                              start=m == 0, stop=m == KE - 1)
                last.then_inc(S["layer2_mm"], 1)

            pe_.wait_ge(S["l_moe"], 16 * (E - 2))
            pe_.wait_ge(S["l_moe_late"], 16 * 2)
            pe_.wait_ge(S["tile_expert"], 1)
            input_tile(0, 0, 0)
            input_tile(1, 1, 0)
            layer1(0, 0)

            def expert_step(i, ring, lap):
                if not isinstance(i, int) or i + 1 < SLOT_TILES:
                    layer1(i + 1, (ring + 1) % XR)
                if not isinstance(i, int) or i + 2 < SLOT_TILES:
                    input_tile(i + 2, (ring + 2) % XR, lap + (ring + 2) // XR)
                layer2(i)

            expert_steps(pe_, expert_step)

        @block.scalar
        def _(act):
            f = act.activation

            def norm_square(n, c):
                act.wait_ge(n.centered, c + 1)
                f(sq[:, c % 2, :, :], xc[:, c % 2, :, :], ACT.Square).then_inc(n.squared, 1)

            def norm_rstd(n, c):
                act.wait_ge(n.var, c + 1)
                if c >= 2:
                    act.wait_ge(n.done, c - 1)
                f(rs[:, c % 2, :], PS[:, n.var_banks[c % len(n.var_banks)], 0:CT], ACT.Ln,
                  bias=eps[:, 0:1]).then_inc(n.logged, 1)
                act.wait_ge(n.logged, c + 1)
                f(rs[:, c % 2, :], rs[:, c % 2, :], ACT.Exp, scale=-0.5).then_inc(n.rstd, 1)

            act.preload_act_table_set("natural_log_exp_and_others")
            act.wait_ge(S["l_vec"], 16)
            act.wait_ge(S["c_dve"], 1)
            def patches_out(c):
                act.wait_ge(S["embedded"], c + 1)
                for m in range(KD):
                    to = hT[:, m, chunk(c)].rearrange("p (i t) -> p i t", i=CI)[:, :, 1:SEQ]
                    last = f(to, PS[:, 2 * (c % 2) + m, 0:CP].rearrange("p (i t) -> p i t", i=CI), ACT.Identity,
                             bias=vcol("tok_b", m))
                last.then_inc(S["stream_set"], 1)

            def second_rstd(c):
                act.wait_ge(S["second_var"], c + 1)
                f(rs2[:, c % 2, :], rs2[:, c % 2, :], ACT.Ln, bias=eps[:, 0:1]).then_inc(S["second_logged"], 1)
                act.wait_ge(S["second_logged"], c + 1)
                f(rs2[:, c % 2, :], rs2[:, c % 2, :], ACT.Exp, scale=-0.5).then_inc(S["second_rstd"], 1)

            patches_out(0)
            patches_out(1)
            norm_square(n0, 0)
            patches_out(2)
            norm_square(n0, 1)
            norm_rstd(n0, 0)
            second_rstd(0)
            patches_out(3)
            norm_square(n0, 2)
            norm_rstd(n0, 1)
            second_rstd(1)
            norm_square(n0, 3)
            norm_rstd(n0, 2)

            def affine(c):
                act.wait_ge(S["second_scaled"], c + 1)
                for m in range(KD):
                    part = nT[:, m, chunk(c)]
                    last = f(part, part, ACT.Identity, bias=vcol("b_attn", m), scale=vcol("g_attn", m))
                last.then_inc(S["normed_images"], CI)

            def probabilities(n, g):
                act.wait_ge(S["less_max"], 2 * n + g + 1)
                if not isinstance(n, int) or n >= 1:
                    act.wait_ge(S["transposed"], 2 * n + g - 1)
                f(ex[g][0:SEQ, :, :], sh[g][0:SEQ, :, :], ACT.Exp, scale=float(HD) ** -0.5).then_inc(S["probabilities"], 1)

            def keys_out(n, pos, p):
                act.wait_ge(S["half_out"], 2 * p + 2)
                if not isinstance(n, int) or n >= 2:
                    act.wait_ge(S["scores_mm"], 2 * n - 2)
                half = pos % 2 * SEQ
                for h in range(HG):
                    last = f(kx[pos % 2][:, 0, h, :], qk[:, pos // 2, KD, half:half + SEQ], ACT.Copy,
                             scale=head_of[:, h:h + 1])
                last.then_inc(S["keys0_out"], 1)

            def copy_transposed(n, g):
                act.wait_ge(S["transposed"], 2 * n + g + 1)
                if g == 0 and (not isinstance(n, int) or n >= 1):
                    act.wait_ge(S["output_transposed"], n)
                if not isinstance(n, int) or n >= 1:
                    act.wait_ge(S["weighted"], 2 * n + g - 1)
                f(pT[g][0:SEQ, :, :], PS[0:SEQ, 4:6, 0:HB * SEQ], ACT.Copy).then_inc(S["transposed_out"], 1)

            def copy_output(n):
                act.wait_ge(S["output_transposed"], n + 1)
                f(nT[:, :, bass.ds(n * SEQ, SEQ)],
                  PS[:, 5, HB * SEQ:(HB + KD) * SEQ].rearrange("p (k s) -> p k s", k=KD), ACT.Copy
                  ).then_inc(S["output_out"], 1)

            keys_out(0, 0, 0)
            second_rstd(2)
            norm_rstd(n0, 3)
            keys_out(1, 1, 0)
            probabilities(0, 0)
            second_rstd(3)

            def project_out(c):
                act.wait_ge(S["projected"], c + 1)
                for m in range(KD):
                    last = f(nT[:, m, chunk(c)], PS[:, PROJECTED[c] + m, 0:CT], ACT.Identity, bias=vcol("out_b", m))
                last.then_inc(S["projected_out"], 1)

            def step(i, pos, p):
                copy_transposed(i, 0)
                if not isinstance(i, int) or i > 0:
                    copy_output(i - 1)
                probabilities(i, 1)
                if isinstance(i, int) and i == IMG - 1:
                    project_out(0)
                copy_transposed(i, 1)
                if isinstance(i, int) and i == 0:
                    affine(2)
                    affine(3)
                if not isinstance(i, int) or i + 1 < IMG:
                    probabilities(i + 1, 0)
                if not isinstance(i, int) or i + 2 < IMG:
                    keys_out(i + 2, (pos + 2) % CI, p if pos % 2 else p + 1)

            attention_steps(act, step)
            project_out(1)
            copy_output(IMG - 1)

            norm_square(n1, 0)
            project_out(2)
            norm_square(n1, 1)
            project_out(3)
            norm_rstd(n1, 0)
            norm_rstd(n1, 1)
            for c in range(2, NCH):
                norm_square(n1, c)
                norm_rstd(n1, c)

            def tanh(n, c, first):
                act.wait_ge(S["drive_mm"], n + NCH)
                if first and c < 2:
                    act.wait_ge(n1.done, NCH)
                else:
                    act.wait_ge(S["velocity"], n - 2)
                for m in range(KD):
                    last = f(u[:, c % 2, m, :], PS[:, 2 * c + m, 0:CT], ACT.Tanh, bias=vcol("b_inl", m))
                last.then_inc(S["tanh_done"], 1)

            def decay(n, c, first):
                act.wait_ge(S["velocity"], n)
                if not (first and c < 2):
                    act.wait_ge(S["decayed_less_state"], n - 2)
                f(pe[:, c % 2, :, :], eT[:, :, chunk(c)], ACT.Copy, scale=1.0 - DT).then_inc(S["decayed"], 1)

            def iteration(n, first):
                for c in range(NCH):
                    tanh(n + (c + 1), c, first)
                    if c >= 1:
                        decay(n + c, c - 1, first)
                decay(n + NCH, NCH - 1, first)

            iteration(0, True)
            with act.Fori(1, ITERS - 1) as t:
                iteration(t * NCH, False)
            for c in range(NCH):
                tanh((ITERS - 1) * NCH + c + 1, c, False)

            act.preload_act_table_set("natural_log_exp_and_others")
            norm_square(n2, 0)
            norm_square(n2, 1)
            norm_rstd(n2, 0)
            norm_rstd(n2, 1)
            norm_square(n2, 2)
            norm_rstd(n2, 2)

            def gelu(c, m):
                i = c * KF + m
                act.wait_ge(S["ff_in_mm"], i + 1)
                if c >= 2 and m == 0:
                    act.wait_ge(S["ff_out_mm"], KD * (c - 1))
                f(fh[c % 2][:, m, :], PS[:, 4 + i % 2, 0:CT], ACT.Gelu, bias=vcol("ff_b1", m)).then_inc(S["gelu_done"], 1)

            def ff_bias(c, ms=range(KD)):
                for m in ms:
                    act.wait_ge(S["ff_out_mm"], KD * c + m + 1)
                    if c >= 1 and m == 0:
                        act.wait_ge(S["ff_added"], c)
                    f(ffb_buf[:, m, :], PS[:, 6 + m, 0:CT], ACT.Identity, bias=vcol("ff_b2", m)
                      ).then_inc(S["ff_out_biased"], 1)

            for c in range(2):
                for m in range(KF):
                    gelu(c, m)
                    if c == 0 and m == 0:
                        norm_square(n2, 3)
            ff_bias(0)
            for c in range(2, NCH):
                for m in range(KF):
                    gelu(c, m)
                    if m == KF - 2:
                        norm_square(n3, c - 2)
                act.preload_act_table_set("natural_log_exp_and_others")
                if c == 2:
                    norm_rstd(n2, 3)
                norm_rstd(n3, c - 2)
                if c < NCH - 1:
                    ff_bias(c - 1)

            def row_out(t):
                act.wait_ge(S["row_transposed"], t + 1)
                f(rows[t], PS[:, 3 + t % 2 * 2, 0:D], ACT.Copy).then_inc(S["row_out"], 1)

            def exponentials(batch):
                act.wait_ge(S["shifted"], batch + 1)
                part = pr[:, ROUTED[batch][0]:ROUTED[batch][1], :]
                f(part, part, ACT.Exp).then_inc(S["exponentials"], 1)

            def gates_out(batch):
                act.wait_ge(S["gates_transposed"], batch + 1)
                act.wait_ge(S["ff_out_mm"], KD * NCH)
                a, b = ROUTED[batch][0] * P, min(ROUTED[batch][1] * P, TOK)
                f(gT[0:E, a:b], PS[0:E, 4, 0:b - a], ACT.Copy).then_inc(S["gates_out"], 1)

            def residual_row_out(t):
                n = P if t < NT - 1 else LAST
                act.wait_ge(S["residual_row_mm"], t + 1)
                if t >= 2:
                    act.wait_ge(S[f"acc_set{t % 2}"], 16 * (t // 2))
                else:
                    act.wait_ge(n3.done, 3)
                f(hrow[0:n, t % 2, :], PS[0:n, 6 + t % 2, 0:D], ACT.Copy).then_inc(S["residual_row_out"], 1)
                act.wait_ge(S["residual_row_out"], t + 1)
                act.dma_start(out[t * P:t * P + n, :], hrow[0:n, t % 2, :]).then_inc(S[f"acc_set{t % 2}"], 16)

            exponentials(0)
            ff_bias(2)
            for t in range(*ROUTED[0]):
                row_out(t)
            ff_bias(3, (0,))
            norm_square(n3, 2)
            ff_bias(3, (1,))
            norm_rstd(n3, 2)
            gates_out(0)
            norm_square(n3, 3)
            exponentials(1)
            residual_row_out(0)
            norm_rstd(n3, 3)
            for t in range(*ROUTED[1]):
                row_out(t)
            for t in range(1, ROUTED[0][1]):
                residual_row_out(t)
            exponentials(2)
            for t in range(*ROUTED[2]):
                row_out(t)
            for batch in (1, 2):
                gates_out(batch)
                for t in range(*ROUTED[batch]):
                    residual_row_out(t)

            def expert_of(i):
                return act.value_load(tile_expert[0:1, bass.ds(i, 1)], min_val=0, max_val=E - 1)

            def relu(i, ring):
                e = expert_of(i)
                f(b1t[:, ring % 2, :], vecs[:, bass.ds(e * KE + vec_at["moe_b1"], KE)], ACT.Copy
                  ).then_inc(S["bias_in"], 1)
                act.wait_ge(S["bias_in"], i + 1)
                act.wait_ge(S["layer1_mm"], i + 1)
                if not isinstance(i, int) or i > 0:
                    act.wait_ge(S["layer2_mm"], i)
                for m in range(KE):
                    last = f(hid[:, m, :], PS[:, 2 * (ring % 2) + m // 4, (m % 4) * P:(m % 4 + 1) * P], ACT.Relu,
                             bias=b1t[:, ring % 2, m:m + 1])
                last.then_inc(S["relu_done"], 1)

            act.wait_ge(S["tile_expert"], 1)
            def expert_step(i, ring, lap):
                relu(i, ring)

            expert_steps(act, expert_step)

        @block.vector
        def _(dve):
            tt, ts = dve.tensor_tensor, dve.tensor_scalar

            dve.memset(mean_m[:, :], 1.0 / D)
            dve.memset(ones[:, :], 1.0)
            dve.memset(eps[:, :], EPS).then_inc(S["c_dve"], 1)
            dve.wait_ge(S["l_vec"], 16)
            for m in range(KD):
                to = hT[:, m, :].rearrange("p (i t) -> p i t", i=IMG)[:, :, 0]
                last = dve.tensor_copy(to, vcol("cls", m).broadcast_to([P, IMG]))
            last.then_inc(S["class_set"], 1)

            def norm_center(n, c):
                dve.wait_ge(n.mean, c + 1)
                tt(xc[:, c % 2, :, :], n.source[:, :, chunk(c)],
                   over_k(PS[:, n.mean_banks[c % len(n.mean_banks)], 0:CT], CT), ALU.subtract
                   ).then_inc(n.centered, 1)

            def norm_out(n, c, dst, affine=None):
                dve.wait_ge(n.rstd, c + 1)
                ins = tt(dst[:, :, chunk(c)], xc[:, c % 2, :, :], over_k(rs[:, c % 2, :], CT), ALU.mult)
                if affine is None:
                    ins.then_inc(n.done, 1)
                    return
                ins.then_inc(n.scaled, 1)
                dve.wait_ge(n.scaled, c + 1)
                for m in range(KD):
                    ins = ts(dst[:, m, chunk(c)], dst[:, m, chunk(c)], vcol(affine[0], m), vcol(affine[1], m),
                             ALU.mult, ALU.add)
                ins.then_inc(n.done, 1)

            def second_var(c):
                var, r, v2 = PS[:, n0.var_banks[c], 0:CT], rs[:, c % 2, :], rs2[:, c % 2, :]
                dve.wait_ge(n0.rstd, c + 1)
                tt(v2, r, r, ALU.mult).then_inc(S["rstd_squared"], 1)
                dve.wait_ge(S["rstd_squared"], c + 1)
                tt(v2, v2, var, ALU.mult).then_inc(S["second_var"], 1)

            def first_out(c):
                tt(x0T[:, :, chunk(c)], xc[:, c % 2, :, :], over_k(rs[:, c % 2, :], CT), ALU.mult
                   ).then_inc(n0.done, 1)

            def second_out(c):
                dve.wait_ge(n0.done, c + 1)
                dve.wait_ge(S["second_rstd"], c + 1)
                tt(nT[:, :, chunk(c)], x0T[:, :, chunk(c)], over_k(rs2[:, c % 2, :], CT), ALU.mult
                   ).then_inc(S["second_scaled"], 1)

            norm_center(n0, 0)
            dve.wait_ge(S["c_int"], 1)
            dve.tensor_copy(fw[:, :], iw[:, :]).then_inc(S["c_dve"], 1)
            for k in range(2):
                last = dve.tensor_copy(pairs[:, k, :, 1].bitcast(I32), iw[:, NT:2 * NT])
            last.then_inc(S["numbers"], 1)
            dve.wait_ge(S["c_dve"], 2)
            ts(valid[:, :], token_no, float(TOK), None, ALU.is_lt).then_inc(S["c_dve"], 1)
            norm_center(n0, 1)
            second_var(0)
            first_out(0)
            second_out(0)
            norm_center(n0, 2)

            def half_out(n, pos):
                dve.wait_ge(S["half_mm"], n + 1)
                if not isinstance(n, int) or n >= 4:
                    dve.wait_ge(S["scores_mm"], 2 * n - 4 - pos % 2 * 2)
                m = pos % 2 * KD
                tt(qk[:, pos // 2, m:m + KD, :], PS[:, 6, 0:KD * 2 * SEQ].rearrange("p (m s) -> p m s", m=KD),
                   vcol("qk_b", m, KD).unsqueeze(2).broadcast_to([P, KD, 2 * SEQ]), ALU.add
                   ).then_inc(S["half_out"], 1)

            def values_out(n, par):
                dve.wait_ge(S["values_mm"], n + 1)
                tt(va[par][0:SEQ, :, 0:HD], PS[0:SEQ, 7, 0:D].rearrange("p (h d) -> p h d", h=H),
                   vb_rows[0:SEQ, :].rearrange("p (h d) -> p h d", h=H), ALU.add).then_inc(S["values_out"], 1)

            def masked_max(n, g):
                dve.wait_ge(S["scores_mm"], 2 * n + g + 1)
                if not isinstance(n, int) or n >= 1:
                    dve.wait_ge(S["probabilities"], 2 * n + g - 1)
                to = sh[g][0:SEQ, :, :]
                tt(to.rearrange("p (b h) s -> p b h s", b=2),
                   PS[0:SEQ, 2 * g:2 * g + 2, 0:HB * SEQ].rearrange("p b (h s) -> p b h s", h=HB),
                   mask[0:SEQ, :].unsqueeze(1).unsqueeze(1).broadcast_to([SEQ, 2, HB, SEQ]), ALU.add
                   ).then_inc(S["masked"], 1)
                dve.wait_ge(S["masked"], 2 * n + g + 1)
                dve.tensor_reduce(mx[0:SEQ, g, :], to, AX_X, ALU.max).then_inc(S["max_taken"], 1)

            def less_max(n, g):
                dve.wait_ge(S["max_taken"], 2 * n + g + 1)
                to = sh[g][0:SEQ, :, :]
                tt(to, to, mx[0:SEQ, g, :].unsqueeze(2).broadcast_to([SEQ, HG, SEQ]), ALU.subtract
                   ).then_inc(S["less_max"], 1)

            def normalize(n):
                dve.wait_ge(S["weighted"], 2 * n + 2)
                o = PS[0:SEQ, 7, 0:H * (HD + 1)].rearrange("p (h d) -> p h d", h=H)
                dve.reciprocal(rc[0:SEQ, :], o[:, :, HD]).then_inc(S["sums_inverted"], 1)
                dve.wait_ge(S["sums_inverted"], n + 1)
                if not isinstance(n, int) or n >= 1:
                    dve.wait_ge(S["output_transposed"], n)
                tt(att[0:SEQ, :, :], o[:, :, 0:HD], rc[0:SEQ, :].unsqueeze(2).broadcast_to([SEQ, H, HD]), ALU.mult
                   ).then_inc(S["normalized"], 1)

            for i in range(2):
                dve.memset(va[i][0:SEQ, :, HD:HD + 1], 1.0)
            dve.wait_ge(S["l_rows"], 16 * 4)
            half_out(0, 0)
            second_var(1)
            first_out(1)
            dve.wait_ge(n0.done, 2)
            norm_center(n0, 3)
            second_out(1)
            half_out(1, 1)
            values_out(0, 0)
            second_var(2)
            first_out(2)
            half_out(2, 2)
            masked_max(0, 0)
            less_max(0, 0)
            second_var(3)
            masked_max(0, 1)
            values_out(1, 1)

            def step(i, pos, p):
                after = (pos + 1) % CI
                if not isinstance(i, int) or i > 0:
                    normalize(i - 1)
                less_max(i, 1)
                if isinstance(i, int) and i == 0:
                    first_out(3)
                    second_out(2)
                    second_out(3)
                if not isinstance(i, int) or i + 3 < IMG:
                    half_out(i + 3, (pos + 3) % CI)
                if not isinstance(i, int) or i + 1 < IMG:
                    if not isinstance(i, int) or i > 0:
                        values_out(i + 1, after % 2)
                    masked_max(i + 1, 0)
                    less_max(i + 1, 0)
                    masked_max(i + 1, 1)

            attention_steps(dve, step)

            def add_attention(c):
                dve.wait_ge(S["projected_out"], c + 1)
                tt(x0T[:, :, chunk(c)], x0T[:, :, chunk(c)], nT[:, :, chunk(c)], ALU.add).then_inc(S["attention_added"], 1)

            dve.wait_ge(S["l_mid"], 16 * 3)
            ts(wxd[:, :, :], wx[:, :, :], DT * DT, None, ALU.mult).then_inc(S["wxd"], 1)
            add_attention(0)
            normalize(IMG - 1)
            add_attention(1)
            norm_center(n1, 0)
            add_attention(2)
            norm_center(n1, 1)
            dve.wait_ge(S["output_transposed"], IMG)
            norm_out(n1, 0, xsT, ("g1", "b1"))
            add_attention(3)
            norm_center(n1, 2)
            norm_out(n1, 1, xsT, ("g1", "b1"))
            norm_center(n1, 3)
            norm_out(n1, 2, xsT, ("g1", "b1"))
            norm_out(n1, 3, xsT, ("g1", "b1"))

            def advance(n, c, first):
                dve.wait_ge(S["tanh_done"], n)
                if first:
                    tt(eT[:, :, chunk(c)], u[:, c % 2, :, :], xsT[:, :, chunk(c)], ALU.subtract).then_inc(S["velocity"], 1)
                else:
                    dve.wait_ge(S["decayed_less_state"], n - NCH)
                    tt(eT[:, :, chunk(c)], u[:, c % 2, :, :], rT[:, :, chunk(c)], ALU.add).then_inc(S["velocity"], 1)
                dve.wait_ge(S["velocity"], n)
                dve.scalar_tensor_tensor(out=xsT[:, :, chunk(c)], in0=eT[:, :, chunk(c)], scalar=DT * DT,
                                         in1=xsT[:, :, chunk(c)], op0=ALU.mult, op1=ALU.add).then_inc(S["state"], 1)

            for c in range(NCH):
                advance(c + 1, c, True)
            with dve.Fori(1, ITERS - 1) as t:
                for c in range(NCH):
                    advance(t * NCH + (c + 1), c, False)

            def last_advance(c):
                n = (ITERS - 1) * NCH + c + 1
                advance(n, c, False)
                dve.wait_ge(S["state"], n)
                tt(x0T[:, :, chunk(c)], x0T[:, :, chunk(c)], xsT[:, :, chunk(c)], ALU.add).then_inc(S["loop_added"], 1)

            for c in range(3):
                last_advance(c)
            norm_center(n2, 0)
            last_advance(3)
            norm_center(n2, 1)
            norm_out(n2, 0, xsT, ("g2", "b2"))
            norm_center(n2, 2)
            norm_out(n2, 1, xsT, ("g2", "b2"))
            norm_center(n2, 3)
            norm_out(n2, 2, xsT, ("g2", "b2"))

            def residual(c):
                dve.wait_ge(S["ff_out_biased"], KD * (c + 1))
                tt(x0T[:, :, chunk(c)], x0T[:, :, chunk(c)], ffb_buf[:, :, :], ALU.add).then_inc(S["ff_added"], 1)
                dve.wait_ge(S["ff_added"], c + 1)
                tt(hT[:, :, chunk(c)], hT[:, :, chunk(c)], x0T[:, :, chunk(c)], ALU.add).then_inc(S["block_added"], 1)

            dve.wait_ge(S["drive_mm"], NCH)
            dve.memset(nT[:, :, TOK:TP], 0.0)
            residual(0)
            norm_center(n3, 0)
            norm_out(n2, 3, xsT, ("g2", "b2"))
            norm_out(n3, 0, nT)
            residual(1)
            norm_center(n3, 1)
            norm_out(n3, 1, nT)

            done = [0]
            reduce = dve.tensor_reduce

            def link(ins):
                done[0] += 1
                ins.then_inc(S["route"], 1)
                dve.wait_ge(S["route"], done[0])

            def choose(batch):
                first, behind = ROUTED[batch]
                n = behind - first
                b = slice(first, behind)
                p, s_ = pr[:, b, :], scr[:, b, :]

                def over_e(ap):
                    return ap.unsqueeze(2).broadcast_to([P, n, E])

                dve.wait_ge(S["logits_mm"], behind)
                link(tt(p, PS[:, ROUTED_IN[batch], first * E:behind * E].rearrange("p (t e) -> p t e", t=n),
                        gb_rows[:, :].unsqueeze(1).broadcast_to([P, n, E]), ALU.add))
                link(reduce(s9[:, 0, b], p, AX_X, ALU.max))
                tt(p, p, over_e(s9[:, 0, b]), ALU.subtract).then_inc(S["shifted"], 1)
                dve.wait_ge(S["exponentials"], batch + 1)
                link(reduce(s9[:, 1, b], p, AX_X, ALU.add))
                link(dve.reciprocal(s9[:, 2, b], s9[:, 1, b]))
                link(tt(p, p, over_e(s9[:, 2, b]), ALU.mult))
                for k in range(2):
                    top = s9[:, 3 + k, b]
                    link(reduce(top, p, AX_X, ALU.max))
                    link(tt(s_, p, over_e(top), ALU.is_equal))
                    link(tt(s_, s_, rank.unsqueeze(1).broadcast_to([P, n, E]), ALU.mult))
                    link(reduce(s9[:, 5, b], s_, AX_X, ALU.max))
                    link(tt(oh[k][:, b, :], s_, over_e(s9[:, 5, b]), ALU.is_equal))
                    if k == 0:
                        link(dve.scalar_tensor_tensor(out=p, in0=oh[0][:, b, :], scalar=-2.0, in1=p, op0=ALU.mult,
                                                      op1=ALU.add))
                link(tt(s_, oh[0][:, b, :], oh[1][:, b, :], ALU.add))
                tt(member[:, b, :], s_, over_e(valid[:, b]), ALU.mult).then_inc(S["member"], 1)
                for k in range(2):
                    last = dve.tensor_copy(pairs[:, k, b, 0], s9[:, 3 + k, b])
                last.then_inc(S["pairs"], 1)

            def place(batch):
                first, behind = ROUTED[batch]
                n = behind - first
                b = slice(first, behind)
                s_, s2 = scr[:, b, :], scr2[:, b, :]
                bank = ROUTED_IN[batch]
                dve.wait_ge(S["member"], batch + 1)
                dve.wait_ge(S["ranks_mm"], batch + 1)
                if batch == 0:
                    link(dve.tensor_copy(pre[:, 0, :], region))
                for t in range(first, behind):
                    link(tt(pre[:, t + 1, :], PS[:, bank, (2 * NT + t) * E:(2 * NT + t + 1) * E], pre[:, t, :], ALU.add))
                link(tt(s_, PS[:, bank, (NT + first) * E:(NT + behind) * E].rearrange("p (t e) -> p t e", t=n),
                        pre[:, b, :], ALU.add))
                for k in range(2):
                    link(tt(s2, s_, oh[k][:, b, :], ALU.mult))
                    link(reduce(slot_f[:, k, b], s2, AX_X, ALU.add))
                dve.tensor_copy(slot_i[:, :, b], slot_f[:, :, b]).then_inc(S["slot_no"], 1)

            def gates_by_expert(batch):
                b = slice(*ROUTED[batch])
                n = ROUTED[batch][1] - ROUTED[batch][0]
                link(tt(scr[:, b, :], oh[0][:, b, :], s9[:, 3, b].unsqueeze(2).broadcast_to([P, n, E]), ALU.mult))
                link(tt(scr2[:, b, :], oh[1][:, b, :], s9[:, 4, b].unsqueeze(2).broadcast_to([P, n, E]), ALU.mult))
                tt(gates[:, b, :], scr[:, b, :], scr2[:, b, :], ALU.add).then_inc(S["gates"], 1)

            choose(0)
            residual(2)
            norm_center(n3, 2)
            place(0)
            gates_by_expert(0)
            residual(3)
            norm_out(n3, 2, nT)
            norm_center(n3, 3)
            choose(1)
            norm_out(n3, 3, nT)
            place(1)
            choose(2)
            gates_by_expert(1)
            place(2)
            gates_by_expert(2)

            link(tt(scr[:, 0, :], pre[:, NT, :], region, ALU.subtract))
            link(tt(tiles_k[:, :, :], scr[:, 0, :].unsqueeze(2).broadcast_to([P, E, NT]),
                    multiples.unsqueeze(1).broadcast_to([P, E, NT]), ALU.is_gt))
            link(reduce(tiles_e[:, :], tiles_k[:, :, :], AX_X, ALU.add))
            link(tt(start_k[:, :, :], before[:, :, :], tiles_e[:, :].unsqueeze(1).broadcast_to([P, E, E]), ALU.mult))
            link(reduce(start_e[:, :], start_k[:, :, :], AX_X, ALU.add))
            link(tt(te_k[:, :, :], start_e[:, 1:E].unsqueeze(1).broadcast_to([P, SLOT_TILES, E - 1]),
                    tile_no.unsqueeze(2).broadcast_to([P, SLOT_TILES, E - 1]), ALU.is_le))
            link(reduce(te[:, :], te_k[:, :, :], AX_X, ALU.add))
            link(ts(past_e[:, :], tiles_e[:, 0:E - 1], -float(P), float(CAP), ALU.mult, ALU.add))
            link(tt(te_k[:, :, :], te_k[:, :, :], past_e[:, :].unsqueeze(1).broadcast_to([P, SLOT_TILES, E - 1]),
                    ALU.mult))
            link(reduce(tb[:, :], te_k[:, :, :], AX_X, ALU.add))
            link(dve.scalar_tensor_tensor(out=tb[:, :], in0=tile_no, scalar=float(P), in1=tb[:, :], op0=ALU.mult,
                                          op1=ALU.add))
            dve.tensor_copy(tile_base[:, :], tb[:, :])
            dve.tensor_copy(tile_expert[:, :], te[:, :]).then_inc(S["tile_expert"], 1)

            def input_out(i, ring):
                dve.wait_ge(S["input_transposed"], i + 1)
                if not isinstance(i, int) or i >= 2:
                    dve.wait_ge(S["layer1_mm"], i - 1)
                dve.tensor_copy(xt[:, ring % 2, :, :], PS[:, 5, 0:D].rearrange("p (k t) -> p k t", k=KD)
                                ).then_inc(S["input_out"], 1)

            def weights_in(i, ring):
                w = dve.value_load(tile_expert[0:1, bass.ds(i, 1)], min_val=0, max_val=E - 1) * WE
                if not isinstance(i, int) or i >= 2:
                    dve.wait_ge(S["layer1_mm"], i - 1)
                dve.tensor_copy(w1[ring % 2], W[:, bass.ds(w, KD * EH)].rearrange("p (k n) -> p k n", k=KD)
                                ).then_inc(S["weights_in"], 1)

            def gated(i, ring):
                gate = info[:, i, 0:1] if isinstance(i, int) else info[:, bass.ds(i, 1), 0].rearrange("p o -> p o")
                dve.wait_ge(S["layer2_mm"], i + 1)
                if not isinstance(i, int) or i >= 2:
                    dve.wait_ge(S["rows_added"], 16 * (i - 1))
                ts(yt[:, ring % 2, :], PS[:, 4, 0:D], gate, None, ALU.mult).then_inc(S["gated"], 1)

            dve.wait_ge(S["tile_expert"], 1)
            dve.wait_ge(S["l_moe"], 16 * (E - 2))
            dve.wait_ge(S["l_moe_late"], 16 * 2)
            weights_in(0, 0)
            dve.wait_ge(S["residual_row_mm"], NT)
            weights_in(1, 1)
            input_out(0, 0)
            input_out(1, 1)

            def expert_step(i, ring, lap):
                if not isinstance(i, int) or i + 2 < SLOT_TILES:
                    input_out(i + 2, (ring + 2) % XR)
                if isinstance(i, int) and i == 0:
                    weights_in(2, 2)
                if not isinstance(i, int) or i + 3 < SLOT_TILES:
                    weights_in(i + 3, (ring + 3) % XR)
                gated(i, ring)

            expert_steps(dve, expert_step)


def by_partition(w):
    return w.reshape(w.shape[0] // P, P, -1).transpose(1, 0, 2)


def columns(b):
    return b.reshape(-1, P).T


def layout(np, a):
    x = a["x"].reshape(IMG, 3, 8, 16, 8, 16).transpose(0, 2, 4, 3, 5, 1).reshape(NCH, CP, KPATCH, P)
    w1 = a["L0_ffn_w1"].reshape(E, KD, P, EH).transpose(0, 2, 1, 3).reshape(E, P, KD * EH)
    w2 = a["L0_ffn_w2"].reshape(E, KE, P, D).transpose(0, 2, 1, 3).reshape(E, P, KE * D)
    qkv_b = a["L0_attn_qkv_b"]
    by_name = {
        "tok_b": a["L0_tok_b"], "cls": a["cls_tok"].reshape(D), "g_attn": a["L0_attn_g_attn"],
        "b_attn": a["L0_attn_b_attn"], "g1": a["L0_attn_g1"], "b1": a["L0_attn_b1"], "g2": a["L0_attn_g2"],
        "b2": a["L0_attn_b2"], "b_inl": a["L0_attn_b_inl"], "qk_b": qkv_b[0:2 * D], "out_b": a["L0_attn_out_b"],
        "ff_b1": a["L0_attn_ff_b1"], "ff_b2": a["L0_attn_ff_b2"], "moe_b1": a["L0_ffn_b1"].reshape(E * EH),
    }
    return {
        "patches": x.transpose(0, 3, 2, 1), "tok_w": by_partition(a["L0_tok_W"].T),
        "qkv_w": by_partition(a["L0_attn_qkv_w"]), "out_w": by_partition(a["L0_attn_out_w"]),
        "ctx_w": by_partition(a["L0_attn_w_ctx"]), "x_w": by_partition(a["L0_attn_w_x"]),
        "ff1_w": by_partition(a["L0_attn_ff_w1"]), "ff2_w": by_partition(a["L0_attn_ff_w2"]),
        "moe_w": np.concatenate([w1, w2], axis=2), "gate_w": by_partition(a["L0_ffn_gate_w"].T),
        "vec": np.concatenate([columns(by_name[n]) for n, _ in VEC], axis=1),
        "v_b": qkv_b[2 * D:3 * D].reshape(1, D), "gate_b": a["L0_ffn_gate_b"].reshape(1, E),
        "moe_b2": a["L0_ffn_b2"],
    }


def kernel(**inputs):
    import numpy as np
    import concourse.bacc as bacc
    from concourse.bass_utils import run_bass_kernel_spmd

    nc = bacc.Bacc("TRN2", target_bir_lowering=False, num_devices=1)
    arrays, args = {}, {}
    for name, a in layout(np, {n: np.asarray(v) for n, v in inputs.items()}).items():
        a = np.ascontiguousarray(a)
        arrays[name] = a
        args[name] = nc.dram_tensor(name, a.shape, F32, kind="ExternalInput").ap()
    out = nc.dram_tensor("out", (TOK + P, D), F32, kind="ExternalOutput").ap()
    vit_block(nc, out=out, **args)
    result = run_bass_kernel_spmd(nc, [arrays], core_ids=[0])
    return result.results[0]["out"][:TOK].reshape(IMG, SEQ, D)
```
